# Optimizing a Trainium2 kernel written in Bass

```python
import numpy as np
import jax
import jax.numpy as jnp

def _softmax(x, axis=-1):
    return jax.nn.softmax(x, axis=axis)

def _gelu(x):
    return jax.nn.gelu(x, approximate=True)

def _silu(x):
    return jax.nn.silu(x)

def _sigmoid(x):
    return jax.nn.sigmoid(x)

def _layernorm(x, axis=-1, eps=1e-05):
    m = jnp.mean(x, axis=axis, keepdims=True)
    v = jnp.var(x, axis=axis, keepdims=True)
    return (x - m) / jnp.sqrt(v + eps)

def _scatter_add(tgt, idx, src, axis=0):
    return tgt.at[idx].add(src)

def _segment_sum(src, seg, n):
    return jax.ops.segment_sum(src, seg, n)
kernel_name = 'mk_gps_d4_gnn_r32_8a6ed6'

def setup_inputs(seed: int=0):
    np.random.seed(seed)
    _w = jnp.asarray

    def _rec_inputs():
        import jax
        import jax.numpy as jnp
        _gk = jax.random.key(seed)
        x = -0.0003713 + 1 * jax.random.normal(jax.random.fold_in(_gk, 1), (3125, 256), jnp.float32)
        src = jax.random.randint(jax.random.fold_in(_gk, 2), (50000,), 0, 3125, jnp.int32)
        dst = jnp.minimum((3125 * jax.random.uniform(jax.random.fold_in(_gk, 3), (50000,)) ** 2.0).astype(jnp.int32), 99999)
        _o = jnp.argsort(dst, stable=True)
        src = src[_o]
        dst = dst[_o]
        edge_weight = jax.random.uniform(jax.random.fold_in(_gk, 13), (50000,), jnp.float32, 0.0, 0.0624999)
        edge_weight_n2 = jax.random.uniform(jax.random.fold_in(_gk, 14), (50000,), jnp.float32, 0.0, 0.0624999)
        return (x, src, dst, edge_weight, edge_weight_n2)
    x, src, dst, edge_weight, edge_weight_n2 = _rec_inputs()

    def _L0_gnn_setup():
        import jax, jax.numpy as jnp
        import numpy as np
        N = 50000
        E = 25000
        D_IN = 256
        D_OUT = 256

        def _spmm(row, col, val, h, n_nodes):
            return jax.ops.segment_sum(val[:, None] * h[col], row, num_segments=n_nodes)
        if __name__ == '__main__':
            out = reference(**setup_inputs())
            print(out.shape, out.dtype)
        key = jax.random.key(seed)
        ks = jax.random.split(key, 12)
        stdv = 1.0 / np.sqrt(D_OUT)
        u = lambda k, shape, s: jax.random.uniform(k, shape, jnp.float32, -s, s)
        return {'x': jax.random.normal(ks[0], (N, D_IN), jnp.float32), 'val_low': jax.random.uniform(ks[1], (E,), jnp.float32) * (1.0 / 16.0), 'val_high': jax.random.uniform(ks[2], (E,), jnp.float32) * (1.0 / 16.0), 'weight_low': u(ks[3], (D_IN, D_OUT), stdv), 'weight_high': u(ks[4], (D_IN, D_OUT), stdv), 'weight_mlp': u(ks[5], (D_IN, D_OUT), stdv), 'att_vec_low': u(ks[6], (D_OUT, 1), 1.0), 'att_vec_high': u(ks[7], (D_OUT, 1), 1.0), 'att_vec_mlp': u(ks[8], (D_OUT, 1), 1.0), 'att_vec': u(ks[9], (3, 3), 1.0 / np.sqrt(3.0)), 'row': jax.random.randint(ks[10], (E,), 0, N), 'col': jax.random.randint(ks[11], (E,), 0, N)}
    _L0_gnn_all = _L0_gnn_setup()
    _L0_gnn_in = {k: v for k, v in _L0_gnn_all.items() if k in ('weight_low', 'weight_high', 'weight_mlp', 'att_vec_low', 'att_vec_high', 'att_vec_mlp', 'att_vec')}
    del _L0_gnn_all

    def _L0_mix_setup():
        import jax, jax.numpy as jnp
        import numpy as np
        D_MODEL = 256
        NUM_HEADS = 8
        DEPTH = D_MODEL // NUM_HEADS
        B, L = (32, 128)

        def _feature_map(x):
            return jax.nn.elu(x) + 1.0
        key = jax.random.key(seed)
        ks = jax.random.split(key, 9)
        sc = 1.0 / np.sqrt(D_MODEL)
        return {'x': jax.random.normal(ks[0], (B, L, D_MODEL), dtype=jnp.float32), 'wq': jax.random.normal(ks[1], (D_MODEL, D_MODEL), dtype=jnp.float32) * sc, 'bq': jnp.zeros((D_MODEL,), dtype=jnp.float32), 'wk': jax.random.normal(ks[2], (D_MODEL, D_MODEL), dtype=jnp.float32) * sc, 'bk': jnp.zeros((D_MODEL,), dtype=jnp.float32), 'wv': jax.random.normal(ks[3], (D_MODEL, D_MODEL), dtype=jnp.float32) * sc, 'bv': jnp.zeros((D_MODEL,), dtype=jnp.float32), 'wo': jax.random.normal(ks[4], (D_MODEL, D_MODEL), dtype=jnp.float32) * sc, 'bo': jnp.zeros((D_MODEL,), dtype=jnp.float32)}
    _L0_mix_all = _L0_mix_setup()
    _L0_mix_in = {k: v for k, v in _L0_mix_all.items() if k in ('wq', 'bq', 'wk', 'bk', 'wv', 'bv', 'wo', 'bo')}
    del _L0_mix_all

    def _L0_ffn_setup():
        import jax, jax.numpy as jnp
        import numpy as np
        E = 8
        K = 2
        D = 256
        H = 512
        DOUT = 256
        EPS = 1e-05
        key = jax.random.key(seed)
        ks = jax.random.split(key, 9)
        s = 0.02
        return {'x': jax.random.normal(ks[0], (4, 256, D), jnp.float32), 'gamma': 1.0 + 0.05 * jax.random.normal(ks[1], (D,), jnp.float32), 'beta': 0.05 * jax.random.normal(ks[2], (D,), jnp.float32), 'Wr': 0.01 * jax.random.normal(ks[3], (D, E), jnp.float32), 'br': jnp.zeros((E,), jnp.float32), 'W1': s * jax.random.normal(ks[4], (E, D, H), jnp.float32), 'b1': s * jax.random.normal(ks[5], (E, H), jnp.float32), 'W2': s * jax.random.normal(ks[6], (E, H, DOUT), jnp.float32), 'b2': s * jax.random.normal(ks[7], (E, DOUT), jnp.float32)}
    _L0_ffn_all = _L0_ffn_setup()
    _L0_ffn_in = {k: v for k, v in _L0_ffn_all.items() if k in ('gamma', 'beta', 'Wr', 'br', 'W1', 'b1', 'W2', 'b2')}
    del _L0_ffn_all

    def _L1_gnn_setup():
        import jax, jax.numpy as jnp
        import numpy as np
        N_NODES = 10000
        N_EDGES = 10000
        D = 256
        key = jax.random.key(seed)
        k_x, k_w, k_m, k_s, k_d = jax.random.split(key, 5)
        x = jax.random.normal(k_x, (N_NODES, D), dtype=jnp.float32)
        W = jax.random.normal(k_w, (D, D), dtype=jnp.float32)
        M = jax.random.normal(k_m, (D, D), dtype=jnp.float32)
        edge_src = jax.random.randint(k_s, (N_EDGES,), 0, N_NODES, dtype=jnp.int64)
        edge_dst = jax.random.randint(k_d, (N_EDGES,), 0, N_NODES, dtype=jnp.int64)
        return {'x': x, 'W': W, 'M': M, 'edge_src': edge_src, 'edge_dst': edge_dst}
    _L1_gnn_all = _L1_gnn_setup()
    _L1_gnn_in = {k: v for k, v in _L1_gnn_all.items() if k in ('W', 'M')}
    del _L1_gnn_all

    def _L1_mix_setup():
        import jax, jax.numpy as jnp
        import numpy as np
        B, L, D, H = (4, 512, 256, 8)
        DK = D // H

        def _heads(t):
            b, l, d = t.shape
            return t.reshape(b, l, H, DK).transpose(0, 2, 1, 3)
        key = jax.random.key(seed)
        ks = jax.random.split(key, 9)
        s = 0.02
        return {'x': jax.random.normal(ks[0], (B, L, D), dtype=jnp.float32), 'Wq': jax.random.normal(ks[1], (D, D), dtype=jnp.float32) * s, 'bq': jnp.zeros((D,), dtype=jnp.float32), 'Wk': jax.random.normal(ks[2], (D, D), dtype=jnp.float32) * s, 'bk': jnp.zeros((D,), dtype=jnp.float32), 'Wv': jax.random.normal(ks[3], (D, D), dtype=jnp.float32) * s, 'bv': jnp.zeros((D,), dtype=jnp.float32), 'Wfc': jax.random.normal(ks[4], (D, D), dtype=jnp.float32) * s, 'bfc': jnp.zeros((D,), dtype=jnp.float32)}
    _L1_mix_all = _L1_mix_setup()
    _L1_mix_in = {k: v for k, v in _L1_mix_all.items() if k in ('Wq', 'bq', 'Wk', 'bk', 'Wv', 'bv', 'Wfc', 'bfc')}
    del _L1_mix_all

    def _L1_ffn_setup():
        import jax, jax.numpy as jnp
        import numpy as np
        B, K, D = (512, 16, 256)
        E = 32
        H = int(D * 0.25)
        key = jax.random.key(seed)
        ks = jax.random.split(key, 7)
        d_rs = D ** (-0.5)
        h_rs = H ** (-0.5)
        x = jax.random.normal(ks[0], (B, K, D), dtype=jnp.float32)
        router_w = jax.random.uniform(ks[1], (E, D), jnp.float32, -d_rs, d_rs)
        router_b = jax.random.uniform(ks[2], (E,), jnp.float32, -d_rs, d_rs)
        W1 = jax.random.uniform(ks[3], (E, D, H), jnp.float32, -h_rs, h_rs)
        b1 = jax.random.uniform(ks[4], (E, H), jnp.float32, -h_rs, h_rs)
        W2 = jax.random.uniform(ks[5], (E, H, D), jnp.float32, -d_rs, d_rs)
        b2 = jax.random.uniform(ks[6], (E, D), jnp.float32, -d_rs, d_rs)
        return {'x': x, 'router_w': router_w, 'router_b': router_b, 'W1': W1, 'b1': b1, 'W2': W2, 'b2': b2}
    _L1_ffn_all = _L1_ffn_setup()
    _L1_ffn_in = {k: v for k, v in _L1_ffn_all.items() if k in ('router_w', 'router_b', 'W1', 'b1', 'W2', 'b2')}
    del _L1_ffn_all

    def _L2_gnn_setup():
        import jax, jax.numpy as jnp
        import numpy as np
        N_NODES = 50000
        N_EDGES = 25000
        C = 256
        EPS = 1e-05

        def _bn(x, gamma, beta, mean, var):
            return (x - mean) * jax.lax.rsqrt(var + EPS) * gamma + beta
        key = jax.random.key(seed)
        ks = jax.random.split(key, 8)
        x = jax.random.normal(ks[0], (N_NODES, C), dtype=jnp.float32)
        edge_index = jax.random.randint(ks[1], (2, N_EDGES), 0, N_NODES, dtype=jnp.int64)
        W = jax.random.normal(ks[2], (2 * C, C), dtype=jnp.float32) * (1.0 / np.sqrt(2 * C))
        b = jnp.zeros((C,), dtype=jnp.float32)
        bn1_gamma = jnp.ones((C,), jnp.float32)
        bn1_beta = jnp.zeros((C,), jnp.float32)
        bn1_mean = jax.random.normal(ks[3], (C,), jnp.float32) * 0.1
        bn1_var = jax.random.uniform(ks[4], (C,), jnp.float32, 0.5, 1.5)
        bn2_gamma = jnp.ones((C,), jnp.float32)
        bn2_beta = jnp.zeros((C,), jnp.float32)
        bn2_mean = jax.random.normal(ks[5], (C,), jnp.float32) * 0.1
        bn2_var = jax.random.uniform(ks[6], (C,), jnp.float32, 0.5, 1.5)
        return {'x': x, 'edge_index': edge_index, 'W': W, 'b': b, 'bn1_gamma': bn1_gamma, 'bn1_beta': bn1_beta, 'bn1_mean': bn1_mean, 'bn1_var': bn1_var, 'bn2_gamma': bn2_gamma, 'bn2_beta': bn2_beta, 'bn2_mean': bn2_mean, 'bn2_var': bn2_var}
    _L2_gnn_all = _L2_gnn_setup()
    _L2_gnn_in = {k: v for k, v in _L2_gnn_all.items() if k in ('W', 'b', 'bn1_gamma', 'bn1_beta', 'bn1_mean', 'bn1_var', 'bn2_gamma', 'bn2_beta', 'bn2_mean', 'bn2_var')}
    del _L2_gnn_all

    def _L2_mix_setup():
        import jax, jax.numpy as jnp
        import numpy as np
        B, N, C = (8, 256, 256)
        H, D, S = (8, 32, 32)
        HID = 4 * C

        def layernorm(x, w, b, eps=1e-05):
            mu = jnp.mean(x, axis=-1, keepdims=True)
            var = jnp.mean(jnp.square(x - mu), axis=-1, keepdims=True)
            return (x - mu) * jax.lax.rsqrt(var + eps) * w + b

        def linear_no_attn(x, Wx, bx, Wq, Wk, Wv, Wo, bo):
            x_mid = x @ Wx.T + bx
            x_mid = x_mid.reshape(x.shape[0], x.shape[1], H, D).transpose(0, 2, 1, 3)
            q = jax.nn.softmax(x_mid @ Wq.T, axis=-1)
            k = jax.nn.softmax(x_mid @ Wk.T, axis=-2)
            v = x_mid @ Wv.T
            kv = jnp.einsum('bhns,bhnd->bhsd', k, v)
            qkv = jnp.einsum('bhns,bhsd->bhnd', q, kv)
            qkv = qkv.transpose(0, 2, 1, 3).reshape(x.shape[0], x.shape[1], H * D)
            return qkv @ Wo.T + bo
        key = jax.random.key(seed)
        ks = jax.random.split(key, 16)
        s = lambda fan: 1.0 / np.sqrt(fan)
        return {'fx': jax.random.normal(ks[0], (B, N, C), jnp.float32), 'ln1_w': jnp.ones((C,), jnp.float32), 'ln1_b': jnp.zeros((C,), jnp.float32), 'Wx': jax.random.uniform(ks[1], (C, C), jnp.float32, -s(C), s(C)), 'bx': jax.random.uniform(ks[2], (C,), jnp.float32, -s(C), s(C)), 'Wq': jax.random.uniform(ks[3], (S, D), jnp.float32, -s(D), s(D)), 'Wk': jax.random.uniform(ks[4], (S, D), jnp.float32, -s(D), s(D)), 'Wv': jax.random.uniform(ks[5], (D, D), jnp.float32, -s(D), s(D)), 'Wo': jax.random.uniform(ks[6], (C, C), jnp.float32, -s(C), s(C)), 'bo': jax.random.uniform(ks[7], (C,), jnp.float32, -s(C), s(C)), 'ln2_w': jnp.ones((C,), jnp.float32), 'ln2_b': jnp.zeros((C,), jnp.float32), 'W1': jax.random.uniform(ks[8], (HID, C), jnp.float32, -s(C), s(C)), 'b1': jax.random.uniform(ks[9], (HID,), jnp.float32, -s(C), s(C)), 'W2': jax.random.uniform(ks[10], (C, HID), jnp.float32, -s(HID), s(HID)), 'b2': jax.random.uniform(ks[11], (C,), jnp.float32, -s(HID), s(HID))}
    _L2_mix_all = _L2_mix_setup()
    _L2_mix_in = {k: v for k, v in _L2_mix_all.items() if k in ('ln1_w', 'ln1_b', 'Wx', 'bx', 'Wq', 'Wk', 'Wv', 'Wo', 'bo', 'ln2_w', 'ln2_b', 'W1', 'b1', 'W2', 'b2')}
    del _L2_mix_all

    def _L2_ffn_setup():
        import jax, jax.numpy as jnp
        import numpy as np
        B, N, D = (16, 128, 256)
        NUM_EXPERTS, TOP_K, HEADS = (4, 2, 4)
        N_EDGES = 32768
        LN_EPS = 1e-05

        def _layernorm(x, g, b):
            mu = x.mean(-1, keepdims=True)
            var = ((x - mu) ** 2).mean(-1, keepdims=True)
            return (x - mu) * jax.lax.rsqrt(var + LN_EPS) * g + b

        def _forward(x, edge_index, W_gat, att_src, att_dst, b_gat, ln_gamma, ln_beta, W1, b1, W2, b2):
            Bc, Nc, Dc = x.shape
            M = Bc * Nc
            x_flat = x.reshape(M, Dc)
            h = (x_flat @ W_gat).reshape(M, HEADS, NUM_EXPERTS)
            loops = jnp.arange(M, dtype=edge_index.dtype)
            src = jnp.concatenate([edge_index[0], loops])
            dst = jnp.concatenate([edge_index[1], loops])
            a_src = (h * att_src).sum(-1)
            a_dst = (h * att_dst).sum(-1)
            e = jax.nn.leaky_relu(a_src[src] + a_dst[dst], negative_slope=0.2)
            e_max = jax.ops.segment_max(e, dst, num_segments=M)
            ee = jnp.exp(e - e_max[dst])
            denom = jax.ops.segment_sum(ee, dst, num_segments=M)
            alpha = ee / (denom[dst] + 1e-16)
            msg = h[src] * alpha[:, :, None]
            agg = jax.ops.segment_sum(msg, dst, num_segments=M).reshape(M, HEADS * NUM_EXPERTS) + b_gat
            scores = _layernorm(agg, ln_gamma, ln_beta).reshape(M, HEADS, NUM_EXPERTS).mean(1)
            scores = scores.reshape(Bc, Nc, NUM_EXPERTS)
            topk_s, topk_i = jax.lax.top_k(scores, TOP_K)
            w = jax.nn.softmax(topk_s, axis=-1)
            out = jnp.zeros_like(x)
            for ei in range(NUM_EXPERTS):
                g = jnp.where(topk_i == ei, w, 0.0).sum(-1)
                hh = jax.nn.gelu(x @ W1[ei] + b1[ei], approximate=False)
                out = out + g[..., None] * (hh @ W2[ei] + b2[ei])
            return out
        key = jax.random.key(seed)
        ks = jax.random.split(key, 8)
        s = 0.05
        return {'x': jax.random.normal(ks[0], (B, N, D), jnp.float32), 'W_gat': jax.random.normal(ks[1], (D, HEADS * NUM_EXPERTS), jnp.float32) * s, 'att_src': jax.random.normal(ks[2], (HEADS, NUM_EXPERTS), jnp.float32) * s, 'att_dst': jax.random.normal(ks[3], (HEADS, NUM_EXPERTS), jnp.float32) * s, 'b_gat': jnp.zeros((HEADS * NUM_EXPERTS,), jnp.float32), 'ln_gamma': jnp.ones((HEADS * NUM_EXPERTS,), jnp.float32), 'ln_beta': jnp.zeros((HEADS * NUM_EXPERTS,), jnp.float32), 'W1': jax.random.normal(ks[4], (NUM_EXPERTS, D, 2 * D), jnp.float32) * s, 'b1': jnp.zeros((NUM_EXPERTS, 2 * D), jnp.float32), 'W2': jax.random.normal(ks[5], (NUM_EXPERTS, 2 * D, D), jnp.float32) * s, 'b2': jnp.zeros((NUM_EXPERTS, D), jnp.float32), 'edge_index': jax.random.randint(ks[6], (2, N_EDGES), 0, B * N, jnp.int32)}
    _L2_ffn_all = _L2_ffn_setup()
    _L2_ffn_in = {k: v for k, v in _L2_ffn_all.items() if k in ('W_gat', 'att_src', 'att_dst', 'b_gat', 'ln_gamma', 'ln_beta', 'W1', 'b1', 'W2', 'b2', 'edge_index')}
    del _L2_ffn_all

    def _L3_gnn_setup():
        import jax, jax.numpy as jnp
        import numpy as np
        N_NODES = 3125
        F_DIM = 256
        NNZ = 50000

        def _prelu(x, a):
            return jnp.where(x >= 0, x, a * x)

        def _hconv(x, W, b, src, dst, n):
            xt = x @ W
            ones = jnp.ones(src.shape, xt.dtype)
            D = jax.ops.segment_sum(ones, src, num_segments=n)
            B = jax.ops.segment_sum(ones, dst, num_segments=n)
            Dinv = jnp.where(D > 0, 1.0 / D, 0.0)
            Binv = jnp.where(B > 0, 1.0 / B, 0.0)
            m = jax.ops.segment_sum(xt[src], dst, num_segments=n) * Binv[:, None]
            out = jax.ops.segment_sum(m[dst], src, num_segments=n) * Dinv[:, None]
            return out + b
        key = jax.random.key(seed)
        k0, k1, k2, k3 = jax.random.split(key, 4)
        x = jax.random.normal(k0, (N_NODES, F_DIM), dtype=jnp.float32)
        edge_index = jax.random.randint(k1, (2, NNZ), 0, N_NODES, dtype=jnp.int32)
        scale = (2.0 / F_DIM) ** 0.5
        W1 = jax.random.normal(k2, (F_DIM, F_DIM), dtype=jnp.float32) * scale
        W2 = jax.random.normal(k3, (F_DIM, F_DIM), dtype=jnp.float32) * scale
        b1 = jnp.zeros((F_DIM,), jnp.float32)
        b2 = jnp.zeros((F_DIM,), jnp.float32)
        a = jnp.full((1,), 0.25, jnp.float32)
        return {'x': x, 'edge_index': edge_index, 'W1': W1, 'b1': b1, 'W2': W2, 'b2': b2, 'a': a}
    _L3_gnn_all = _L3_gnn_setup()
    _L3_gnn_in = {k: v for k, v in _L3_gnn_all.items() if k in ('W1', 'b1', 'W2', 'b2', 'a')}
    del _L3_gnn_all

    def _L3_mix_setup():
        import jax, jax.numpy as jnp
        import numpy as np
        NUM_HEADS = 8
        key = jax.random.key(seed)
        ks = jax.random.split(key, 5)
        B, N, C = (8, 512, 256)
        x = jax.random.normal(ks[0], (B, N, C), dtype=jnp.float32)
        Wq = jax.random.normal(ks[1], (C, C), dtype=jnp.float32) * 0.02
        Wkv = jax.random.normal(ks[2], (2 * C, C), dtype=jnp.float32) * 0.02
        Wproj = jax.random.normal(ks[3], (C, C), dtype=jnp.float32) * 0.02
        bproj = jnp.zeros((C,), dtype=jnp.float32)
        return {'x': x, 'Wq': Wq, 'Wkv': Wkv, 'Wproj': Wproj, 'bproj': bproj}
    _L3_mix_all = _L3_mix_setup()
    _L3_mix_in = {k: v for k, v in _L3_mix_all.items() if k in ('Wq', 'Wkv', 'Wproj', 'bproj')}
    del _L3_mix_all

    def _L3_ffn_setup():
        import jax, jax.numpy as jnp
        import numpy as np
        NUM_EXPERTS = 8
        TOP_K = 2
        B, S, D = (8, 256, 256)

        def _moe(tokens, router_w, w1, b1, w2, b2):
            N = tokens.shape[0]
            E = router_w.shape[0]
            logits = tokens.astype(jnp.float32) @ router_w.astype(jnp.float32).T
            probs = jax.nn.softmax(logits, axis=-1)
            rw, re = jax.lax.top_k(probs, TOP_K)
            if TOP_K > 1:
                rw = rw / jnp.maximum(rw.sum(-1, keepdims=True), 1e-12)
            rw = rw.astype(tokens.dtype)
            combine = jnp.zeros((N, E), tokens.dtype).at[jnp.arange(N)[:, None], re].set(rw)
            out = tokens
            for e in range(E):
                h = jax.nn.gelu(tokens @ w1[e] + b1[e], approximate=False)
                y = h @ w2[e] + b2[e]
                out = out + combine[:, e:e + 1] * y
            return out
        key = jax.random.key(seed)
        ks = jax.random.split(key, 4)
        scale = 1.0 / np.sqrt(D).astype(np.float32)
        return {'input_embeddings': jax.random.normal(ks[0], (B, S, D), jnp.float32), 'router_w': jax.random.normal(ks[1], (NUM_EXPERTS, D), jnp.float32) * scale, 'w1': jax.random.normal(ks[2], (NUM_EXPERTS, D, D), jnp.float32) * scale, 'b1': jnp.zeros((NUM_EXPERTS, D), jnp.float32), 'w2': jax.random.normal(ks[3], (NUM_EXPERTS, D, D), jnp.float32) * scale, 'b2': jnp.zeros((NUM_EXPERTS, D), jnp.float32)}
    _L3_ffn_all = _L3_ffn_setup()
    _L3_ffn_in = {k: v for k, v in _L3_ffn_all.items() if k in ('router_w', 'w1', 'b1', 'w2', 'b2')}
    del _L3_ffn_all
    return {'x': x, 'src': src, 'dst': dst, 'edge_weight': edge_weight, 'edge_weight_n2': edge_weight_n2, 'L0_gnn_weight_low': _L0_gnn_in['weight_low'], 'L0_gnn_weight_high': _L0_gnn_in['weight_high'], 'L0_gnn_weight_mlp': _L0_gnn_in['weight_mlp'], 'L0_gnn_att_vec_low': _L0_gnn_in['att_vec_low'], 'L0_gnn_att_vec_high': _L0_gnn_in['att_vec_high'], 'L0_gnn_att_vec_mlp': _L0_gnn_in['att_vec_mlp'], 'L0_gnn_att_vec': _L0_gnn_in['att_vec'], 'L0_mix_wq': _L0_mix_in['wq'], 'L0_mix_bq': _L0_mix_in['bq'], 'L0_mix_wk': _L0_mix_in['wk'], 'L0_mix_bk': _L0_mix_in['bk'], 'L0_mix_wv': _L0_mix_in['wv'], 'L0_mix_bv': _L0_mix_in['bv'], 'L0_mix_wo': _L0_mix_in['wo'], 'L0_mix_bo': _L0_mix_in['bo'], 'L0_ffn_gamma': _L0_ffn_in['gamma'], 'L0_ffn_beta': _L0_ffn_in['beta'], 'L0_ffn_Wr': _L0_ffn_in['Wr'], 'L0_ffn_br': _L0_ffn_in['br'], 'L0_ffn_W1': _L0_ffn_in['W1'], 'L0_ffn_b1': _L0_ffn_in['b1'], 'L0_ffn_W2': _L0_ffn_in['W2'], 'L0_ffn_b2': _L0_ffn_in['b2'], 'L1_gnn_W': _L1_gnn_in['W'], 'L1_gnn_M': _L1_gnn_in['M'], 'L1_mix_Wq': _L1_mix_in['Wq'], 'L1_mix_bq': _L1_mix_in['bq'], 'L1_mix_Wk': _L1_mix_in['Wk'], 'L1_mix_bk': _L1_mix_in['bk'], 'L1_mix_Wv': _L1_mix_in['Wv'], 'L1_mix_bv': _L1_mix_in['bv'], 'L1_mix_Wfc': _L1_mix_in['Wfc'], 'L1_mix_bfc': _L1_mix_in['bfc'], 'L1_ffn_router_w': _L1_ffn_in['router_w'], 'L1_ffn_router_b': _L1_ffn_in['router_b'], 'L1_ffn_W1': _L1_ffn_in['W1'], 'L1_ffn_b1': _L1_ffn_in['b1'], 'L1_ffn_W2': _L1_ffn_in['W2'], 'L1_ffn_b2': _L1_ffn_in['b2'], 'L2_gnn_W': _L2_gnn_in['W'], 'L2_gnn_b': _L2_gnn_in['b'], 'L2_gnn_bn1_gamma': _L2_gnn_in['bn1_gamma'], 'L2_gnn_bn1_beta': _L2_gnn_in['bn1_beta'], 'L2_gnn_bn1_mean': _L2_gnn_in['bn1_mean'], 'L2_gnn_bn1_var': _L2_gnn_in['bn1_var'], 'L2_gnn_bn2_gamma': _L2_gnn_in['bn2_gamma'], 'L2_gnn_bn2_beta': _L2_gnn_in['bn2_beta'], 'L2_gnn_bn2_mean': _L2_gnn_in['bn2_mean'], 'L2_gnn_bn2_var': _L2_gnn_in['bn2_var'], 'L2_mix_ln1_w': _L2_mix_in['ln1_w'], 'L2_mix_ln1_b': _L2_mix_in['ln1_b'], 'L2_mix_Wx': _L2_mix_in['Wx'], 'L2_mix_bx': _L2_mix_in['bx'], 'L2_mix_Wq': _L2_mix_in['Wq'], 'L2_mix_Wk': _L2_mix_in['Wk'], 'L2_mix_Wv': _L2_mix_in['Wv'], 'L2_mix_Wo': _L2_mix_in['Wo'], 'L2_mix_bo': _L2_mix_in['bo'], 'L2_mix_ln2_w': _L2_mix_in['ln2_w'], 'L2_mix_ln2_b': _L2_mix_in['ln2_b'], 'L2_mix_W1': _L2_mix_in['W1'], 'L2_mix_b1': _L2_mix_in['b1'], 'L2_mix_W2': _L2_mix_in['W2'], 'L2_mix_b2': _L2_mix_in['b2'], 'L2_ffn_W_gat': _L2_ffn_in['W_gat'], 'L2_ffn_att_src': _L2_ffn_in['att_src'], 'L2_ffn_att_dst': _L2_ffn_in['att_dst'], 'L2_ffn_b_gat': _L2_ffn_in['b_gat'], 'L2_ffn_ln_gamma': _L2_ffn_in['ln_gamma'], 'L2_ffn_ln_beta': _L2_ffn_in['ln_beta'], 'L2_ffn_W1': _L2_ffn_in['W1'], 'L2_ffn_b1': _L2_ffn_in['b1'], 'L2_ffn_W2': _L2_ffn_in['W2'], 'L2_ffn_b2': _L2_ffn_in['b2'], 'L2_ffn_edge_index': _L2_ffn_in['edge_index'], 'L3_gnn_W1': _L3_gnn_in['W1'], 'L3_gnn_b1': _L3_gnn_in['b1'], 'L3_gnn_W2': _L3_gnn_in['W2'], 'L3_gnn_b2': _L3_gnn_in['b2'], 'L3_gnn_a': _L3_gnn_in['a'], 'L3_mix_Wq': _L3_mix_in['Wq'], 'L3_mix_Wkv': _L3_mix_in['Wkv'], 'L3_mix_Wproj': _L3_mix_in['Wproj'], 'L3_mix_bproj': _L3_mix_in['bproj'], 'L3_ffn_router_w': _L3_ffn_in['router_w'], 'L3_ffn_w1': _L3_ffn_in['w1'], 'L3_ffn_b1': _L3_ffn_in['b1'], 'L3_ffn_w2': _L3_ffn_in['w2'], 'L3_ffn_b2': _L3_ffn_in['b2']}

def reference(x, src, dst, edge_weight, edge_weight_n2, L0_gnn_weight_low, L0_gnn_weight_high, L0_gnn_weight_mlp, L0_gnn_att_vec_low, L0_gnn_att_vec_high, L0_gnn_att_vec_mlp, L0_gnn_att_vec, L0_mix_wq, L0_mix_bq, L0_mix_wk, L0_mix_bk, L0_mix_wv, L0_mix_bv, L0_mix_wo, L0_mix_bo, L0_ffn_gamma, L0_ffn_beta, L0_ffn_Wr, L0_ffn_br, L0_ffn_W1, L0_ffn_b1, L0_ffn_W2, L0_ffn_b2, L1_gnn_W, L1_gnn_M, L1_mix_Wq, L1_mix_bq, L1_mix_Wk, L1_mix_bk, L1_mix_Wv, L1_mix_bv, L1_mix_Wfc, L1_mix_bfc, L1_ffn_router_w, L1_ffn_router_b, L1_ffn_W1, L1_ffn_b1, L1_ffn_W2, L1_ffn_b2, L2_gnn_W, L2_gnn_b, L2_gnn_bn1_gamma, L2_gnn_bn1_beta, L2_gnn_bn1_mean, L2_gnn_bn1_var, L2_gnn_bn2_gamma, L2_gnn_bn2_beta, L2_gnn_bn2_mean, L2_gnn_bn2_var, L2_mix_ln1_w, L2_mix_ln1_b, L2_mix_Wx, L2_mix_bx, L2_mix_Wq, L2_mix_Wk, L2_mix_Wv, L2_mix_Wo, L2_mix_bo, L2_mix_ln2_w, L2_mix_ln2_b, L2_mix_W1, L2_mix_b1, L2_mix_W2, L2_mix_b2, L2_ffn_W_gat, L2_ffn_att_src, L2_ffn_att_dst, L2_ffn_b_gat, L2_ffn_ln_gamma, L2_ffn_ln_beta, L2_ffn_W1, L2_ffn_b1, L2_ffn_W2, L2_ffn_b2, L2_ffn_edge_index, L3_gnn_W1, L3_gnn_b1, L3_gnn_W2, L3_gnn_b2, L3_gnn_a, L3_mix_Wq, L3_mix_Wkv, L3_mix_Wproj, L3_mix_bproj, L3_ffn_router_w, L3_ffn_w1, L3_ffn_b1, L3_ffn_w2, L3_ffn_b2):
    import jax
    import jax.numpy as jnp

    def _L0_gnn_ref(x, val_low, val_high, weight_low, weight_high, weight_mlp, att_vec_low, att_vec_high, att_vec_mlp, att_vec, row, col):
        import jax, jax.numpy as jnp
        import numpy as np
        N = 50000
        E = 25000
        D_IN = 256
        D_OUT = 256

        def _spmm(row, col, val, h, n_nodes):
            return jax.ops.segment_sum(val[:, None] * h[col], row, num_segments=n_nodes)
        if __name__ == '__main__':
            out = reference(**setup_inputs())
            print(out.shape, out.dtype)
        n = x.shape[0]
        output_low = jax.nn.relu(_spmm(row, col, val_low, x @ weight_low, n))
        output_high = jax.nn.relu(_spmm(row, col, val_high, x @ weight_high, n))
        output_mlp = jax.nn.relu(x @ weight_mlp)
        T = 3.0
        logits = jnp.concatenate([output_low @ att_vec_low, output_high @ att_vec_high, output_mlp @ att_vec_mlp], axis=1)
        att = jax.nn.softmax(jax.nn.sigmoid(logits) @ att_vec / T, axis=1)
        return 3.0 * (att[:, 0:1] * output_low + att[:, 1:2] * output_high + att[:, 2:3] * output_mlp)

    def _L0_mix_ref(x, wq, bq, wk, bk, wv, bv, wo, bo):
        import jax, jax.numpy as jnp
        import numpy as np
        D_MODEL = 256
        NUM_HEADS = 8
        DEPTH = D_MODEL // NUM_HEADS
        B, L = (32, 128)

        def _feature_map(x):
            return jax.nn.elu(x) + 1.0
        b, l, _ = x.shape
        q = (x @ wq + bq).reshape(b, l, NUM_HEADS, DEPTH)
        k = (x @ wk + bk).reshape(b, l, NUM_HEADS, DEPTH)
        v = (x @ wv + bv).reshape(b, l, NUM_HEADS, DEPTH)
        q = _feature_map(q)
        k = _feature_map(k)
        kv = jnp.einsum('blhd,blhe->bhde', k, v)
        k_sum = jnp.sum(k, axis=1)
        qkv = jnp.einsum('blhd,bhde->blhe', q, kv)
        normalizer = jnp.einsum('blhd,bhd->blh', q, k_sum) + 1e-06
        out = qkv / normalizer[..., None]
        out = out.reshape(b, l, D_MODEL)
        return out @ wo + bo

    def _L0_ffn_ref(x, gamma, beta, Wr, br, W1, b1, W2, b2):
        import jax, jax.numpy as jnp
        import numpy as np
        E = 8
        K = 2
        D = 256
        H = 512
        DOUT = 256
        EPS = 1e-05
        mu = jnp.mean(x, axis=-1, keepdims=True)
        var = jnp.mean(jnp.square(x - mu), axis=-1, keepdims=True)
        xn = (x - mu) * jax.lax.rsqrt(var + EPS) * gamma + beta
        logits = jnp.einsum('bsd,de->bse', xn, Wr) + br
        top_vals, top_idx = jax.lax.top_k(logits, K)
        w = jax.nn.softmax(top_vals, axis=-1)
        w_full = jnp.einsum('bsk,bske->bse', w, jax.nn.one_hot(top_idx, E, dtype=w.dtype))
        y = jnp.zeros(x.shape[:-1] + (DOUT,), x.dtype)
        for e in range(E):
            h = jax.nn.gelu(jnp.einsum('bsd,dh->bsh', xn, W1[e]) + b1[e], approximate=False)
            y_e = jnp.einsum('bsh,hd->bsd', h, W2[e]) + b2[e]
            y = y + y_e * w_full[..., e, None]
        return y

    def _L1_gnn_ref(x, W, M, edge_src, edge_dst):
        import jax, jax.numpy as jnp
        import numpy as np
        N_NODES = 10000
        N_EDGES = 10000
        D = 256
        self_term = x @ W
        msg = x @ M
        agg = jax.ops.segment_sum(msg[edge_src], edge_dst, num_segments=x.shape[0])
        return jax.nn.relu(self_term + agg)

    def _L1_mix_ref(x, Wq, bq, Wk, bk, Wv, bv, Wfc, bfc):
        import jax, jax.numpy as jnp
        import numpy as np
        B, L, D, H = (4, 512, 256, 8)
        DK = D // H

        def _heads(t):
            b, l, d = t.shape
            return t.reshape(b, l, H, DK).transpose(0, 2, 1, 3)
        q = _heads(x @ Wq.T + bq)
        k = _heads(x @ Wk.T + bk)
        v = _heads(x @ Wv.T + bv)
        seq_len = q.shape[-2]
        p_attn = jnp.einsum('bhnd,bhne->bhde', k, v) / seq_len
        out = jnp.einsum('bhnd,bhde->bhne', q, p_attn)
        out = out.transpose(0, 2, 1, 3).reshape(x.shape[0], seq_len, H * DK)
        return out @ Wfc.T + bfc

    def _L1_ffn_ref(x, router_w, router_b, W1, b1, W2, b2):
        import jax, jax.numpy as jnp
        import numpy as np
        B, K, D = (512, 16, 256)
        E = 32
        H = int(D * 0.25)
        xf = x.reshape(-1, D)
        logits = xf @ router_w.T + router_b
        idx = jnp.argmax(logits, axis=-1)
        w1t = jnp.take(W1, idx, axis=0)
        h = jnp.einsum('nd,ndh->nh', xf, w1t) + jnp.take(b1, idx, axis=0)
        h = jax.nn.relu(h)
        w2t = jnp.take(W2, idx, axis=0)
        out = jnp.einsum('nh,nhd->nd', h, w2t) + jnp.take(b2, idx, axis=0)
        out = jax.nn.relu(out)
        return out.reshape(x.shape)

    def _L2_gnn_ref(x, edge_index, W, b, bn1_gamma, bn1_beta, bn1_mean, bn1_var, bn2_gamma, bn2_beta, bn2_mean, bn2_var):
        import jax, jax.numpy as jnp
        import numpy as np
        N_NODES = 50000
        N_EDGES = 25000
        C = 256
        EPS = 1e-05

        def _bn(x, gamma, beta, mean, var):
            return (x - mean) * jax.lax.rsqrt(var + EPS) * gamma + beta
        n = x.shape[0]
        src = edge_index[0]
        dst = edge_index[1]
        x_j = x[src]
        x_i = x[dst]
        msg = jnp.concatenate([x_j - x_i, x_i], axis=-1)
        msg = msg @ W + b
        msg = jax.nn.relu(_bn(msg, bn1_gamma, bn1_beta, bn1_mean, bn1_var))
        agg = jax.ops.segment_max(msg, dst, num_segments=n)
        agg = jnp.where(jnp.isfinite(agg), agg, 0.0)
        out = _bn(agg, bn2_gamma, bn2_beta, bn2_mean, bn2_var)
        return out + x

    def _L2_mix_ref(fx, ln1_w, ln1_b, Wx, bx, Wq, Wk, Wv, Wo, bo, ln2_w, ln2_b, W1, b1, W2, b2):
        import jax, jax.numpy as jnp
        import numpy as np
        B, N, C = (8, 256, 256)
        H, D, S = (8, 32, 32)
        HID = 4 * C

        def layernorm(x, w, b, eps=1e-05):
            mu = jnp.mean(x, axis=-1, keepdims=True)
            var = jnp.mean(jnp.square(x - mu), axis=-1, keepdims=True)
            return (x - mu) * jax.lax.rsqrt(var + eps) * w + b

        def linear_no_attn(x, Wx, bx, Wq, Wk, Wv, Wo, bo):
            x_mid = x @ Wx.T + bx
            x_mid = x_mid.reshape(x.shape[0], x.shape[1], H, D).transpose(0, 2, 1, 3)
            q = jax.nn.softmax(x_mid @ Wq.T, axis=-1)
            k = jax.nn.softmax(x_mid @ Wk.T, axis=-2)
            v = x_mid @ Wv.T
            kv = jnp.einsum('bhns,bhnd->bhsd', k, v)
            qkv = jnp.einsum('bhns,bhsd->bhnd', q, kv)
            qkv = qkv.transpose(0, 2, 1, 3).reshape(x.shape[0], x.shape[1], H * D)
            return qkv @ Wo.T + bo
        h = linear_no_attn(layernorm(fx, ln1_w, ln1_b), Wx, bx, Wq, Wk, Wv, Wo, bo) + fx
        y = layernorm(h, ln2_w, ln2_b)
        y = jax.nn.gelu(y @ W1.T + b1, approximate=False)
        y = y @ W2.T + b2
        return y + h

    def _L2_ffn_ref(x, W_gat, att_src, att_dst, b_gat, ln_gamma, ln_beta, W1, b1, W2, b2, edge_index):
        import jax, jax.numpy as jnp
        import numpy as np
        B, N, D = (16, 128, 256)
        NUM_EXPERTS, TOP_K, HEADS = (4, 2, 4)
        N_EDGES = 32768
        LN_EPS = 1e-05

        def _layernorm(x, g, b):
            mu = x.mean(-1, keepdims=True)
            var = ((x - mu) ** 2).mean(-1, keepdims=True)
            return (x - mu) * jax.lax.rsqrt(var + LN_EPS) * g + b

        def _forward(x, edge_index, W_gat, att_src, att_dst, b_gat, ln_gamma, ln_beta, W1, b1, W2, b2):
            Bc, Nc, Dc = x.shape
            M = Bc * Nc
            x_flat = x.reshape(M, Dc)
            h = (x_flat @ W_gat).reshape(M, HEADS, NUM_EXPERTS)
            loops = jnp.arange(M, dtype=edge_index.dtype)
            src = jnp.concatenate([edge_index[0], loops])
            dst = jnp.concatenate([edge_index[1], loops])
            a_src = (h * att_src).sum(-1)
            a_dst = (h * att_dst).sum(-1)
            e = jax.nn.leaky_relu(a_src[src] + a_dst[dst], negative_slope=0.2)
            e_max = jax.ops.segment_max(e, dst, num_segments=M)
            ee = jnp.exp(e - e_max[dst])
            denom = jax.ops.segment_sum(ee, dst, num_segments=M)
            alpha = ee / (denom[dst] + 1e-16)
            msg = h[src] * alpha[:, :, None]
            agg = jax.ops.segment_sum(msg, dst, num_segments=M).reshape(M, HEADS * NUM_EXPERTS) + b_gat
            scores = _layernorm(agg, ln_gamma, ln_beta).reshape(M, HEADS, NUM_EXPERTS).mean(1)
            scores = scores.reshape(Bc, Nc, NUM_EXPERTS)
            topk_s, topk_i = jax.lax.top_k(scores, TOP_K)
            w = jax.nn.softmax(topk_s, axis=-1)
            out = jnp.zeros_like(x)
            for ei in range(NUM_EXPERTS):
                g = jnp.where(topk_i == ei, w, 0.0).sum(-1)
                hh = jax.nn.gelu(x @ W1[ei] + b1[ei], approximate=False)
                out = out + g[..., None] * (hh @ W2[ei] + b2[ei])
            return out
        return _forward(x, edge_index, W_gat, att_src, att_dst, b_gat, ln_gamma, ln_beta, W1, b1, W2, b2)

    def _L3_gnn_ref(x, edge_index, W1, b1, W2, b2, a):
        import jax, jax.numpy as jnp
        import numpy as np
        N_NODES = 3125
        F_DIM = 256
        NNZ = 50000

        def _prelu(x, a):
            return jnp.where(x >= 0, x, a * x)

        def _hconv(x, W, b, src, dst, n):
            xt = x @ W
            ones = jnp.ones(src.shape, xt.dtype)
            D = jax.ops.segment_sum(ones, src, num_segments=n)
            B = jax.ops.segment_sum(ones, dst, num_segments=n)
            Dinv = jnp.where(D > 0, 1.0 / D, 0.0)
            Binv = jnp.where(B > 0, 1.0 / B, 0.0)
            m = jax.ops.segment_sum(xt[src], dst, num_segments=n) * Binv[:, None]
            out = jax.ops.segment_sum(m[dst], src, num_segments=n) * Dinv[:, None]
            return out + b
        src, dst = (edge_index[0], edge_index[1])
        n = x.shape[0]
        h = _prelu(_hconv(x, W1, b1, src, dst, n), a)
        h = _hconv(h, W2, b2, src, dst, n) + x
        return _prelu(h, a)

    def _L3_mix_ref(x, Wq, Wkv, Wproj, bproj):
        import jax, jax.numpy as jnp
        import numpy as np
        NUM_HEADS = 8
        B, N, C = x.shape
        h = NUM_HEADS
        d = C // h
        q = jnp.einsum('bnc,oc->bno', x, Wq).reshape(B, N, h, d).transpose(0, 2, 1, 3)
        kv = jnp.einsum('bnc,oc->bno', x, Wkv).reshape(B, N, 2, h, d)
        k = kv[:, :, 0].transpose(0, 2, 1, 3)
        v = kv[:, :, 1].transpose(0, 2, 1, 3)
        q = jax.nn.elu(q) + 1.0
        k = jax.nn.elu(k) + 1.0
        k_sum = k.sum(axis=2)
        D_inv = 1.0 / jnp.maximum(jnp.einsum('bhnd,bhd->bhn', q, k_sum), 1e-06)
        context = jnp.einsum('bhnd,bhne->bhde', k, v)
        attn = jnp.einsum('bhnd,bhde->bhne', q, context) * D_inv[..., None]
        out = attn.transpose(0, 2, 1, 3).reshape(B, N, C)
        out = jnp.einsum('bnc,oc->bno', out, Wproj) + bproj
        return out

    def _L3_ffn_ref(input_embeddings, router_w, w1, b1, w2, b2):
        import jax, jax.numpy as jnp
        import numpy as np
        NUM_EXPERTS = 8
        TOP_K = 2
        B, S, D = (8, 256, 256)

        def _moe(tokens, router_w, w1, b1, w2, b2):
            N = tokens.shape[0]
            E = router_w.shape[0]
            logits = tokens.astype(jnp.float32) @ router_w.astype(jnp.float32).T
            probs = jax.nn.softmax(logits, axis=-1)
            rw, re = jax.lax.top_k(probs, TOP_K)
            if TOP_K > 1:
                rw = rw / jnp.maximum(rw.sum(-1, keepdims=True), 1e-12)
            rw = rw.astype(tokens.dtype)
            combine = jnp.zeros((N, E), tokens.dtype).at[jnp.arange(N)[:, None], re].set(rw)
            out = tokens
            for e in range(E):
                h = jax.nn.gelu(tokens @ w1[e] + b1[e], approximate=False)
                y = h @ w2[e] + b2[e]
                out = out + combine[:, e:e + 1] * y
            return out
        b, s, d = input_embeddings.shape
        tokens = input_embeddings.reshape(b * s, d)
        return _moe(tokens, router_w, w1, b1, w2, b2).reshape(b, s, d)
    edge_index = jnp.stack([src, dst])
    xn = _layernorm(x, axis=-1)
    x = x + _L0_gnn_ref(xn, edge_weight, edge_weight_n2, L0_gnn_weight_low, L0_gnn_weight_high, L0_gnn_weight_mlp, L0_gnn_att_vec_low, L0_gnn_att_vec_high, L0_gnn_att_vec_mlp, L0_gnn_att_vec, src, dst) + _L0_mix_ref(xn[None], L0_mix_wq, L0_mix_bq, L0_mix_wk, L0_mix_bk, L0_mix_wv, L0_mix_bv, L0_mix_wo, L0_mix_bo)[0]
    x = x + _L0_ffn_ref(_layernorm(x, axis=-1)[None], L0_ffn_gamma, L0_ffn_beta, L0_ffn_Wr, L0_ffn_br, L0_ffn_W1, L0_ffn_b1, L0_ffn_W2, L0_ffn_b2)[0]
    xn = _layernorm(x, axis=-1)
    x = x + _L1_gnn_ref(xn, L1_gnn_W, L1_gnn_M, src, dst) + _L1_mix_ref(xn[None], L1_mix_Wq, L1_mix_bq, L1_mix_Wk, L1_mix_bk, L1_mix_Wv, L1_mix_bv, L1_mix_Wfc, L1_mix_bfc)[0]
    x = x + _L1_ffn_ref(_layernorm(x, axis=-1)[None], L1_ffn_router_w, L1_ffn_router_b, L1_ffn_W1, L1_ffn_b1, L1_ffn_W2, L1_ffn_b2)[0]
    xn = _layernorm(x, axis=-1)
    x = x + _L2_gnn_ref(xn, edge_index, L2_gnn_W, L2_gnn_b, L2_gnn_bn1_gamma, L2_gnn_bn1_beta, L2_gnn_bn1_mean, L2_gnn_bn1_var, L2_gnn_bn2_gamma, L2_gnn_bn2_beta, L2_gnn_bn2_mean, L2_gnn_bn2_var) + _L2_mix_ref(xn[None], L2_mix_ln1_w, L2_mix_ln1_b, L2_mix_Wx, L2_mix_bx, L2_mix_Wq, L2_mix_Wk, L2_mix_Wv, L2_mix_Wo, L2_mix_bo, L2_mix_ln2_w, L2_mix_ln2_b, L2_mix_W1, L2_mix_b1, L2_mix_W2, L2_mix_b2)[0]
    x = x + _L2_ffn_ref(_layernorm(x, axis=-1)[None], L2_ffn_W_gat, L2_ffn_att_src, L2_ffn_att_dst, L2_ffn_b_gat, L2_ffn_ln_gamma, L2_ffn_ln_beta, L2_ffn_W1, L2_ffn_b1, L2_ffn_W2, L2_ffn_b2, L2_ffn_edge_index)[0]
    xn = _layernorm(x, axis=-1)
    x = x + _L3_gnn_ref(xn, edge_index, L3_gnn_W1, L3_gnn_b1, L3_gnn_W2, L3_gnn_b2, L3_gnn_a) + _L3_mix_ref(xn[None], L3_mix_Wq, L3_mix_Wkv, L3_mix_Wproj, L3_mix_bproj)[0]
    x = x + _L3_ffn_ref(_layernorm(x, axis=-1)[None], L3_ffn_router_w, L3_ffn_w1, L3_ffn_b1, L3_ffn_w2, L3_ffn_b2)[0]
    return x

_drawn_inputs = setup_inputs


def setup_inputs(seed=0):
    import zlib

    import numpy as np

    out = dict(_drawn_inputs(seed))
    spreads = {'L0_mix_bq': (0.0, 0.8),
     'L0_mix_bk': (0.0, 0.8),
     'L0_mix_bv': (0.0, 0.1),
     'L0_mix_bo': (0.0, 0.1),
     'L0_ffn_br': (0.0, 0.1),
     'L1_mix_bq': (0.0, 0.8),
     'L1_mix_bk': (0.0, 0.8),
     'L1_mix_bv': (0.0, 0.8),
     'L1_mix_bfc': (0.0, 0.8),
     'L2_gnn_b': (0.0, 2.0),
     'L2_gnn_bn1_gamma': (1.0, 0.6),
     'L2_gnn_bn1_beta': (0.0, 2.0),
     'L2_gnn_bn2_gamma': (1.0, 0.6),
     'L2_gnn_bn2_beta': (0.0, 2.0),
     'L2_mix_ln1_w': (1.0, 0.6),
     'L2_mix_ln1_b': (0.0, 0.8),
     'L2_mix_ln2_w': (1.0, 0.6),
     'L2_mix_ln2_b': (0.0, 0.8),
     'L2_ffn_b_gat': (0.0, 0.8),
     'L2_ffn_ln_gamma': (1.0, 0.6),
     'L2_ffn_ln_beta': (0.0, 0.8),
     'L2_ffn_b1': (0.0, 2.0),
     'L2_ffn_b2': (0.0, 2.0),
     'L3_gnn_b1': (0.0, 2.0),
     'L3_gnn_b2': (0.0, 2.0),
     'L3_mix_bproj': (0.0, 2.0),
     'L3_ffn_b1': (0.0, 2.0),
     'L3_ffn_b2': (0.0, 2.0)}
    factors = {'edge_weight': 2.756,
     'edge_weight_n2': 2.712,
     'L0_gnn_att_vec_low': 8.0,
     'L0_gnn_att_vec_high': 8.0,
     'L0_gnn_att_vec_mlp': 8.0,
     'L0_gnn_att_vec': 3.853,
     'L0_mix_wq': 8.0,
     'L0_ffn_gamma': 7.924,
     'L0_ffn_beta': 4.675,
     'L0_ffn_b1': 4.959,
     'L1_mix_Wq': 8.0,
     'L1_mix_Wk': 8.0,
     'L1_mix_Wv': 8.0,
     'L1_mix_Wfc': 8.0,
     'L1_ffn_router_w': 8.0,
     'L1_ffn_router_b': 8.0,
     'L1_ffn_W1': 8.0,
     'L1_ffn_b1': 8.0,
     'L1_ffn_W2': 8.0,
     'L1_ffn_b2': 8.0,
     'L2_gnn_W': 183.808,
     'L2_gnn_bn1_mean': 200.0,
     'L2_gnn_bn1_var': 200.0,
     'L2_gnn_bn2_mean': 200.0,
     'L2_gnn_bn2_var': 200.0,
     'L2_mix_Wx': 8.0,
     'L2_mix_bx': 8.0,
     'L2_mix_Wq': 8.0,
     'L2_mix_Wk': 8.0,
     'L2_mix_Wv': 8.0,
     'L2_mix_Wo': 8.0,
     'L2_mix_bo': 200.0,
     'L2_mix_W1': 8.0,
     'L2_mix_b1': 54.776,
     'L2_mix_W2': 8.0,
     'L2_mix_b2': 200.0,
     'L2_ffn_W_gat': 8.0,
     'L2_ffn_att_src': 8.0,
     'L2_ffn_att_dst': 8.0,
     'L2_ffn_W1': 8.0,
     'L2_ffn_W2': 8.0,
     'L3_gnn_W1': 8.0,
     'L3_gnn_W2': 8.0,
     'L3_mix_Wq': 200.0,
     'L3_mix_Wkv': 8.0,
     'L3_mix_Wproj': 8.0,
     'L3_ffn_router_w': 8.0,
     'L3_ffn_w1': 8.0,
     'L3_ffn_w2': 7.607}
    for name, (base, spread) in spreads.items():
        noise = np.random.default_rng([zlib.crc32(name.encode()), seed]).standard_normal(out[name].shape)
        drawn = base * np.exp(spread * noise) if base else spread * noise
        out[name] = jnp.asarray(drawn.astype(out[name].dtype))
    for name, factor in factors.items():
        out[name] = (out[name] * factor).astype(out[name].dtype)
    return out
```

```python
from contextlib import ExitStack

import concourse.bass as bass
from concourse import mybir

F32 = mybir.dt.float32
BF16 = mybir.dt.bfloat16
I32 = mybir.dt.int32
U32 = mybir.dt.uint32
ALU = mybir.AluOpType
ACT = mybir.ActivationFunctionType
AX_X = mybir.AxisListType.X

N = 3125
D = 256
TP = 125
NT = N // TP
KC = D // 128
U = 5
E_MAIN = 50000
E_GAT = 32768
EDGES = 128
NULL_KEY = 127.0
FAR = 1.0e30
EPS = 1e-5


def edge_tiles(edges):
    return (edges + NT * (EDGES - 1)) // EDGES


ET_MAIN = -(-edge_tiles(E_MAIN) // 16) * 16
ET_GAT = -(-edge_tiles(E_GAT) // 20) * 20
ET_PAD = 8


def run_slots(eng, count, unroll, phases):
    def slot(first, j):
        for lag, phase in phases:
            piece = first + (j - lag)
            if isinstance(piece, int) and not 0 <= piece < count:
                continue
            phase(piece, (j - lag) % unroll)

    assert count % unroll == 0 and all(lag <= unroll for lag, _ in phases)
    peeled = 2 if max(lag for lag, _ in phases) > 0 else 1
    for i in range(peeled * unroll):
        slot(i - i % unroll, i % unroll)
    with eng.Fori(peeled, count // unroll) as r:
        for j in range(unroll):
            slot(r * unroll, j)
    for j in range(max(lag for lag, _ in phases)):
        slot(count, j)


def at(tile, count=TP):
    return bass.ds(tile * count, count)


class Core:

    def __init__(self, nc, ctx):
        self.nc, self.ctx = nc, ctx

    def keep(self, name, shape, dt=F32):
        return self.ctx.enter_context(self.nc.sbuf_tensor(name, shape, dt))

    def software_dma_semaphore(self, name):
        return self.ctx.enter_context(self.nc.semaphore(name))


def constants(core):
    nc = core.nc
    core.col_i = core.keep("col_i", [128, 128], I32)
    core.row_i = core.keep("row_i", [128, 1], I32)
    core.col = core.keep("col", [128, 128])
    core.row = core.keep("row", [128, 1])
    core.ident = core.keep("ident", [128, 128])
    core.ones = core.keep("ones", [128, 128])
    core.zeros = core.keep("zeros", [128, 128])
    core.wide_zeros = core.keep("wide_zeros", [128, D + 4])
    core.same_head = core.keep("same_head", [128, 128])
    core.head_of = core.keep("head_of", [128, 4])
    row_head = core.keep("row_head", [128, 1])
    col_head = core.keep("col_head", [128, 128])
    with nc.semaphore("numbers_written") as numbers_written, nc.Block() as block:
        @block.gpsimd
        def _(pool):
            nc.gpsimd.iota(core.col_i[:], [[1, 128]], base=0, channel_multiplier=0).then_inc(numbers_written, 1)
            nc.gpsimd.iota(core.row_i[:], [[0, 1]], base=0, channel_multiplier=1).then_inc(numbers_written, 1)

        @block.vector
        def _(dve):
            nc.vector.memset(core.ones[:], 1.0)
            nc.vector.memset(core.zeros[:], 0.0)
            nc.vector.memset(core.wide_zeros[:], 0.0)
            dve.wait_ge(numbers_written, 2)
            nc.vector.tensor_copy(core.col[:], core.col_i[:])
            nc.vector.tensor_copy(core.row[:], core.row_i[:])
            dve.drain()
            nc.vector.tensor_scalar(core.ident[:], core.col[:], core.row[:, 0:1], None, ALU.is_equal)
            nc.vector.tensor_scalar(row_head[:], core.row[:], 32.0, None, ALU.is_ge)
            nc.vector.tensor_scalar(col_head[:], core.col[:], 32.0, None, ALU.is_ge)
            for first in (64.0, 96.0):
                dve.drain()
                nc.vector.scalar_tensor_tensor(row_head[:], core.row[:], first, row_head[:], ALU.is_ge, ALU.add)
                nc.vector.scalar_tensor_tensor(col_head[:], core.col[:], first, col_head[:], ALU.is_ge, ALU.add)
            dve.drain()
            nc.vector.tensor_scalar(core.same_head[:], col_head[:], row_head[:, 0:1], None, ALU.is_equal)
            nc.vector.tensor_scalar(core.head_of[:], core.col[:, 0:4], row_head[:, 0:1], None, ALU.is_equal)


def group_edges(core, name, edges, et, key, other, weights, records, edge_group):
    nc = core.nc
    P = 125 if edges % 125 == 0 else 128
    T = edges // P
    G = NT
    K, B = 8, 2
    CH = 16
    record_slots = nc.dram_tensor(f"{name}_record_slots", (128 * et, 4), F32).ap()
    with ExitStack() as c:
        def sb(n, shape, dt=F32):
            return c.enter_context(nc.sbuf_tensor(f"{name}_{n}", shape, dt))

        def sem(n):
            return c.enter_context(nc.semaphore(f"{name}_{n}"))

        key_i = sb("key_i", [P, T], I32)
        other_i = sb("other_i", [P, T], I32)
        key_f = sb("key_f", [P, T])
        weight_s = sb("weight_s", [P, 2, T])
        high = sb("high", [P, T])
        bound = sb("bound", [P, G + 1])
        above = sb("above", [P, T, G + 1])
        member = sb("member", [P, T, G], BF16)
        rank = sb("rank", [P, T, G])
        before = sb("before", [P, T + 1, G])
        upper = sb("upper", [P, P], BF16)
        ones_b = sb("ones_b", [P, P], BF16)
        zero_row = sb("zero_row", [P, T])
        count_i = sb("count_i", [P, G], I32)
        tiles_f = sb("tiles_f", [P, G])
        tile_end = sb("tile_end", [P, G])
        slot_start = sb("slot_start", [P, G])
        pos = sb("pos", [P, T])
        pos_i = sb("pos_i", [P, T], I32)
        part_i = sb("part_i", [P, T], I32)
        tile_i = sb("tile_i", [P, T], I32)
        tile_f = sb("tile_f", [P, T])
        rec = sb("rec", [P, T, 4])
        null = sb("null", [128, et * 4])
        number_i = sb("number_i", [1, et + ET_PAD], I32)
        number = sb("number", [1, et + ET_PAD])
        group_f = sb("group_f", [1, et + ET_PAD])
        slot_s = sb("slot_s", [P, B, K], I32)
        rec_s = sb("rec_s", [P, B, K, 4])
        counts = c.enter_context(nc.psum_tensor(f"{name}_counts", [P, 4, 2, 512], F32))
        lists_landed = sem("lists_landed")
        nulls_made = sem("nulls_made")
        nulls_stored = sem("nulls_stored")
        numbers_made = sem("numbers_made")
        members_made = sem("members_made")
        counts_made = sem("counts_made")
        counts_read = sem("counts_read")
        staged = sem("staged")
        batch_begun = sem("batch_begun")
        scattered = [core.software_dma_semaphore(f"{name}_scattered{b}") for b in range(B)]
        records_landed = sem("records_landed")
        block = c.enter_context(nc.Block())
        CN = T // CH
        R = T // (K * B)

        @block.sync
        def _(sp):
            sp.dma_start(key_i[:], key.rearrange("(p t) -> p t", p=P)).then_inc(lists_landed, 16)
            sp.dma_start(other_i[:], other.rearrange("(p t) -> p t", p=P)).then_inc(lists_landed, 16)
            for w, weight in enumerate(weights):
                sp.dma_start(weight_s[:, w, :], weight.rearrange("(p t) -> p t", p=P)).then_inc(lists_landed, 16)
            sp.wait_ge(nulls_made, 1)
            sp.dma_start(record_slots.rearrange("(p t) w -> p (t w)", p=128), null[:]).then_inc(nulls_stored, 16)
            for b in range(B):
                sp.wait_ge(scattered[b], 16 * K * R)
            sp.dma_start(records[:, 0:et, :], record_slots.rearrange("(p t) w -> p t w", p=128)).then_inc(records_landed, 16)
            sp.wait_ge(records_landed, 16)

        @block.gpsimd
        def _(pool):
            nc.gpsimd.iota(number_i[:], [[1, et + ET_PAD]], base=0, channel_multiplier=0).then_inc(numbers_made, 1)
            pool.wait_ge(nulls_stored, 16)
            with pool.Fori(0, R) as r:
                for b in range(B):
                    pool.wait_ge(staged, r * B + b + 1)
                    pool.sem_inc(batch_begun, 1)
                    for k in range(K):
                        nc.gpsimd.indirect_dma_start(
                            out=record_slots,
                            out_offset=bass.IndirectOffsetOnAxis(ap=slot_s[:, b, k:k + 1].bitcast(U32), axis=0),
                            in_=rec_s[:, b, k, :], in_offset=None).then_inc(scattered[b], 16)

        @block.tensor
        def _(pe):
            pe.wait_ge(members_made, 1)
            for n in range(CN):
                if n >= 4:
                    pe.wait_ge(counts_read, n - 3)
                rhs = member[:, n * CH:(n + 1) * CH, :]
                nc.tensor.matmul(counts[:, n % 4, 0, 0:CH * G], upper[:], rhs, start=True, stop=True)
                nc.tensor.matmul(counts[:, n % 4, 1, 0:CH * G], ones_b[:], rhs, start=True, stop=True).then_inc(counts_made, 1)

        @block.scalar
        def _(act):
            for n in range(CN):
                act.wait_ge(counts_made, n + 1)
                nc.scalar.copy(rank[:, n * CH:(n + 1) * CH, :], counts[:, n % 4, 0, 0:CH * G])
                nc.scalar.copy(above[:, n * CH:(n + 1) * CH, 0:G], counts[:, n % 4, 1, 0:CH * G]).then_inc(counts_read, 1)

        @block.vector
        def _(dve):
            v = nc.vector
            v.memset(null[:], 0.0)
            v.memset(zero_row[:], 0.0)
            v.memset(ones_b[:], 1.0)
            v.memset(before[:, 0, :], 0.0)
            v.memset(records[:, et:et + ET_PAD, :], 0.0)
            if len(weights) < 2:
                v.memset(rec[:, :, 2 + len(weights):4], 0.0)
            v.tensor_scalar(upper[:], core.col[0:P, 0:P], core.row[0:P, 0:1], None, ALU.is_gt)
            v.tensor_scalar(bound[:], core.col[0:P, 0:G + 1], float(TP), None, ALU.mult)
            dve.drain()
            v.memset(null[:].rearrange("p (t w) -> p t w", w=4)[:, :, 1:2], NULL_KEY)
            v.memset(records[:, et:et + ET_PAD, 1:2], NULL_KEY)
            dve.drain().then_inc(nulls_made, 1)
            dve.wait_ge(lists_landed, 16 * (2 + len(weights)))
            v.tensor_copy(key_f[:], key_i[:])
            v.tensor_copy(rec[:, :, 0], other_i[:])
            for w in range(len(weights)):
                v.tensor_copy(rec[:, :, 2 + w], weight_s[:, w, :])
            dve.drain()
            v.tensor_tensor(above[:], key_f[:].unsqueeze(2).broadcast_to([P, T, G + 1]),
                            bound[:].unsqueeze(1).broadcast_to([P, T, G + 1]), ALU.is_ge)
            dve.drain()
            v.tensor_tensor(member[:], above[:, :, 0:G], above[:, :, 1:G + 1], ALU.subtract)
            v.tensor_reduce(high[:], above[:, :, 1:G], AX_X, ALU.add)
            dve.drain().then_inc(members_made, 1)
            v.scalar_tensor_tensor(rec[:, :, 1], high[:], -float(TP), key_f[:], ALU.mult, ALU.add)
            dve.wait_ge(counts_read, CN)
            for g in range(G):
                v.tensor_tensor_scan(before[:, 1:T + 1, g], above[:, 0:T, g], zero_row[:], 0.0, ALU.add, ALU.add)
            dve.drain()
            v.tensor_scalar(count_i[:], before[:, T, :], float(EDGES - 1), None, ALU.add)
            dve.drain()
            v.tensor_scalar(count_i[:], count_i[:], 7, None, ALU.arith_shift_right)
            dve.drain()
            v.tensor_copy(tiles_f[:], count_i[:])
            dve.drain()
            v.tensor_tensor_scan(tile_end[:], tiles_f[:], zero_row[:, 0:G], 0.0, ALU.add, ALU.add)
            v.tensor_tensor(rank[:], rank[:], before[:, 0:T, :], ALU.add)
            dve.drain()
            v.tensor_tensor(slot_start[:], tile_end[:], tiles_f[:], ALU.subtract)
            dve.drain()
            v.tensor_scalar(slot_start[:], slot_start[:], float(EDGES), None, ALU.mult)
            dve.drain()
            v.tensor_tensor(rank[:], rank[:], slot_start[:].unsqueeze(1).broadcast_to([P, T, G]), ALU.add)
            dve.drain()
            v.tensor_tensor(rank[:], rank[:], member[:], ALU.mult)
            dve.drain()
            v.tensor_reduce(pos[:], rank[:], AX_X, ALU.add)
            dve.drain()
            v.tensor_copy(pos_i[:], pos[:])
            dve.drain()
            v.tensor_scalar(part_i[:], pos_i[:], EDGES - 1, None, ALU.bitwise_and)
            v.tensor_scalar(tile_i[:], pos_i[:], 7, None, ALU.arith_shift_right)
            dve.drain()
            v.tensor_copy(pos[:], part_i[:])
            v.tensor_copy(tile_f[:], tile_i[:])
            dve.drain()
            v.scalar_tensor_tensor(pos_i[:], pos[:], float(et), tile_f[:], ALU.mult, ALU.add)
            dve.drain()


            def stage(r, b):
                t = (r * B + b) * K
                v.tensor_copy(slot_s[:, b, :], pos_i[:, bass.ds(t, K)])
                v.tensor_copy(rec_s[:, b, :, :], rec[:, bass.ds(t, K), :])
                dve.drain().then_inc(staged, 1)

            for b in range(B):
                stage(0, b)
            with dve.Fori(1, R) as r:
                for b in range(B):
                    dve.wait_ge(scattered[b], r * (16 * K))
                    stage(r, b)
            dve.wait_ge(numbers_made, 1)
            v.tensor_copy(number[:], number_i[:])
            v.memset(group_f[:], 0.0)
            dve.drain()
            for g in range(G - 1):
                v.scalar_tensor_tensor(group_f[:], number[:], tile_end[0:1, g:g + 1], group_f[:], ALU.is_ge, ALU.add)
                dve.drain()
            v.tensor_copy(edge_group[:], group_f[:])


def sum_edges(core, name, table, records, edge_group, sums, words=(None,), counted=False):
    nc = core.nc
    K, NB, NP = 4, 4, 2
    Q = ET_MAIN // K
    nw = len(words)
    W = D + 1 if counted else D
    assert not (counted and nw > 1)
    with ExitStack() as c:
        def sb(n, shape, dt=F32):
            return c.enter_context(nc.sbuf_tensor(f"{name}_{n}", shape, dt))

        def sem(n):
            return c.enter_context(nc.semaphore(f"{name}_{n}"))

        index = sb("index", [128, NB, K], I32)
        rows = sb("rows", [128, NB, K, W])
        pick = sb("pick", [128, NB, K, nw, TP])
        psum = c.enter_context(nc.psum_tensor(f"{name}_psum", [128, NP, K, 512], F32))
        indexed = sem("indexed")
        batch_begun = sem("batch_begun")
        gathered = [core.software_dma_semaphore(f"{name}_gathered{b}") for b in range(NB)]
        picked = sem("picked")
        summed = sem("summed")
        added = sem("added")
        sums_cleared = sem("sums_cleared")
        block = c.enter_context(nc.Block())

        def round_of(q, j):
            return (q - j) // NB + 1 if isinstance(q, int) else q // NB + 1

        @block.gpsimd
        def _(pool):
            def gather(q, j):
                pool.wait_ge(indexed, q + 1)
                pool.sem_inc(batch_begun, 1)
                if not (isinstance(q, int) and q < NB):
                    pool.wait_ge(summed, q - (NB - 1))
                    pool.sem_inc(batch_begun, 1)
                for k in range(K):
                    nc.gpsimd.indirect_dma_start(
                        out=rows[:, j, k, 0:D], out_offset=None, in_=table,
                        in_offset=bass.IndirectOffsetOnAxis(ap=index[:, j, k:k + 1].bitcast(U32), axis=0),
                    ).then_inc(gathered[j], 16)

            run_slots(pool, Q, NB, [(0, gather)])

        @block.tensor
        def _(pe):
            def add_up(q, j):
                pe.wait_ge(picked, q + 1)
                pe.wait_ge(gathered[j], (q - j) * (16 * K // NB) + 16 * K)
                if not (isinstance(q, int) and q < NP):
                    pe.wait_ge(added, q - (NP - 1))
                for k in range(K):
                    for w in range(nw):
                        ins = nc.tensor.matmul(psum[0:TP, j % NP, k, w * D:w * D + W], pick[:, j, k, w, :],
                                               rows[:, j, k, :], start=True, stop=True)
                ins.then_inc(summed, 1)

            run_slots(pe, Q, NB, [(0, add_up)])

        @block.vector
        def _(dve):
            v = nc.vector
            v.memset(sums[:], 0.0)
            if counted:
                v.memset(rows[:, :, :, D:D + 1], 1.0)
            dve.drain()

            def number(q, j):
                if not (isinstance(q, int) and q < NB):
                    dve.wait_ge(gathered[j], (q - j) * (16 * K // NB))
                v.tensor_copy(index[:, j, :], records[:, bass.ds(q * K, K), 0])
                dve.drain().then_inc(indexed, 1)

            def choose(q, j):
                if not (isinstance(q, int) and q < NB):
                    dve.wait_ge(summed, q - (NB - 1))
                for k in range(K):
                    t = q * K + k
                    for w, word in enumerate(words):
                        if word is None:
                            v.tensor_scalar(pick[:, j, k, w, :], core.col[:, 0:TP], records[:, bass.ds(t, 1), 1],
                                            None, ALU.is_equal)
                        else:
                            v.tensor_scalar(pick[:, j, k, w, :], core.col[:, 0:TP], records[:, bass.ds(t, 1), 1],
                                            records[:, bass.ds(t, 1), word], ALU.is_equal, ALU.mult)
                dve.drain().then_inc(picked, 1)

            def collect(q, j):
                _, groups = nc.values_load_multi_w_load_instructions(
                    edge_group[0:1, bass.ds(q * K, K)], [mybir.EngineType.DVE], min_val=0, max_val=NT - 1)
                dve.wait_ge(summed, q + 1)
                for k in range(K):
                    total = sums[:, bass.ds(groups[k], 1), :]
                    v.tensor_tensor(total, total, psum[0:TP, j % NP, k, 0:W * nw].unsqueeze(1), ALU.add)
                    last = dve.drain()
                last.then_inc(added, 1)

            run_slots(dve, Q, NB, [(0, number), (1, choose), (3, collect)])


def reuse(eng, sem, piece, j, buffers, unroll=U, each=1):
    back = next(i for i in range(1, unroll + 1) if ((j - i) % unroll) % buffers == j % buffers)
    if not (isinstance(piece, int) and piece < back):
        eng.wait_ge(sem, (piece - (back - 1)) * each)


def layer_norm(core, name, src, normed=None, table=None, turned=None, twice=False, gain=None, shift=None):
    nc = core.nc
    with ExitStack() as c:
        def sb(n, shape, dt=F32):
            return c.enter_context(nc.sbuf_tensor(f"{name}_{n}", shape, dt))

        def sem(n):
            return c.enter_context(nc.semaphore(f"{name}_{n}"))

        stats = sb("stats", [TP, NT, 6])
        mean = sb("mean", [TP, NT])
        var = sb("var", [TP, NT])
        tmp = sb("tmp", [TP, NT])
        dev = sb("dev", [TP, NT])
        scale = sb("scale", [TP, NT])
        dev2 = sb("dev2", [TP, NT])
        out_s = sb("out_s", [TP, U, D])
        pt = c.enter_context(nc.psum_tensor(f"{name}_pt", [128, U, 512], F32))
        var_ready, dev_ready, var2_ready, dev2_ready = sem("var"), sem("dev"), sem("var2"), sem("dev2")
        rows_done, rows_turned, turned_moved, rows_kept = sem("rows_done"), sem("rows_turned"), sem("turned_moved"), sem("rows_kept")
        rows_stored = [sem(f"rows_stored{j}") for j in range(U)]
        block = c.enter_context(nc.Block())

        @block.vector
        def _(dve):
            v = nc.vector
            with dve.Fori(0, NT) as t:
                v.bn_stats(stats[:, bass.ds(t, 1), :], src[:, bass.ds(t, 1), :])
            dve.drain()
            v.tensor_tensor(mean[:], stats[:, :, 1], stats[:, :, 4], ALU.add)
            v.tensor_tensor(tmp[:], stats[:, :, 1], stats[:, :, 4], ALU.subtract)
            v.tensor_tensor(var[:], stats[:, :, 2], stats[:, :, 5], ALU.add)
            dve.drain()
            v.tensor_tensor(tmp[:], tmp[:], tmp[:], ALU.mult)
            v.tensor_scalar(var[:], var[:], 1.0 / D, EPS, ALU.mult, ALU.add)
            dve.drain()
            v.scalar_tensor_tensor(var[:], tmp[:], 0.25, var[:], ALU.mult, ALU.add)
            dve.drain().then_inc(var_ready, 1)
            dve.wait_ge(dev_ready, 1)
            v.reciprocal(scale[:], dev[:])
            dve.drain()
            if twice:
                v.tensor_tensor(tmp[:], scale[:], scale[:], ALU.mult)
                v.tensor_scalar(var[:], var[:], -EPS, None, ALU.add)
                dve.drain()
                v.tensor_tensor(var[:], var[:], tmp[:], ALU.mult)
                dve.drain()
                v.tensor_scalar(var[:], var[:], EPS, None, ALU.add)
                dve.drain().then_inc(var2_ready, 1)
                dve.wait_ge(dev2_ready, 1)
                v.reciprocal(tmp[:], dev2[:])
                dve.drain()
                v.tensor_tensor(scale[:], scale[:], tmp[:], ALU.mult)
                dve.drain()
            v.scalar_tensor_tensor(mean[:], mean[:], -0.5, scale[:], ALU.mult, ALU.mult)
            dve.drain()

            def norm(t, j):
                if turned is not None:
                    reuse(dve, rows_turned, t, j, U)
                if normed is not None:
                    reuse(dve, rows_kept, t, j, U)
                if table is not None and not (isinstance(t, int) and t < U):
                    dve.wait_ge(rows_stored[j], (t - j) * 16 // U if isinstance(t, int) else (t - j) // U * 16)
                v.tensor_scalar(out_s[:, j, :], src[:, bass.ds(t, 1), :], scale[:, bass.ds(t, 1)], mean[:, bass.ds(t, 1)],
                                ALU.mult, ALU.add).then_inc(rows_done, 1)

            run_slots(dve, NT, U, [(0, norm)])

        @block.tensor
        def _(pe):
            def turn(t, j):
                pe.wait_ge(rows_done, t + 1)
                reuse(pe, turned_moved, t, j, U)
                for h in range(KC):
                    ins = nc.tensor.transpose(pt[:, j, h * TP:(h + 1) * TP], out_s[:, j, h * 128:(h + 1) * 128], core.ident[0:TP, 0:TP])
                ins.then_inc(rows_turned, 1)

            if turned is not None:
                run_slots(pe, NT, U, [(0, turn)])

        @block.scalar
        def _(act):
            act.wait_ge(var_ready, 1)
            nc.scalar.activation(dev[:], var[:], ACT.Sqrt).then_inc(dev_ready, 1)
            if twice:
                act.wait_ge(var2_ready, 1)
                nc.scalar.activation(dev2[:], var[:], ACT.Sqrt).then_inc(dev2_ready, 1)

            def move(t, j):
                act.wait_ge(rows_turned, t + 1)
                for h in range(KC):
                    source = pt[:, j, h * TP:(h + 1) * TP]
                    if gain is None:
                        ins = nc.scalar.copy(turned[:, h, at(t)], source)
                    else:
                        ins = nc.scalar.activation(turned[:, h, at(t)], source, ACT.Identity,
                                                   bias=shift[:, h:h + 1], scale=gain[:, h:h + 1])
                ins.then_inc(turned_moved, 1)

            if turned is not None:
                run_slots(act, NT, U, [(0, move)])

        @block.gpsimd
        def _(pool):
            def keep(t, j):
                pool.wait_ge(rows_done, t + 1)
                nc.gpsimd.tensor_copy(normed[:, bass.ds(t, 1), :], out_s[:, j:j + 1, :]).then_inc(rows_kept, 1)

            if normed is not None:
                run_slots(pool, NT, U, [(0, keep)])

        @block.sync
        def _(sp):
            def store(t, j):
                sp.wait_ge(rows_done, t + 1)
                sp.dma_start(table[at(t), :], out_s[:, j, :]).then_inc(rows_stored[j], 16)

            if table is not None:
                run_slots(sp, NT, U, [(0, store)])
                for j in range(U):
                    sp.wait_ge(rows_stored[j], 16 * (NT // U))


def turn_rows(core, name, src, turned, scale=None):
    nc = core.nc
    with ExitStack() as c:
        def sem(n):
            return c.enter_context(nc.semaphore(f"{name}_{n}"))

        out_s = c.enter_context(nc.sbuf_tensor(f"{name}_out_s", [TP, U, D], F32))
        pt = c.enter_context(nc.psum_tensor(f"{name}_pt", [128, U, 512], F32))
        rows_done, rows_turned, turned_moved = sem("rows_done"), sem("rows_turned"), sem("turned_moved")
        block = c.enter_context(nc.Block())

        @block.vector
        def _(dve):
            def stage(t, j):
                reuse(dve, rows_turned, t, j, U)
                factor = 1.0 if scale is None else scale[:, bass.ds(t, 1)]
                nc.vector.tensor_scalar(out_s[:, j, :], src[:, bass.ds(t, 1), :], factor, None, ALU.mult).then_inc(rows_done, 1)

            run_slots(dve, NT, U, [(0, stage)])

        @block.tensor
        def _(pe):
            def turn(t, j):
                pe.wait_ge(rows_done, t + 1)
                reuse(pe, turned_moved, t, j, U)
                for h in range(KC):
                    ins = nc.tensor.transpose(pt[:, j, h * TP:(h + 1) * TP], out_s[:, j, h * 128:(h + 1) * 128], core.ident[0:TP, 0:TP])
                ins.then_inc(rows_turned, 1)

            run_slots(pe, NT, U, [(0, turn)])

        @block.scalar
        def _(act):
            def move(t, j):
                act.wait_ge(rows_turned, t + 1)
                nc.scalar.copy(turned[:, :, at(t)], pt[:, j, 0:2 * TP].rearrange("p (h n) -> p h n", h=KC)).then_inc(turned_moved, 1)

            run_slots(act, NT, U, [(0, move)])


def project(core, name, sources, jobs, width, evacuate, loads=(), before=None):
    nc = core.nc
    banks = -(-width // 512)
    with ExitStack() as c:
        def sem(n):
            return c.enter_context(nc.semaphore(f"{name}_{n}"))

        staged = c.enter_context(nc.sbuf_tensor(f"{name}_staged", [128, U, len(sources), KC, TP], F32))
        out = c.enter_context(nc.psum_tensor(f"{name}_out", [128, U if banks == 1 else 3, banks * 512], F32))
        buffers = U if banks == 1 else 3
        weights_landed, sources_staged, products_made, products_taken = sem("weights_landed"), sem("sources_staged"), sem("products_made"), sem("products_taken")
        block = c.enter_context(nc.Block())

        @block.sync
        def _(sp):
            for tile, dram in loads:
                sp.dma_start(tile, dram).then_inc(weights_landed, 16)

        @block.gpsimd
        def _(pool):
            def stage(t, j):
                reuse(pool, products_made, t, j, U)
                for s, source in enumerate(sources):
                    ins = nc.gpsimd.tensor_copy(staged[:, j, s, :, :], source[:, :, at(t)])
                ins.then_inc(sources_staged, 1)

            run_slots(pool, NT, U, [(0, stage)])

        @block.tensor
        def _(pe):
            if loads:
                pe.wait_ge(weights_landed, 16 * len(loads))

            def multiply(t, j):
                pe.wait_ge(sources_staged, t + 1)
                reuse(pe, products_taken, t, j, buffers)
                for s, weight, col, opens, closes in jobs:
                    for h in range(KC):
                        ins = nc.tensor.matmul(out[0:TP, j % buffers, col:col + weight.shape[-1]], staged[:, j, s, h, :],
                                               weight[:, h, :], start=opens and h == 0, stop=closes and h == KC - 1)
                ins.then_inc(products_made, 1)

            run_slots(pe, NT, U, [(0, multiply)])

        @block.vector
        def _(dve):
            if loads:
                dve.wait_ge(weights_landed, 16 * len(loads))
            if before is not None:
                before(dve)
                dve.drain()

            def take(t, j):
                dve.wait_ge(products_made, t + 1)
                evacuate(dve, t, j, out[0:TP, j % buffers, 0:width])
                dve.drain().then_inc(products_taken, 1)

            run_slots(dve, NT, U, [(0, take)])


def halves(matrix):
    return matrix.rearrange("(h p) n -> p h n", p=128)


def spread(row, count=TP):
    return row.partition_broadcast(count)


def gate_top2(core, name, scores, experts, gates, of_softmax):
    nc = core.nc
    shape = [TP, NT, experts]
    with ExitStack() as c:
        def sb(n, shape, dt=F32):
            return c.enter_context(nc.sbuf_tensor(f"{name}_{n}", shape, dt))

        def sem(n):
            return c.enter_context(nc.semaphore(f"{name}_{n}"))

        best, second, index = sb("best", [TP, NT]), sb("second", [TP, NT]), sb("index", [TP, NT])
        lower, pick, rest = sb("lower", shape), sb("pick", shape), sb("rest", shape)
        less_max, exped = sem("less_max"), sem("exped")
        block = c.enter_context(nc.Block())
        number = core.col[0:TP, 0:experts].unsqueeze(1).broadcast_to(shape)

        @block.scalar
        def _(act):
            act.wait_ge(less_max, 1)
            target = scores if of_softmax else second
            nc.scalar.activation(target[:], target[:], ACT.Exp).then_inc(exped, 1)

        @block.vector
        def _(dve):
            v = nc.vector

            def first_max(values, best):
                v.tensor_reduce(best[:], values[:], AX_X, ALU.max)
                dve.drain()
                v.tensor_tensor(lower[:], values[:], best[:].unsqueeze(2).broadcast_to(shape), ALU.is_lt)
                dve.drain()
                v.scalar_tensor_tensor(lower[:], lower[:], 64.0, number, ALU.mult, ALU.add)
                dve.drain()
                v.tensor_reduce(index[:], lower[:], AX_X, ALU.min)
                dve.drain()
                v.tensor_tensor(pick[:], number, index[:].unsqueeze(2).broadcast_to(shape), ALU.is_equal)
                dve.drain()

            if of_softmax:
                v.tensor_reduce(best[:], scores[:], AX_X, ALU.max)
                dve.drain()
                v.tensor_tensor(scores[:], scores[:], best[:].unsqueeze(2).broadcast_to(shape), ALU.subtract)
                dve.drain().then_inc(less_max, 1)
                dve.wait_ge(exped, 1)
                v.tensor_reduce(second[:], scores[:], AX_X, ALU.add)
                dve.drain()
                v.reciprocal(best[:], second[:])
                dve.drain()
                v.tensor_tensor(scores[:], scores[:], best[:].unsqueeze(2).broadcast_to(shape), ALU.mult)
                dve.drain()
            first_max(scores, best)
            v.tensor_copy(gates[:], pick[:])
            v.scalar_tensor_tensor(rest[:], pick[:], -FAR, scores[:], ALU.mult, ALU.add)
            dve.drain()
            first_max(rest, second)
            if of_softmax:
                v.tensor_tensor(index[:], best[:], second[:], ALU.add)
                dve.drain()
                v.tensor_scalar(index[:], index[:], 1e-12, None, ALU.max)
            else:
                v.tensor_tensor(second[:], second[:], best[:], ALU.subtract)
                dve.drain()
                v.memset(best[:], 1.0)
                dve.drain().then_inc(less_max, 1)
                dve.wait_ge(exped, 1)
                v.tensor_tensor(index[:], best[:], second[:], ALU.add)
            dve.drain()
            v.reciprocal(index[:], index[:])
            dve.drain()
            v.tensor_tensor(best[:], best[:], index[:], ALU.mult)
            v.tensor_tensor(second[:], second[:], index[:], ALU.mult)
            dve.drain()
            v.tensor_tensor(gates[:], gates[:], best[:].unsqueeze(2).broadcast_to(shape), ALU.mult)
            v.tensor_tensor(pick[:], pick[:], second[:].unsqueeze(2).broadcast_to(shape), ALU.mult)
            dve.drain()
            v.tensor_tensor(gates[:], gates[:], pick[:], ALU.add)


def pick_expert(core, name, scores, experts, chosen):
    nc = core.nc
    shape = [TP, NT, experts]
    with ExitStack() as c:
        def sb(n, shape, dt=F32):
            return c.enter_context(nc.sbuf_tensor(f"{name}_{n}", shape, dt))

        def sem(n):
            return c.enter_context(nc.semaphore(f"{name}_{n}"))

        best, index = sb("best", [TP, NT]), sb("index", [TP, NT])
        lower, pick_s = sb("lower", shape), sb("pick_s", [TP, U, experts])
        pt = c.enter_context(nc.psum_tensor(f"{name}_pt", [experts, U, 512], F32))
        picked, turned, moved = sem("picked"), sem("turned"), sem("moved")
        block = c.enter_context(nc.Block())
        number = core.col[0:TP, 0:experts].unsqueeze(1).broadcast_to(shape)

        @block.vector
        def _(dve):
            v = nc.vector
            v.tensor_reduce(best[:], scores[:], AX_X, ALU.max)
            dve.drain()
            v.tensor_tensor(lower[:], scores[:], best[:].unsqueeze(2).broadcast_to(shape), ALU.is_lt)
            dve.drain()
            v.scalar_tensor_tensor(lower[:], lower[:], 64.0, number, ALU.mult, ALU.add)
            dve.drain()
            v.tensor_reduce(index[:], lower[:], AX_X, ALU.min)
            dve.drain()

            def pick(t, j):
                reuse(dve, turned, t, j, U)
                v.tensor_scalar(pick_s[:, j, :], core.col[0:TP, 0:experts], index[:, bass.ds(t, 1)], None,
                                ALU.is_equal).then_inc(picked, 1)

            run_slots(dve, NT, U, [(0, pick)])

        @block.tensor
        def _(pe):
            def turn(t, j):
                pe.wait_ge(picked, t + 1)
                reuse(pe, moved, t, j, U)
                nc.tensor.transpose(pt[:, j, 0:TP], pick_s[:, j, :], core.ident[0:TP, 0:TP]).then_inc(turned, 1)

            run_slots(pe, NT, U, [(0, turn)])

        @block.scalar
        def _(act):
            def move(t, j):
                act.wait_ge(turned, t + 1)
                nc.scalar.copy(chosen[:, at(t)], pt[:, j, 0:TP]).then_inc(moved, 1)

            run_slots(act, NT, U, [(0, move)])


def feed_forward(core, name, x_t, units, chunks, load_weights, b1, function, w1, w2, take, gates=None, b2=None,
                 chosen=None, loads=()):
    nc = core.nc
    HID = chunks * 128
    with ExitStack() as c:
        def sb(n, shape, dt=F32):
            return c.enter_context(nc.sbuf_tensor(f"{name}_{n}", shape, dt))

        def sem(n):
            return c.enter_context(nc.semaphore(f"{name}_{n}"))

        hidden_s = sb("hidden_s", [128, 2, chunks, TP])
        hidden_p = c.enter_context(nc.psum_tensor(f"{name}_hidden_p", [128, 2, 512], F32))
        out_p = c.enter_context(nc.psum_tensor(f"{name}_out_p", [128, 2, 512], F32))
        if chosen is not None:
            experts = chosen.shape[0]
            expert_i = sb("expert_i", [experts, units * HID], I32)
            push = sb("push", [experts, units * HID])
            less_one = sb("less_one", [experts, N])
            chosen_s = sb("chosen_s", [experts, TP])
        numbers_made, push_made, chosen_staged = sem("numbers_made"), sem("push_made"), sem("chosen_staged")
        weights_landed = [sem(f"weights_landed{e}") for e in range(units)]
        extras_landed = sem("extras_landed")
        hidden_made, hidden_done, out_made, out_taken = sem("hidden_made"), sem("hidden_done"), sem("out_made"), sem("out_taken")
        block = c.enter_context(nc.Block())

        @block.sync
        def _(sp):
            for tile, dram in loads:
                sp.dma_start(tile, dram).then_inc(extras_landed, 16)
            for e in range(units):
                for tile, dram in load_weights(e):
                    sp.dma_start(tile, dram).then_inc(weights_landed[e], 16)

        if chosen is not None:
            @block.gpsimd
            def _(pool):
                nc.gpsimd.iota(expert_i[:], [[1, experts], [0, units * HID // experts]], base=0,
                               channel_multiplier=0).then_inc(numbers_made, 1)

        @block.tensor
        def _(pe):
            if loads:
                pe.wait_ge(extras_landed, 16 * len(loads))
            if chosen is not None:
                pe.wait_ge(push_made, 1)

            def hidden(t, e):
                n = t * units + e
                if isinstance(t, int) and t == 0:
                    pe.wait_ge(weights_landed[e], 16 * len(load_weights(e)))
                if not (isinstance(n, int) and n < 2):
                    pe.wait_ge(hidden_done, n - 1)
                for i in range(chunks):
                    col = (e * chunks + i) * 128
                    out = hidden_p[:, e % 2, i * TP:(i + 1) * TP]
                    for h in range(KC):
                        ins = nc.tensor.matmul(out, w1[:, h, col:col + 128], x_t[:, h, at(t)],
                                               start=h == 0, stop=h == KC - 1 and chosen is None)
                    if chosen is not None:
                        ins = nc.tensor.matmul(out, push[:, col:col + 128], less_one[:, at(t)], start=False, stop=True)
                ins.then_inc(hidden_made, 1)

            def output(t, e):
                n = t * units + e
                pe.wait_ge(hidden_done, n + 1)
                if gates is not None:
                    if not (isinstance(n, int) and n < 2):
                        pe.wait_ge(out_taken, n - 1)
                    out = out_p[0:TP, e % 2, 0:D]
                    opens, closes = True, True
                else:
                    if e == 0 and not (isinstance(t, int) and t == 0):
                        pe.wait_ge(out_taken, t)
                    out = out_p[0:TP, 0, 0:D]
                    opens, closes = e == 0, e == units - 1
                    if e == 0 and chosen is not None:
                        pe.wait_ge(chosen_staged, t + 1)
                        nc.tensor.matmul(out, chosen_s[:], b2[:], start=True, stop=False)
                        opens = False
                for i in range(chunks):
                    ins = nc.tensor.matmul(out, hidden_s[:, e % 2, i, :], w2[:, e * chunks + i, :],
                                           start=opens and i == 0, stop=closes and i == chunks - 1)
                ins.then_inc(out_made, 1)

            def tile(t):
                for e in range(units):
                    hidden(t, e)
                    if e:
                        output(t, e - 1)
                    elif not (isinstance(t, int) and t == 0):
                        output(t - 1, units - 1)

            tile(0)
            with pe.Fori(1, NT) as t:
                tile(t)
            output(NT - 1, units - 1)

        @block.scalar
        def _(act):
            if loads:
                act.wait_ge(extras_landed, 16 * len(loads))

            def tile(t):
                if chosen is not None:
                    if not (isinstance(t, int) and t == 0):
                        act.wait_ge(out_made, (t - 1) * units + 1)
                    nc.scalar.copy(chosen_s[:], chosen[:, at(t)]).then_inc(chosen_staged, 1)
                for e in range(units):
                    n = t * units + e
                    act.wait_ge(hidden_made, n + 1)
                    if not (isinstance(n, int) and n < 2):
                        act.wait_ge(out_made, n - 1)
                    for i in range(chunks):
                        ins = nc.scalar.activation(hidden_s[:, e % 2, i, :], hidden_p[:, e % 2, i * TP:(i + 1) * TP],
                                                   function, bias=b1[:, e * chunks + i:e * chunks + i + 1])
                    ins.then_inc(hidden_done, 1)

            tile(0)
            with act.Fori(1, NT) as t:
                tile(t)

        @block.vector
        def _(dve):
            v = nc.vector
            if chosen is not None:
                dve.wait_ge(numbers_made, 1)
                v.tensor_scalar(push[:], expert_i[:], core.row[0:experts, 0:1], FAR, ALU.is_equal, ALU.mult)
                v.tensor_scalar(less_one[:], chosen[:], -1.0, None, ALU.add)
                dve.drain().then_inc(push_made, 1)
            if loads:
                dve.wait_ge(extras_landed, 16 * len(loads))

            def tile(t):
                mine = core.x[:, bass.ds(t, 1), :]
                if gates is None:
                    dve.wait_ge(out_made, t * units + units)
                    take(dve, t, out_p[0:TP, 0, 0:D])
                    dve.drain().then_inc(out_taken, 1)
                    return
                for e in range(units):
                    gate = gates[:, bass.ds(t, 1), e]
                    v.scalar_tensor_tensor(mine, b2[:, e:e + 1, :], gate, mine, ALU.mult, ALU.add)
                    dve.drain()
                    dve.wait_ge(out_made, t * units + e + 1)
                    v.scalar_tensor_tensor(mine, out_p[0:TP, e % 2, 0:D].unsqueeze(1), gate, mine, ALU.mult, ALU.add)
                    dve.drain().then_inc(out_taken, 1)

            tile(0)
            with dve.Fori(1, NT) as t:
                tile(t)


def attention(core, name, x_t, wq, wkv, wo, bq, bkv, bo, loads, feature, norm):
    nc = core.nc
    G = 128 + 4
    with ExitStack() as c:
        mixing = c.enter_context(nc.sbuf_tensor(f"{name}_mixing", [128, KC, G], F32))
        with ExitStack() as c:
            def sb(n, shape, dt=F32):
                return c.enter_context(nc.sbuf_tensor(f"{name}_{n}", shape, dt))

            def sem(n):
                return c.enter_context(nc.semaphore(f"{name}_{n}"))

            staged = sb("staged", [128, U, KC, TP])
            kv_s = sb("kv_s", [TP, U, 2 * D + 1])
            below_s = sb("below_s", [TP, U, D])
            exp_s = sb("exp_s", [TP, U, D])
            kv_p = c.enter_context(nc.psum_tensor(f"{name}_kv_p", [128, U, 512], F32))
            total_p = c.enter_context(nc.psum_tensor(f"{name}_total_p", [128, KC, 512], F32))
            landed, sources_staged, kv_made, kv_taken = sem("landed"), sem("staged"), sem("kv_made"), sem("kv_taken")
            below_made, exp_made, keys_done, keys_used, all_added = sem("below_made"), sem("exp_made"), sem("keys_done"), sem("keys_used"), sem("all_added")
            block = c.enter_context(nc.Block())

            @block.sync
            def _(sp):
                for tile, dram in loads:
                    sp.dma_start(tile, dram).then_inc(landed, 16)

            @block.gpsimd
            def _(pool):
                def stage(t, j):
                    reuse(pool, kv_made, t, j, U)
                    nc.gpsimd.tensor_copy(staged[:, j, :, :], x_t[:, :, at(t)]).then_inc(sources_staged, 1)

                run_slots(pool, NT, U, [(0, stage)])

            @block.tensor
            def _(pe):
                pe.wait_ge(landed, 16 * len(loads))
                for h in range(KC):
                    nc.tensor.matmul(total_p[:, h, 0:D + 1], core.zeros[:], core.wide_zeros[:, 0:D + 1], start=True, stop=False,
                                     skip_group_check=True)

                def products(t, j):
                    pe.wait_ge(sources_staged, t + 1)
                    reuse(pe, kv_taken, t, j, U)
                    for h in range(KC):
                        ins = nc.tensor.matmul(kv_p[0:TP, j, :], staged[:, j, h, :], wkv[:, h, :], start=h == 0, stop=h == KC - 1)
                    ins.then_inc(kv_made, 1)

                def totals(t, j):
                    pe.wait_ge(keys_done, t + 1)
                    for h in range(KC):
                        ins = nc.tensor.matmul(total_p[:, h, 0:D + 1], kv_s[:, j, h * 128:(h + 1) * 128], kv_s[:, j, D:2 * D + 1],
                                               start=False, stop=False, skip_group_check=True)
                    ins.then_inc(keys_used, 1)

                run_slots(pe, NT, U, [(0, products), (2, totals)])

            @block.scalar
            def _(act):
                def exp(t, j):
                    act.wait_ge(below_made, t + 1)
                    nc.scalar.activation(exp_s[:, j, :], below_s[:, j, :], ACT.Exp).then_inc(exp_made, 1)

                if feature:
                    run_slots(act, NT, U, [(0, exp)])

            @block.vector
            def _(dve):
                v = nc.vector
                v.memset(kv_s[:, :, 2 * D:2 * D + 1], 1.0)
                dve.wait_ge(landed, 16 * len(loads))

                def take(t, j):
                    dve.wait_ge(kv_made, t + 1)
                    reuse(dve, keys_used, t, j, U)
                    if bkv is None:
                        v.tensor_copy(kv_s[:, j, 0:2 * D], kv_p[0:TP, j, :])
                    else:
                        v.tensor_tensor(kv_s[:, j, 0:2 * D], kv_p[0:TP, j, :], bkv[:], ALU.add)
                    dve.drain().then_inc(kv_taken, 1)
                    if feature:
                        v.tensor_scalar(below_s[:, j, :], kv_s[:, j, 0:D], 0.0, None, ALU.min)
                        dve.drain().then_inc(below_made, 1)
                    else:
                        dve.sem_inc(keys_done, 1)

                def join(t, j):
                    dve.wait_ge(exp_made, t + 1)
                    v.scalar_tensor_tensor(kv_s[:, j, 0:D], kv_s[:, j, 0:D], 0.0, exp_s[:, j, :], ALU.max, ALU.add)
                    dve.drain().then_inc(keys_done, 1)

                run_slots(dve, NT, U, [(0, take)] + ([(1, join)] if feature else []))
                dve.wait_ge(keys_used, NT)
                scale = 1.0 / N if norm == "length" else 1.0
                for h in range(KC):
                    v.scalar_tensor_tensor(mixing[:, h, 0:128], total_p[:, h, h * 128:(h + 1) * 128], scale, core.same_head[:],
                                           ALU.mult, ALU.mult)
                    v.tensor_scalar(mixing[:, h, 128:G], core.head_of[:], total_p[:, h, D:D + 1], None, ALU.mult)

        with ExitStack() as c:
            staged_q = c.enter_context(nc.sbuf_tensor(f"{name}_queries", [128, U, KC, TP], F32))
            low = c.enter_context(nc.sbuf_tensor(f"{name}_low", [128, U, KC, TP], F32))
            high = c.enter_context(nc.sbuf_tensor(f"{name}_high", [128, U, KC, TP], F32))
            share = c.enter_context(nc.sbuf_tensor(f"{name}_share", [TP, U, 8], F32))
            mixed = c.enter_context(nc.sbuf_tensor(f"{name}_mixed", [TP, U, D], F32))
            mixed_t = c.enter_context(nc.sbuf_tensor(f"{name}_mixed_t", [128, U, KC, TP], F32))
            q_p = c.enter_context(nc.psum_tensor(f"{name}_q_p", [128, 2, 512], F32))
            mixed_p = c.enter_context(nc.psum_tensor(f"{name}_mixed_p", [128, 2, 512], F32))
            turned_p = c.enter_context(nc.psum_tensor(f"{name}_turned_p", [128, 2, 512], F32))
            out_p = c.enter_context(nc.psum_tensor(f"{name}_out_p", [128, 2, 512], F32))

            def sem(n):
                return c.enter_context(nc.semaphore(f"{name}_{n}"))

            q_made, q_split, high_made, exp_made, queries_done = sem("q_made"), sem("q_split"), sem("high_made"), sem("q_exp_made"), sem("queries_done")
            mixed_made, mixed_done, turned_made, turned_moved, out_made, out_added = (
                sem("mixed_made"), sem("mixed_done"), sem("turned_made"), sem("turned_moved"), sem("out_made"), sem("out_added"))
            block = c.enter_context(nc.Block())

            @block.tensor
            def _(pe):
                def queries(t, j):
                    reuse(pe, high_made if feature else queries_done, t, j, 2)
                    for o in range(KC):
                        for h in range(KC):
                            ins = nc.tensor.matmul(q_p[:, j % 2, o * TP:(o + 1) * TP], wq[:, h, o * 128:(o + 1) * 128],
                                                   x_t[:, h, at(t)], start=h == 0, stop=h == KC - 1)
                    ins.then_inc(q_made, 1)

                def mix(t, j):
                    pe.wait_ge(queries_done, t + 1)
                    reuse(pe, mixed_done, t, j, 2)
                    for h in range(KC):
                        ins = nc.tensor.matmul(mixed_p[0:TP, j % 2, h * G:(h + 1) * G], staged_q[:, j, h, :], mixing[:, h, :],
                                               start=True, stop=True)
                    ins.then_inc(mixed_made, 1)

                def turn(t, j):
                    pe.wait_ge(mixed_done, t + 1)
                    reuse(pe, turned_moved, t, j, 2)
                    for h in range(KC):
                        ins = nc.tensor.transpose(turned_p[:, j % 2, h * TP:(h + 1) * TP], mixed[:, j, h * 128:(h + 1) * 128],
                                                  core.ident[0:TP, 0:TP])
                    ins.then_inc(turned_made, 1)

                def output(t, j):
                    pe.wait_ge(turned_moved, t + 1)
                    reuse(pe, out_added, t, j, 2)
                    for h in range(KC):
                        ins = nc.tensor.matmul(out_p[0:TP, j % 2, 0:D], mixed_t[:, j, h, :], wo[:, h, :], start=h == 0, stop=h == KC - 1)
                    ins.then_inc(out_made, 1)

                run_slots(pe, NT, U, [(0, queries), (1, mix), (2, turn), (3, output)])

            def half(tile, j, h):
                return tile[:, j % 2, h * TP:(h + 1) * TP]

            @block.scalar
            def _(act):
                def split(t, j):
                    act.wait_ge(q_made, t + 1)
                    target = high if feature else staged_q
                    reuse(act, queries_done if feature else mixed_made, t, j, U)
                    for h in range(KC):
                        if bq is None:
                            ins = nc.scalar.copy(target[:, j, h, :], half(q_p, j, h))
                        else:
                            ins = nc.scalar.activation(target[:, j, h, :], half(q_p, j, h), ACT.Identity, bias=bq[:, h:h + 1])
                    ins.then_inc(high_made if feature else queries_done, 1)
                    if feature:
                        act.wait_ge(q_split, t + 1)
                        nc.scalar.activation(low[:, j, :, :], low[:, j, :, :], ACT.Exp).then_inc(exp_made, 1)

                def move(t, j):
                    act.wait_ge(turned_made, t + 1)
                    reuse(act, out_made, t, j, U)
                    nc.scalar.copy(mixed_t[:, j, :, :], turned_p[:, j % 2, 0:2 * TP].rearrange("p (h n) -> p h n", h=KC)
                                   ).then_inc(turned_moved, 1)

                run_slots(act, NT, U, [(0, split), (2, move)])

            @block.vector
            def _(dve):
                v = nc.vector
                if bo is not None:
                    v.tensor_tensor(core.x[:], core.x[:], bo[:].unsqueeze(1).broadcast_to([TP, NT, D]), ALU.add)
                    dve.drain()

                def below(t, j):
                    dve.wait_ge(high_made, t + 1)
                    v.tensor_scalar(low[:, j, :, :], high[:, j, :, :], 0.0, None, ALU.min)
                    dve.drain().then_inc(q_split, 1)

                def join(t, j):
                    dve.wait_ge(exp_made, t + 1)
                    reuse(dve, mixed_made, t, j, U)
                    v.scalar_tensor_tensor(staged_q[:, j, :, :], high[:, j, :, :], 0.0, low[:, j, :, :], ALU.max, ALU.add)
                    dve.drain().then_inc(queries_done, 1)

                def share_out(t, j):
                    dve.wait_ge(mixed_made, t + 1)
                    reuse(dve, turned_made, t, j, U)
                    sums = mixed_p[0:TP, j % 2, 0:2 * G].rearrange("p (h g) -> p h g", h=KC)
                    if norm == "length":
                        v.tensor_copy(mixed[:, j, :].rearrange("p (h g) -> p h g", h=KC), sums[:, :, 0:128])
                    else:
                        how = ALU.add if norm == "add" else ALU.max
                        v.tensor_scalar(share[:, j, :].rearrange("p (h g) -> p h g", h=KC), sums[:, :, 128:G], 1e-6, None, how)
                        dve.drain()
                        v.reciprocal(share[:, j, :], share[:, j, :])
                        dve.drain()
                        for h in range(KC):
                            v.tensor_tensor(mixed[:, j, h * 128:(h + 1) * 128].rearrange("p (g d) -> p g d", g=4),
                                            sums[:, h, 0:128].rearrange("p (g d) -> p g d", g=4),
                                            share[:, j, 4 * h:4 * h + 4].unsqueeze(2).broadcast_to([TP, 4, 32]), ALU.mult)
                    dve.drain().then_inc(mixed_done, 1)

                def add(t, j):
                    dve.wait_ge(out_made, t + 1)
                    mine = core.x[:, bass.ds(t, 1), :]
                    v.tensor_tensor(mine, mine, out_p[0:TP, j % 2, 0:D].unsqueeze(1), ALU.add)
                    dve.drain().then_inc(out_added, 1)

                run_slots(dve, NT, U, ([(0, below), (1, join)] if feature else []) + [(1, share_out), (3, add)])


def blend(core, name, low, high, mlp, attend, attend_mix, loads):
    nc = core.nc
    with ExitStack() as c:
        def sb(n, shape, dt=F32):
            return c.enter_context(nc.sbuf_tensor(f"{name}_{n}", shape, dt))

        def sem(n):
            return c.enter_context(nc.semaphore(f"{name}_{n}"))

        product = sb("product", [TP, NT, D])
        logit, mix, term = sb("logit", [TP, NT, 3]), sb("mix", [TP, NT, 3]), sb("term", [TP, NT, 3])
        best = sb("best", [TP, NT])
        landed, logits_made, sigmoid_made, shifted, exp_made = sem("landed"), sem("logits_made"), sem("sigmoid_made"), sem("shifted"), sem("exp_made")
        block = c.enter_context(nc.Block())

        @block.sync
        def _(sp):
            for tile, dram in loads:
                sp.dma_start(tile, dram).then_inc(landed, 16)

        @block.scalar
        def _(act):
            act.wait_ge(logits_made, 1)
            nc.scalar.activation(logit[:], logit[:], ACT.Sigmoid).then_inc(sigmoid_made, 1)
            act.wait_ge(shifted, 1)
            nc.scalar.activation(mix[:], mix[:], ACT.Exp).then_inc(exp_made, 1)

        @block.vector
        def _(dve):
            v = nc.vector
            dve.wait_ge(landed, 16 * len(loads))
            for k, branch in enumerate((low, high, mlp)):
                v.tensor_tensor(product[:], branch, attend[:, k:k + 1, :].broadcast_to([TP, NT, D]), ALU.mult)
                dve.drain()
                v.tensor_reduce(logit[:, :, k], product[:], AX_X, ALU.add)
                dve.drain()
            v.memset(mix[:], 0.0)
            dve.drain().then_inc(logits_made, 1)
            dve.wait_ge(sigmoid_made, 1)
            shape = [TP, NT, 3]
            for k in range(3):
                v.tensor_tensor(term[:], logit[:, :, k:k + 1].broadcast_to(shape),
                                attend_mix[:, 3 * k:3 * k + 3].unsqueeze(1).broadcast_to(shape), ALU.mult)
                dve.drain()
                v.tensor_tensor(mix[:], mix[:], term[:], ALU.add)
                dve.drain()
            v.tensor_scalar(mix[:], mix[:], 1.0 / 3.0, None, ALU.mult)
            dve.drain()
            v.tensor_reduce(best[:], mix[:], AX_X, ALU.max)
            dve.drain()
            v.tensor_tensor(mix[:], mix[:], best[:].unsqueeze(2).broadcast_to(shape), ALU.subtract)
            dve.drain().then_inc(shifted, 1)
            dve.wait_ge(exp_made, 1)
            v.tensor_reduce(best[:], mix[:], AX_X, ALU.add)
            dve.drain()
            v.reciprocal(best[:], best[:])
            dve.drain()
            v.tensor_scalar(best[:], best[:], 3.0, None, ALU.mult)
            dve.drain()
            v.tensor_tensor(mix[:], mix[:], best[:].unsqueeze(2).broadcast_to(shape), ALU.mult)
            dve.drain()
            for k, branch in enumerate((low, high, mlp)):
                with dve.Fori(0, NT) as t:
                    mine = core.x[:, bass.ds(t, 1), :]
                    v.scalar_tensor_tensor(mine, branch[:, bass.ds(t, 1), :], mix[:, bass.ds(t, 1), k], mine, ALU.mult, ALU.add)
                dve.drain()


def max_edges(core, name, table, records, edge_group, best):
    nc = core.nc
    K, NB = 4, 4
    Q = ET_MAIN // K
    FLAG = float(2.0 ** 100)
    with ExitStack() as c:
        def sb(n, shape, dt=F32):
            return c.enter_context(nc.sbuf_tensor(f"{name}_{n}", shape, dt))

        def psum(n, shape):
            return c.enter_context(nc.psum_tensor(f"{name}_{n}", shape, F32))

        def sem(n):
            return c.enter_context(nc.semaphore(f"{name}_{n}"))

        index = sb("index", [128, NB, K], I32)
        rows = sb("rows", [128, NB, K, D])
        own = sb("own", [128, ET_MAIN + ET_PAD])
        flag = sb("flag", [128, ET_MAIN + ET_PAD])
        diag = sb("diag", [128, K, 128])
        lower = sb("lower", [128, K, 128])
        rank = sb("rank", [128, K])
        perm = sb("perm", [128, 2, K, 129])
        perm_flag = sb("perm_flag", [128, K, 128])
        flags = sb("flags", [128, K, 128])
        break_s = sb("break_s", [128, K, 128])
        node = sb("node", [128, K, 2])
        last_of = sb("last_of", [128, K])
        pick = sb("pick", [128, 2, K, TP])
        scanned = sb("scanned", [128, 2, KC, K * 128])
        back_s = sb("back_s", [128, 2, K, D])
        absent = sb("absent", [TP, K])
        own_p = psum("own_p", [128, 512])
        flag_p = psum("flag_p", [128, 512])
        turned_p = psum("turned_p", [128, KC, 512])
        node_p = psum("node_p", [128, 512])
        out_p = psum("out_p", [128, K, D])
        indexed, batch_begun = sem("indexed"), sem("batch_begun")
        gathered = [core.software_dma_semaphore(f"{name}_gathered{b}") for b in range(NB)]
        diag_made, own_made, ordered, flagged, sorted_, flags_moved, scanned_done, back_made, back_moved, out_made, taken, keys_made = (
            sem(n) for n in ("diag_made", "own_made", "ordered", "flagged", "sorted", "flags_moved", "scanned_done", "back_made",
                             "back_moved", "out_made", "taken", "keys_made"))
        block = c.enter_context(nc.Block())

        @block.gpsimd
        def _(pool):
            def gather(q, j):
                pool.wait_ge(indexed, q + 1)
                pool.sem_inc(batch_begun, 1)
                if not (isinstance(q, int) and q < NB):
                    pool.wait_ge(sorted_, q - (NB - 1))
                    pool.sem_inc(batch_begun, 1)
                for k in range(K):
                    nc.gpsimd.indirect_dma_start(
                        out=rows[:, j, k, :], out_offset=None, in_=table,
                        in_offset=bass.IndirectOffsetOnAxis(ap=index[:, j, k:k + 1].bitcast(U32), axis=0),
                    ).then_inc(gathered[j], 16)

            run_slots(pool, Q, NB, [(0, gather)])

        @block.scalar
        def _(act):
            act.wait_ge(keys_made, 1)

            def make_diag(q, j):
                reuse(act, own_made, q, j, 1, NB)
                for k in range(K):
                    ins = nc.scalar.activation(diag[:, k, :], core.ident[:], ACT.Copy, scale=own[:, bass.ds(q * K + k, 1)])
                ins.then_inc(diag_made, 1)

            def move_back(q, j):
                act.wait_ge(back_made, q + 1)
                reuse(act, out_made, q, j, 2, NB)
                nc.scalar.copy(back_s[:, j % 2, :, :], turned_p[:].rearrange("p h (k d) -> p (h k) d", d=D)).then_inc(back_moved, 1)

            def make_flag(q, j):
                act.wait_ge(ordered, q + 1)
                reuse(act, sorted_, q, j, 1, NB)
                for k in range(K):
                    ins = nc.scalar.activation(perm_flag[:, k, :], perm[:, j % 2, k, 0:128], ACT.Copy, scale=flag[:, bass.ds(q * K + k, 1)])
                ins.then_inc(flagged, 1)

            def move_flags(q, j):
                act.wait_ge(sorted_, q + 1)
                reuse(act, scanned_done, q, j, 1, NB)
                nc.scalar.copy(flags[:].rearrange("p k e -> p (k e)"), flag_p[:]).then_inc(flags_moved, 1)

            run_slots(act, Q, NB, [(0, make_diag), (3, move_back), (1, make_flag), (2, move_flags)])

        @block.tensor
        def _(pe):
            def spread_own(q, j):
                pe.wait_ge(diag_made, q + 1)
                reuse(pe, ordered, q, j, 1, NB)
                nc.tensor.matmul(own_p[:], core.ones[:], diag[:].rearrange("p k e -> p (k e)"), start=True, stop=True).then_inc(own_made, 1)

            def turn_back(q, j):
                pe.wait_ge(scanned_done, q + 1)
                for k in range(K):
                    for h in range(KC):
                        ins = nc.tensor.transpose(turned_p[:, k // 2, (k % 2) * D + h * 128:(k % 2) * D + (h + 1) * 128],
                                                  scanned[:, j % 2, h, k * 128:(k + 1) * 128], core.ident[:])
                ins.then_inc(back_made, 1)

            def choose(q, j):
                pe.wait_ge(back_moved, q + 1)
                reuse(pe, taken, q, j, 1, NB)
                for k in range(K):
                    nc.tensor.matmul(out_p[0:TP, k, :], pick[:, j % 2, k, :], back_s[:, j % 2, k, :], start=True, stop=True)
                for k in range(K):
                    ins = nc.tensor.matmul(node_p[0:TP, 256 + k:257 + k], pick[:, j % 2, k, :], core.ones[:, 0:1], start=True, stop=True)
                ins.then_inc(out_made, 1)

            def sort(q, j):
                pe.wait_ge(flagged, q + 1)
                pe.wait_ge(gathered[j], (q - j) * (16 * K // NB) + 16 * K)
                reuse(pe, back_moved, q, j, 1, NB)
                reuse(pe, taken, q, j, 1, NB)
                for h in range(KC):
                    for k in range(K):
                        nc.tensor.matmul(turned_p[:, h, k * 128:(k + 1) * 128], rows[:, j, k, h * 128:(h + 1) * 128],
                                         perm[:, j % 2, k, 0:128], start=True, stop=True)
                nc.tensor.matmul(flag_p[:], core.ones[:], perm_flag[:].rearrange("p k e -> p (k e)"), start=True, stop=True)
                for k in range(K):
                    for later in range(2):
                        ins = nc.tensor.matmul(node_p[:, 2 * k + later:2 * k + later + 1], perm[:, j % 2, k, later:later + 128],
                                               records[:, bass.ds(q * K + k, 1), 1], start=True, stop=True)
                ins.then_inc(sorted_, 1)

            run_slots(pe, Q, NB, [(0, spread_own), (3, turn_back), (3, choose), (2, sort)])

        @block.vector
        def _(dve):
            v = nc.vector
            v.memset(best[:], -FAR)
            v.memset(perm[:, :, :, 128:129], 0.0)
            v.memset(break_s[:, :, 0:1], -FAR)
            v.tensor_scalar(own[:], records[:, :, 1], 128.0, core.row[:, 0:1], ALU.mult, ALU.add)
            v.tensor_scalar(flag[:], records[:, :, 1], FLAG, None, ALU.mult)
            dve.drain().then_inc(keys_made, 1)

            def number(q, j):
                if not (isinstance(q, int) and q < NB):
                    dve.wait_ge(gathered[j], (q - j) * (16 * K // NB))
                v.tensor_copy(index[:, j, :], records[:, bass.ds(q * K, K), 0])
                dve.drain().then_inc(indexed, 1)

            def take(q, j):
                _, groups = nc.values_load_multi_w_load_instructions(
                    edge_group[0:1, bass.ds(q * K, K)], [mybir.EngineType.DVE], min_val=0, max_val=NT - 1)
                dve.wait_ge(out_made, q + 1)
                v.tensor_scalar(absent[:], node_p[0:TP, 256:256 + K], -1.0, 4.0 * FAR, ALU.add, ALU.mult)
                dve.drain()
                for k in range(K):
                    mine = best[:, bass.ds(groups[k], 1), :]
                    v.scalar_tensor_tensor(mine, out_p[0:TP, k, :].unsqueeze(1), absent[:, k:k + 1], mine, ALU.add, ALU.max)
                    last = dve.drain()
                last.then_inc(taken, 1)

            def order(q, j):
                dve.wait_ge(own_made, q + 1)
                reuse(dve, sorted_, q, j, 2, NB)
                v.tensor_tensor(lower[:], own_p[:].rearrange("p (k e) -> p k e", k=K),
                                own[:, bass.ds(q * K, K)].unsqueeze(2).broadcast_to([128, K, 128]), ALU.is_lt)
                dve.drain()
                v.tensor_reduce(rank[:], lower[:], AX_X, ALU.add)
                dve.drain()
                v.tensor_tensor(perm[:, j % 2, :, 0:128], core.col[:].unsqueeze(1).broadcast_to([128, K, 128]),
                                rank[:].unsqueeze(2).broadcast_to([128, K, 128]), ALU.is_equal)
                dve.drain().then_inc(ordered, 1)

            def scan(q, j):
                dve.wait_ge(flags_moved, q + 1)
                reuse(dve, out_made, q, j, 2, NB)
                v.tensor_tensor(break_s[:, :, 1:128], flags[:, :, 0:127], flags[:, :, 1:128], ALU.subtract)
                v.tensor_copy(node[:].rearrange("p k l -> p (k l)"), node_p[:, 0:2 * K])
                dve.drain()
                v.tensor_tensor(last_of[:], node[:, :, 0], node[:, :, 1], ALU.not_equal)
                for h in range(KC):
                    v.tensor_tensor_scan(scanned[:, j % 2, h, :], break_s[:].rearrange("p k e -> p (k e)"), turned_p[:, h, :],
                                         -FAR, ALU.add, ALU.max)
                dve.drain()
                v.scalar_tensor_tensor(last_of[:], node[:, :, 0], 1.0, last_of[:], ALU.add, ALU.mult)
                dve.drain()
                v.tensor_scalar(last_of[:], last_of[:], -1.0, None, ALU.add)
                dve.drain()
                v.tensor_tensor(pick[:, j % 2, :, :], core.col[:, 0:TP].unsqueeze(1).broadcast_to([128, K, TP]),
                                last_of[:].unsqueeze(2).broadcast_to([128, K, TP]), ALU.is_equal)
                dve.drain().then_inc(scanned_done, 1)

            run_slots(dve, Q, NB, [(0, number), (1, order), (3, take), (2, scan)])


def small_rows(core, name, body, stores=(), loads=(), functions=()):
    nc = core.nc
    with ExitStack() as c:
        landed, asked, answered, done, stored = (c.enter_context(nc.semaphore(f"{name}_{n}"))
                                                 for n in ("landed", "asked", "answered", "done", "stored"))
        block = c.enter_context(nc.Block())

        @block.sync
        def _(sp):
            for tile, dram in loads:
                sp.dma_start(tile, dram).then_inc(landed, 16)
            if stores:
                sp.wait_ge(done, 1)
                for dram, tile in stores:
                    sp.dma_start(dram, tile).then_inc(stored, 16)
                sp.wait_ge(stored, 16 * len(stores))

        @block.scalar
        def _(act):
            for k, function in enumerate(functions):
                act.wait_ge(asked, k + 1)
                function(act).then_inc(answered, 1)

        @block.vector
        def _(dve):
            if loads:
                dve.wait_ge(landed, 16 * len(loads))

            def call(k):
                dve.drain().then_inc(asked, 1)
                dve.wait_ge(answered, k + 1)

            body(dve, call)
            dve.drain().then_inc(done, 1)


def gat_edges(core, name, table, records, edge_group, gathered_rows, best):
    nc = core.nc
    K, NB = 5, 4
    Q = ET_GAT // K
    with ExitStack() as c:
        def sb(n, shape, dt=F32):
            return c.enter_context(nc.sbuf_tensor(f"{name}_{n}", shape, dt))

        def sem(n):
            return c.enter_context(nc.semaphore(f"{name}_{n}"))

        index = sb("index", [128, NB, K], I32)
        rows = sb("rows", [128, NB, K, 20])
        other = sb("other", [128, K, TP])
        score = sb("score", [128, 2, K, 4, TP])
        top = sb("top", [TP, K, 4])
        turned_p = c.enter_context(nc.psum_tensor(f"{name}_turned_p", [128, K, 4, 128], F32))
        indexed, batch_begun, scored, turned, topped = sem("indexed"), sem("batch_begun"), sem("scored"), sem("turned"), sem("topped")
        gathered = [core.software_dma_semaphore(f"{name}_gathered{b}") for b in range(NB)]
        block = c.enter_context(nc.Block())

        @block.gpsimd
        def _(pool):
            def gather(q, j):
                pool.wait_ge(indexed, q + 1)
                pool.sem_inc(batch_begun, 1)
                if not (isinstance(q, int) and q < NB):
                    pool.wait_ge(scored, q - (NB - 1))
                    pool.sem_inc(batch_begun, 1)
                for k in range(K):
                    nc.gpsimd.indirect_dma_start(
                        out=rows[:, j, k, :], out_offset=None, in_=table,
                        in_offset=bass.IndirectOffsetOnAxis(ap=index[:, j, k:k + 1].bitcast(U32), axis=0),
                    ).then_inc(gathered[j], 16)

            run_slots(pool, Q, NB, [(0, gather)])

        @block.tensor
        def _(pe):
            def turn(q, j):
                pe.wait_ge(scored, q + 1)
                reuse(pe, topped, q, j, 1, NB)
                for k in range(K):
                    for a in range(4):
                        ins = nc.tensor.transpose(turned_p[0:TP, k, a, :], score[:, j % 2, k, a, :], core.ident[:])
                ins.then_inc(turned, 1)

            run_slots(pe, Q, NB, [(2, turn)])

        @block.vector
        def _(dve):
            v = nc.vector

            def number(q, j):
                if not (isinstance(q, int) and q < NB):
                    dve.wait_ge(gathered[j], (q - j) // NB * (16 * K))
                v.tensor_copy(index[:, j, :], records[:, bass.ds(q * K, K), 0])
                dve.drain().then_inc(indexed, 1)

            def rate(q, j):
                for k in range(K):
                    v.tensor_scalar(other[:, k, :], core.col[:, 0:TP], records[:, bass.ds(q * K + k, 1), 1], -FAR,
                                    ALU.not_equal, ALU.mult)
                dve.drain()
                dve.wait_ge(gathered[j], (q - j) // NB * (16 * K) + 16 * K)
                reuse(dve, turned, q, j, 2, NB)
                for k in range(K):
                    v.tensor_tensor(score[:, j % 2, k, :, :], other[:, k:k + 1, :].broadcast_to([128, 4, TP]),
                                    rows[:, j, k, 16:20].unsqueeze(2).broadcast_to([128, 4, TP]), ALU.add)
                v.tensor_copy(gathered_rows[:, bass.ds(q * K, K), :], rows[:, j, :, :])
                dve.drain().then_inc(scored, 1)

            def take(q, j):
                _, groups = nc.values_load_multi_w_load_instructions(
                    edge_group[0:1, bass.ds(q * K, K)], [mybir.EngineType.DVE], min_val=0, max_val=NT - 1)
                dve.wait_ge(turned, q + 1)
                v.tensor_reduce(top[:], turned_p[0:TP, :, :, :], AX_X, ALU.max)
                dve.drain()
                for k in range(K):
                    mine = best[:, bass.ds(groups[k], 1), :]
                    v.tensor_tensor(mine, mine, top[:, k:k + 1, :], ALU.max)
                    last = dve.drain()
                last.then_inc(topped, 1)

            run_slots(dve, Q, NB, [(0, number), (2, rate), (3, take)])


def gat_sums(core, name, records, edge_group, gathered_rows, node_scores, sums):
    nc = core.nc
    K, NB = 5, 4
    Q = ET_GAT // K
    with ExitStack() as c:
        def sb(n, shape, dt=F32):
            return c.enter_context(nc.sbuf_tensor(f"{name}_{n}", shape, dt))

        def psum(n, shape):
            return c.enter_context(nc.psum_tensor(f"{name}_{n}", shape, F32))

        def sem(n):
            return c.enter_context(nc.semaphore(f"{name}_{n}"))

        pick = sb("pick", [128, NB, K, TP])
        pick_t = sb("pick_t", [TP, 2, K, 128])
        raw = sb("raw", [128, K, 4])
        rated = sb("rated", [128, 2, K, 4])
        message = sb("message", [128, 2, K, 20])
        turned_p = psum("turned_p", [128, 2, 1024])
        node_p = psum("node_p", [128, 512])
        out_p = psum("out_p", [128, 512])
        picked, turned, moved, nodes_made, rated_done, exp_made, messages_done, out_made, taken = (
            sem(n) for n in ("picked", "turned", "moved", "nodes_made", "rated_done", "exp_made", "messages_done", "out_made", "taken"))
        block = c.enter_context(nc.Block())

        @block.tensor
        def _(pe):
            def turn(q, j):
                pe.wait_ge(picked, q + 1)
                reuse(pe, moved, q, j, 2, NB)
                for k in range(K):
                    ins = nc.tensor.transpose(turned_p[0:TP, j % 2, k * 128:(k + 1) * 128], pick[:, j, k, :], core.ident[:])
                ins.then_inc(turned, 1)

            def look_up(q, j):
                _, groups = nc.values_load_multi_w_load_instructions(
                    edge_group[0:1, bass.ds(q * K, K)], [mybir.EngineType.PE], min_val=0, max_val=NT - 1)
                pe.wait_ge(moved, q + 1)
                reuse(pe, rated_done, q, j, 1, NB)
                for k in range(K):
                    ins = nc.tensor.matmul(node_p[:, k * 8:(k + 1) * 8], pick_t[:, j % 2, k, :], node_scores[:, bass.ds(groups[k], 1), :],
                                           start=True, stop=True)
                ins.then_inc(nodes_made, 1)

            def add_up(q, j):
                pe.wait_ge(messages_done, q + 1)
                reuse(pe, taken, q, j, 1, NB)
                for k in range(K):
                    ins = nc.tensor.matmul(out_p[0:TP, k * 20:(k + 1) * 20], pick[:, j, k, :], message[:, j % 2, k, :], start=True, stop=True)
                ins.then_inc(out_made, 1)

            run_slots(pe, Q, NB, [(0, turn), (1, look_up), (2, add_up)])

        @block.scalar
        def _(act):
            def move(q, j):
                act.wait_ge(turned, q + 1)
                reuse(act, nodes_made, q, j, 2, NB)
                nc.scalar.copy(pick_t[:, j % 2, :, :], turned_p[0:TP, j % 2, 0:K * 128]).then_inc(moved, 1)

            def exp(q, j):
                act.wait_ge(rated_done, q + 1)
                nc.scalar.activation(rated[:, j % 2, :, :], rated[:, j % 2, :, :], ACT.Exp).then_inc(exp_made, 1)

            run_slots(act, Q, NB, [(0, move), (1, exp)])

        @block.vector
        def _(dve):
            v = nc.vector

            def choose(q, j):
                reuse(dve, out_made, q, j, NB, NB)
                for k in range(K):
                    v.tensor_scalar(pick[:, j, k, :], core.col[:, 0:TP], records[:, bass.ds(q * K + k, 1), 1], None, ALU.is_equal)
                dve.drain().then_inc(picked, 1)

            def rate(q, j):
                dve.wait_ge(nodes_made, q + 1)
                reuse(dve, messages_done, q, j, 2, NB)
                node = node_p[:, 0:8 * K].rearrange("p (k s) -> p k s", k=K)
                v.tensor_tensor(raw[:], gathered_rows[:, bass.ds(q * K, K), 16:20], node[:, :, 0:4], ALU.add)
                dve.drain()
                v.scalar_tensor_tensor(raw[:], raw[:], 0.2, raw[:], ALU.mult, ALU.max)
                dve.drain()
                v.tensor_tensor(rated[:, j % 2, :, :], raw[:], node[:, :, 4:8], ALU.subtract)
                dve.drain().then_inc(rated_done, 1)

            def send(q, j):
                dve.wait_ge(exp_made, q + 1)
                reuse(dve, out_made, q, j, 2, NB)
                for a in range(4):
                    v.tensor_tensor(message[:, j % 2, :, 4 * a:4 * a + 4], gathered_rows[:, bass.ds(q * K, K), 4 * a:4 * a + 4],
                                    rated[:, j % 2, :, a:a + 1].broadcast_to([128, K, 4]), ALU.mult)
                v.tensor_copy(message[:, j % 2, :, 16:20], rated[:, j % 2, :, :])
                dve.drain().then_inc(messages_done, 1)

            def take(q, j):
                _, groups = nc.values_load_multi_w_load_instructions(
                    edge_group[0:1, bass.ds(q * K, K)], [mybir.EngineType.DVE], min_val=0, max_val=NT - 1)
                dve.wait_ge(out_made, q + 1)
                for k in range(K):
                    mine = sums[:, bass.ds(groups[k], 1), :]
                    v.tensor_tensor(mine, mine, out_p[0:TP, k * 20:(k + 1) * 20].unsqueeze(1), ALU.add)
                    last = dve.drain()
                last.then_inc(taken, 1)

            run_slots(dve, Q, NB, [(0, choose), (1, rate), (2, send), (3, take)])


def slice_attention(core, name, x_t, wx, bx, slices, wo, bo, residual, loads, square_loads):
    nc = core.nc
    with ExitStack() as outer:
        def keep(n, shape):
            return outer.enter_context(nc.sbuf_tensor(f"{name}_{n}", shape, F32))

        mid_t = keep("mid_t", [128, KC, N])
        queries = keep("queries", [TP, NT, D])
        tile_best = keep("tile_best", [128, KC, NT])
        key_best = keep("key_best", [128, KC])
        key_best_b = keep("key_best_b", [TP, D])
        mixing = keep("mixing", [128, KC, 128])

        with ExitStack() as c:
            def sem(n):
                return c.enter_context(nc.semaphore(f"{name}_{n}"))

            mid_s = c.enter_context(nc.sbuf_tensor(f"{name}_mid_s", [128, U, KC, TP], F32))
            diag = c.enter_context(nc.sbuf_tensor(f"{name}_diag", [128, KC, 128], F32))
            mid_p = c.enter_context(nc.psum_tensor(f"{name}_mid_p", [128, 3, 512], F32))
            key_p = c.enter_context(nc.psum_tensor(f"{name}_key_p", [128, 3, 512], F32))
            spread_p = c.enter_context(nc.psum_tensor(f"{name}_spread_p", [128, 512], F32))
            landed, slices_cleared, squares_landed = sem("landed"), sem("slices_cleared"), sem("squares_landed")
            mid_made, mid_taken, keys_made, keys_taken, diag_made, spread_made = (
                sem(n) for n in ("mid_made", "mid_taken", "keys_made", "keys_taken", "diag_made", "spread_made"))
            block = c.enter_context(nc.Block())

            @block.sync
            def _(sp):
                for tile, dram in loads:
                    sp.dma_start(tile, dram).then_inc(landed, 16)
                sp.wait_ge(slices_cleared, 1)
                for tile, dram in square_loads:
                    sp.dma_start(tile, dram).then_inc(squares_landed, 16)

            @block.tensor
            def _(pe):
                pe.wait_ge(landed, 16 * len(loads))
                pe.wait_ge(squares_landed, 16 * len(square_loads))

                def mid(t, j):
                    reuse(pe, mid_taken, t, j, 3)
                    for o in range(KC):
                        for h in range(KC):
                            ins = nc.tensor.matmul(mid_p[:, j % 3, o * TP:(o + 1) * TP], wx[:, h, o * 128:(o + 1) * 128],
                                                   x_t[:, h, at(t)], start=h == 0, stop=h == KC - 1)
                    ins.then_inc(mid_made, 1)

                def keys(t, j):
                    pe.wait_ge(mid_taken, t + 1)
                    reuse(pe, keys_taken, t, j, 3)
                    for h in range(KC):
                        ins = nc.tensor.matmul(key_p[:, j % 3, h * TP:(h + 1) * TP], slices[:, 128:256], mid_s[:, j, h, :],
                                               start=True, stop=True)
                    ins.then_inc(keys_made, 1)

                run_slots(pe, NT, U, [(0, mid), (1, keys)])
                pe.wait_ge(diag_made, 1)
                nc.tensor.matmul(spread_p[0:TP, 0:D], core.ones[:, 0:TP], diag[:].rearrange("p h n -> p (h n)"),
                                 start=True, stop=True).then_inc(spread_made, 1)

            @block.scalar
            def _(act):
                act.wait_ge(landed, 16 * len(loads))

                def take(t, j):
                    act.wait_ge(mid_made, t + 1)
                    reuse(act, keys_made, t, j, U)
                    for h in range(KC):
                        nc.scalar.activation(mid_s[:, j, h, :], mid_p[:, j % 3, h * TP:(h + 1) * TP], ACT.Identity, bias=bx[:, h:h + 1])
                    act.drain().then_inc(mid_taken, 1)
                    nc.scalar.copy(mid_t[:, :, at(t)], mid_s[:, j, :, :])

                run_slots(act, NT, U, [(0, take)])

            @block.vector
            def _(dve):
                v = nc.vector
                v.memset(slices[:], 0.0)
                dve.drain().then_inc(slices_cleared, 1)

                def take(t, j):
                    dve.wait_ge(keys_made, t + 1)
                    v.tensor_reduce(tile_best[:, :, bass.ds(t, 1)], key_p[:, j % 3, 0:2 * TP].rearrange("p (h n) -> p h n", h=KC),
                                    AX_X, ALU.max).then_inc(keys_taken, 1)

                run_slots(dve, NT, U, [(0, take)])
                dve.drain()
                v.tensor_reduce(key_best[:], tile_best[:], AX_X, ALU.max)
                dve.drain()
                for h in range(KC):
                    v.tensor_scalar(diag[:, h, :], core.ident[:], key_best[:, h:h + 1], None, ALU.mult)
                dve.drain().then_inc(diag_made, 1)
                dve.wait_ge(spread_made, 1)
                v.tensor_copy(key_best_b[:], spread_p[0:TP, 0:D])

        with ExitStack() as c:
            def sem(n):
                return c.enter_context(nc.semaphore(f"{name}_{n}"))

            staged = c.enter_context(nc.sbuf_tensor(f"{name}_staged", [128, U, KC, TP], F32))
            kv_s = c.enter_context(nc.sbuf_tensor(f"{name}_kv_s", [TP, U, 2 * D + 1], F32))
            query_best = c.enter_context(nc.sbuf_tensor(f"{name}_query_best", [TP, 8], F32))
            qkv_p = c.enter_context(nc.psum_tensor(f"{name}_qkv_p", [128, 3, KC, 512], F32))
            total_p = c.enter_context(nc.psum_tensor(f"{name}_total_p", [128, KC, 512], F32))
            staged_done, qkv_made, qkv_taken, keys_done, keys_used = (
                sem(n) for n in ("staged_done", "qkv_made", "qkv_taken", "keys_done", "keys_used"))
            block = c.enter_context(nc.Block())

            @block.gpsimd
            def _(pool):
                def stage(t, j):
                    reuse(pool, qkv_made, t, j, U)
                    nc.gpsimd.tensor_copy(staged[:, j, :, :], mid_t[:, :, at(t)]).then_inc(staged_done, 1)

                run_slots(pool, NT, U, [(0, stage)])

            @block.tensor
            def _(pe):
                for h in range(KC):
                    nc.tensor.matmul(total_p[:, h, 0:D + 1], core.zeros[:], core.wide_zeros[:, 0:D + 1], start=True, stop=False,
                                     skip_group_check=True)

                def products(t, j):
                    pe.wait_ge(staged_done, t + 1)
                    reuse(pe, qkv_taken, t, j, 3)
                    for h in range(KC):
                        ins = nc.tensor.matmul(qkv_p[0:TP, j % 3, h, 0:384], staged[:, j, h, :], slices[:], start=True, stop=True)
                    ins.then_inc(qkv_made, 1)

                def totals(t, j):
                    pe.wait_ge(keys_done, t + 1)
                    for h in range(KC):
                        ins = nc.tensor.matmul(total_p[:, h, 0:D + 1], kv_s[:, j, h * 128:(h + 1) * 128], kv_s[:, j, D:2 * D + 1],
                                               start=False, stop=False, skip_group_check=True)
                    ins.then_inc(keys_used, 1)

                run_slots(pe, NT, U, [(0, products), (2, totals)])

            @block.scalar
            def _(act):
                def exp(t, j):
                    act.wait_ge(qkv_taken, t + 1)
                    nc.scalar.activation(queries[:, bass.ds(t, 1), :], queries[:, bass.ds(t, 1), :], ACT.Exp)
                    nc.scalar.activation(kv_s[:, j, 0:D], kv_s[:, j, 0:D], ACT.Exp).then_inc(keys_done, 1)

                run_slots(act, NT, U, [(0, exp)])

            @block.vector
            def _(dve):
                v = nc.vector
                v.memset(kv_s[:, :, 2 * D:2 * D + 1], 1.0)

                def take(t, j):
                    dve.wait_ge(qkv_made, t + 1)
                    reuse(dve, keys_used, t, j, U)
                    q = qkv_p[0:TP, j % 3, :, 0:128]
                    for h in range(KC):
                        v.tensor_reduce(query_best[:, 4 * h:4 * h + 4], q[:, h, :].rearrange("p (g s) -> p g s", g=4), AX_X, ALU.max)
                    v.tensor_tensor(kv_s[:, j, 0:D].rearrange("p (h s) -> p h s", h=KC), qkv_p[0:TP, j % 3, :, 128:256],
                                    key_best_b[:].rearrange("p (h s) -> p h s", h=KC), ALU.subtract)
                    v.tensor_copy(kv_s[:, j, D:2 * D].rearrange("p (h s) -> p h s", h=KC), qkv_p[0:TP, j % 3, :, 256:384])
                    dve.drain()
                    for h in range(KC):
                        v.tensor_tensor(queries[:, bass.ds(t, 1), h * 128:(h + 1) * 128].rearrange("p o (g s) -> p (o g) s", g=4),
                                        q[:, h, :].rearrange("p (g s) -> p g s", g=4),
                                        query_best[:, 4 * h:4 * h + 4].unsqueeze(2).broadcast_to([TP, 4, 32]), ALU.subtract)
                    dve.drain().then_inc(qkv_taken, 1)

                run_slots(dve, NT, U, [(0, take)])
                dve.wait_ge(keys_used, NT)

                for h in range(KC):
                    v.reciprocal(key_best[:, h:h + 1], total_p[:, h, D:D + 1])
                dve.drain()
                for h in range(KC):
                    v.scalar_tensor_tensor(mixing[:, h, :], total_p[:, h, h * 128:(h + 1) * 128], key_best[:, h:h + 1],
                                           core.same_head[:], ALU.mult, ALU.mult)

        with ExitStack() as c:
            def sb(n, shape):
                return c.enter_context(nc.sbuf_tensor(f"{name}_{n}", shape, F32))

            def psum(n):
                return c.enter_context(nc.psum_tensor(f"{name}_{n}", [128, 2, 512], F32))

            def sem(n):
                return c.enter_context(nc.semaphore(f"{name}_{n}"))

            query_s, query_t, share = sb("query_s", [TP, U, D]), sb("query_t", [128, U, KC, TP]), sb("share", [TP, U, 8])
            mixed, mixed_t = sb("mixed", [TP, U, D]), sb("mixed_t", [128, U, KC, TP])
            query_p, mixed_p, turned_p, out_p = psum("query_p"), psum("mixed_p"), psum("turned_p"), psum("out_p")
            query_staged, query_turned, query_moved, mixed_made, mixed_done, turned_made, turned_moved, out_made, out_added = (
                sem(n) for n in ("query_staged", "query_turned", "query_moved", "mixed_made", "mixed_done", "turned_made",
                                 "turned_moved", "out_made", "out_added"))
            block = c.enter_context(nc.Block())

            def turn_tile(to, source, j):
                for h in range(KC):
                    ins = nc.tensor.transpose(to[:, j % 2, h * TP:(h + 1) * TP], source[:, j, h * 128:(h + 1) * 128],
                                              core.ident[0:TP, 0:TP])
                return ins

            @block.tensor
            def _(pe):
                def turn_query(t, j):
                    pe.wait_ge(query_staged, t + 1)
                    reuse(pe, query_moved, t, j, 2)
                    turn_tile(query_p, query_s, j).then_inc(query_turned, 1)

                def mix(t, j):
                    pe.wait_ge(query_moved, t + 1)
                    reuse(pe, mixed_done, t, j, 2)
                    for h in range(KC):
                        ins = nc.tensor.matmul(mixed_p[0:TP, j % 2, h * 128:(h + 1) * 128], query_t[:, j, h, :], mixing[:, h, :],
                                               start=True, stop=True)
                    ins.then_inc(mixed_made, 1)

                def turn(t, j):
                    pe.wait_ge(mixed_done, t + 1)
                    reuse(pe, turned_moved, t, j, 2)
                    turn_tile(turned_p, mixed, j).then_inc(turned_made, 1)

                def output(t, j):
                    pe.wait_ge(turned_moved, t + 1)
                    reuse(pe, out_added, t, j, 2)
                    for h in range(KC):
                        ins = nc.tensor.matmul(out_p[0:TP, j % 2, 0:D], mixed_t[:, j, h, :], wo[:, h, :], start=h == 0, stop=h == KC - 1)
                    ins.then_inc(out_made, 1)

                run_slots(pe, NT, U, [(0, turn_query), (1, mix), (2, turn), (3, output)])

            @block.scalar
            def _(act):
                def move(to, source, j):
                    return nc.scalar.copy(to[:, j, :, :], source[:, j % 2, 0:2 * TP].rearrange("p (h n) -> p h n", h=KC))

                def move_query(t, j):
                    act.wait_ge(query_turned, t + 1)
                    reuse(act, mixed_made, t, j, U)
                    move(query_t, query_p, j).then_inc(query_moved, 1)

                def move_mixed(t, j):
                    act.wait_ge(turned_made, t + 1)
                    reuse(act, out_made, t, j, U)
                    move(mixed_t, turned_p, j).then_inc(turned_moved, 1)

                run_slots(act, NT, U, [(0, move_query), (2, move_mixed)])

            @block.vector
            def _(dve):
                v = nc.vector

                def stage(t, j):
                    reuse(dve, query_turned, t, j, U)
                    reuse(dve, mixed_done, t, j, U)
                    mine = queries[:, bass.ds(t, 1), :]
                    v.tensor_copy(query_s[:, j:j + 1, :], mine)
                    v.tensor_reduce(share[:, j, :], mine.rearrange("p o (g s) -> p (o g) s", s=32), AX_X, ALU.add)
                    dve.drain().then_inc(query_staged, 1)
                    v.reciprocal(share[:, j, :], share[:, j, :])

                def share_out(t, j):
                    dve.drain()
                    dve.wait_ge(mixed_made, t + 1)
                    reuse(dve, turned_made, t, j, U)
                    v.tensor_tensor(mixed[:, j, :].rearrange("p (g d) -> p g d", g=8), mixed_p[0:TP, j % 2, 0:D].rearrange("p (g d) -> p g d", g=8),
                                    share[:, j, :].unsqueeze(2).broadcast_to([TP, 8, 32]), ALU.mult)
                    dve.drain().then_inc(mixed_done, 1)

                def add(t, j):
                    dve.wait_ge(out_made, t + 1)
                    mine = residual[:, bass.ds(t, 1), :]
                    v.tensor_tensor(mine, mine, out_p[0:TP, j % 2, 0:D].unsqueeze(1), ALU.add)
                    dve.drain().then_inc(out_added, 1)

                v.tensor_tensor(residual[:], residual[:], bo[:].unsqueeze(1).broadcast_to([TP, NT, D]), ALU.add)
                dve.drain()
                run_slots(dve, NT, U, [(0, stage), (1, share_out), (3, add)])


def across(matrix):
    return matrix.rearrange("(t p) n -> p t n", p=TP)


def wide(row, width=D):
    return row.unsqueeze(1).broadcast_to([TP, NT, width])


class Scope:

    def __init__(self, core, name):
        self.core, self.name, self.stack = core, name, ExitStack()

    def __enter__(self):
        return self

    def __exit__(self, *error):
        self.stack.close()

    def __call__(self, name, shape, dt=F32):
        return self.stack.enter_context(self.core.nc.sbuf_tensor(f"{self.name}_{name}", shape, dt))


def scores_of(core, name, x_t, weight, bias, experts, scores, router, shift):
    nc = core.nc

    def evacuate(dve, t, j, out):
        mine = scores[:, bass.ds(t, 1), :]
        if bias is None:
            nc.vector.tensor_copy(mine, out.unsqueeze(1))
        else:
            nc.vector.tensor_tensor(mine, out.unsqueeze(1), shift[:].unsqueeze(1), ALU.add)

    loads = [(router[:], halves(weight))] + ([] if bias is None else [(shift[:], spread(bias))])
    project(core, name, [x_t], [(0, router, 0, True, True)], experts, evacuate, loads)


def expert_layer(core, name, x_t, gates, experts, chunks, w1, b1, w2, b2):
    nc = core.nc
    H = chunks * 128
    with Scope(core, name) as sb:
        w1_s, w2_s = sb("w1", [128, KC, experts * H]), sb("w2", [128, experts * chunks, D])
        b1_s, b2_s = sb("b1", [128, experts * chunks]), sb("b2", [TP, experts, D])

        def load_weights(e):
            return [(w1_s[:, :, e * H:(e + 1) * H], halves(w1[e])),
                    (w2_s[:, e * chunks:(e + 1) * chunks, :], w2[e].rearrange("(c p) d -> p c d", p=128))]

        feed_forward(core, f"{name}_ff", x_t, experts, chunks, load_weights, b1_s, ACT.Gelu, w1_s, w2_s, None, gates, b2_s,
                     loads=[(b1_s[:], b1), (b2_s[:], spread(b2))])


def linear_attention(core, name, x_t, wq, wkv, wo, bq, bkv, bo, feature, norm):
    with Scope(core, name) as sb:
        wq_s, wkv_s, wo_s = sb("wq", [128, KC, D]), sb("wkv", [128, KC, 2 * D]), sb("wo", [128, KC, D])
        bo_s = sb("bo", [TP, D])
        bq_s, bkv_s = (None, None) if bq is None else (sb("bq", [128, KC]), sb("bkv", [TP, 2 * D]))
        part = 2 * D // len(wkv)
        loads = [(wkv_s[:, :, i * part:(i + 1) * part], halves(w)) for i, w in enumerate(wkv)]
        if bq is not None:
            loads += [(bkv_s[:, i * D:(i + 1) * D], spread(b)) for i, b in enumerate(bkv)] + [(bq_s[:], bq)]
        loads += [(wq_s[:], halves(wq)), (wo_s[:], halves(wo)), (bo_s[:], spread(bo))]
        attention(core, f"{name}_at", x_t, wq_s, wkv_s, wo_s, bq_s, bkv_s, bo_s, loads, feature, norm)


def layer0(core, w, x_t, by_src):
    nc, x = core.nc, core.x
    table = nc.dram_tensor("l0_rows", (N, D), F32).ap()
    layer_norm(core, "l0_norm", x, None, table, x_t)
    with Scope(core, "l0") as sb:
        sums = sb("sums", [TP, NT, 2 * D])
        sum_edges(core, "l0_edges", table, *by_src, sums, words=(2, 3))
        with Scope(core, "l0_gnn") as sb2:
            sums_t, weight = sb2("sums_t", [128, KC, N]), sb2("weight", [128, KC, D])
            for k, branch in enumerate(("low", "high")):
                half = sums[:, :, k * D:(k + 1) * D]
                turn_rows(core, f"l0_turn_{branch}", half, sums_t)

                def evacuate(dve, t, j, out, half=half):
                    nc.vector.tensor_scalar(half[:, bass.ds(t, 1), :], out.unsqueeze(1), 0.0, None, ALU.max)

                project(core, f"l0_{branch}", [sums_t], [(0, weight, 0, True, True)], D, evacuate,
                        [(weight[:], halves(w[f"L0_gnn_weight_{branch}"]))])
        with Scope(core, "l0_mlp") as sb2:
            mlp = sb2("rows", [TP, NT, D])
            with Scope(core, "l0_mlp_weight") as sb3:
                weight = sb3("s", [128, KC, D])

                def evacuate_mlp(dve, t, j, out):
                    nc.vector.tensor_scalar(mlp[:, bass.ds(t, 1), :], out.unsqueeze(1), 0.0, None, ALU.max)

                project(core, "l0_mlp", [x_t], [(0, weight, 0, True, True)], D, evacuate_mlp,
                        [(weight[:], halves(w["L0_gnn_weight_mlp"]))])
            attend, attend_mix = sb2("attend", [TP, 3, D]), sb2("attend_mix", [TP, 9])
            blend(core, "l0_blend", sums[:, :, 0:D], sums[:, :, D:2 * D], mlp[:], attend, attend_mix,
                  [(attend[:, k, :], spread(w[f"L0_gnn_att_vec_{b}"].rearrange("d o -> (d o)"))) for k, b in enumerate(("low", "high", "mlp"))]
                  + [(attend_mix[:], spread(w["L0_gnn_att_vec"].rearrange("a b -> (a b)")))])
    linear_attention(core, "l0_mix", x_t, w["L0_mix_wq"], (w["L0_mix_wk"], w["L0_mix_wv"]), w["L0_mix_wo"], w["L0_mix_bq"],
                     (w["L0_mix_bk"], w["L0_mix_bv"]), w["L0_mix_bo"], True, "add")


def layer0_ffn(core, w, x_t):
    E = 8
    with Scope(core, "l0f") as sb:
        gain, shift = sb("gain", [128, KC]), sb("shift", [128, KC])
        scores, gates, router, bias = sb("scores", [TP, NT, E]), sb("gates", [TP, NT, E]), sb("router", [128, KC, E]), sb("bias", [TP, E])
        small_rows(core, "l0f_load", lambda dve, call: None, (), [(gain[:], w["L0_ffn_gamma"]), (shift[:], w["L0_ffn_beta"])])
        layer_norm(core, "l0f_norm", core.x, None, None, x_t, True, gain, shift)
        scores_of(core, "l0f_scores", x_t, w["L0_ffn_Wr"], w["L0_ffn_br"], E, scores, router, bias)
        gate_top2(core, "l0f_gate", scores, E, gates, False)
        expert_layer(core, "l0f_experts", x_t, gates, E, 4, w["L0_ffn_W1"], w["L0_ffn_b1"], w["L0_ffn_W2"], w["L0_ffn_b2"])


def layer1(core, w, x_t, by_dst):
    nc, x = core.nc, core.x
    table = nc.dram_tensor("l1_rows", (N, D), F32).ap()
    layer_norm(core, "l1_norm", x, None, table, x_t)
    with Scope(core, "l1") as sb:
        sums, sums_t = sb("sums", [TP, NT, D]), sb("sums_t", [128, KC, N])
        own, other = sb("own", [128, KC, D]), sb("other", [128, KC, D])
        sum_edges(core, "l1_edges", table, *by_dst, sums)
        turn_rows(core, "l1_turn", sums, sums_t)

        def evacuate(dve, t, j, out):
            mine = x[:, bass.ds(t, 1), :]
            nc.vector.scalar_tensor_tensor(mine, out.unsqueeze(1), 0.0, mine, ALU.max, ALU.add)

        project(core, "l1_gnn", [x_t, sums_t], [(0, own, 0, True, False), (1, other, 0, False, True)], D, evacuate,
                [(own[:], halves(w["L1_gnn_W"])), (other[:], halves(w["L1_gnn_M"]))])
    linear_attention(core, "l1_mix", x_t, w["L1_mix_Wq"], (w["L1_mix_Wk"], w["L1_mix_Wv"]), w["L1_mix_Wfc"], w["L1_mix_bq"],
                     (w["L1_mix_bk"], w["L1_mix_bv"]), w["L1_mix_bfc"], False, "length")


def layer1_ffn(core, w, x_t):
    nc, x = core.nc, core.x
    E = 32
    layer_norm(core, "l1f_norm", x, None, None, x_t)
    with Scope(core, "l1f") as sb:
        chosen = sb("chosen", [E, N])
        with Scope(core, "l1f_router") as sb2:
            scores, router, bias = sb2("scores", [TP, NT, E]), sb2("weight", [128, KC, E]), sb2("bias", [TP, E])
            scores_of(core, "l1f_scores", x_t, w["L1_ffn_router_w"], w["L1_ffn_router_b"], E, scores, router, bias)
            pick_expert(core, "l1f_pick", scores, E, chosen)
        w1, w2, b1, b2 = sb("w1", [128, KC, 2048]), sb("w2", [128, 16, D]), sb("b1", [128, 16]), sb("b2", [E, D])
        W1, W2 = w["L1_ffn_W1"], w["L1_ffn_W2"]

        def load_weights(e):
            eight = slice(e * 8, (e + 1) * 8)
            return [(w1[:, h, e * 512:(e + 1) * 512].rearrange("p (e h) -> p e h", e=8),
                     W1[eight, h * 128:(h + 1) * 128, :].rearrange("e p h -> p e h")) for h in range(KC)] + [
                (w2[:, e * 4:(e + 1) * 4, :], W2[eight].rearrange("(i two) h d -> (two h) i d", two=2))]

        def take(dve, t, out):
            mine = x[:, bass.ds(t, 1), :]
            nc.vector.scalar_tensor_tensor(mine, out.unsqueeze(1), 0.0, mine, ALU.max, ALU.add)

        feed_forward(core, "l1f_ff", x_t, 4, 4, load_weights, b1, ACT.Relu, w1, w2, take, None, b2, chosen,
                     loads=[(b1[:], w["L1_ffn_b1"]), (b2[:], w["L1_ffn_b2"])])


def layer2(core, w, x_t, by_dst, xn):
    nc, x = core.nc, core.x
    v = nc.vector
    table = nc.dram_tensor("l2_messages", (N, D), F32).ap()
    layer_norm(core, "l2_norm", x, xn, None, x_t)
    with Scope(core, "l2") as sb:
        own = sb("own", [TP, NT, D])
        scale2, shift2 = sb("scale2", [TP, D]), sb("shift2", [TP, D])
        with Scope(core, "l2_messages") as sb2:
            weight = sb2("weight", [128, KC, 2 * D])
            row = {n: sb2(n, [TP, D]) for n in ("gamma1", "beta1", "mean1", "var1", "mean2", "var2", "bias")}
            message = sb2("message", [TP, NT, D])
            both = w["L2_gnn_W"]

            def prepare(dve, call):
                v.tensor_tensor(weight[:, :, D:2 * D], weight[:, :, D:2 * D], weight[:, :, 0:D], ALU.subtract)
                v.tensor_scalar(row["var1"][:], row["var1"][:], EPS, None, ALU.add)
                v.tensor_scalar(row["var2"][:], row["var2"][:], EPS, None, ALU.add)
                call(0)
                call(1)
                v.reciprocal(row["var1"][:], row["var1"][:])
                v.reciprocal(row["var2"][:], row["var2"][:])
                v.tensor_tensor(row["mean1"][:], row["bias"][:], row["mean1"][:], ALU.subtract)
                dve.drain()
                v.tensor_tensor(row["gamma1"][:], row["gamma1"][:], row["var1"][:], ALU.mult)
                v.tensor_tensor(scale2[:], scale2[:], row["var2"][:], ALU.mult)
                dve.drain()
                v.tensor_tensor(row["mean1"][:], row["mean1"][:], row["gamma1"][:], ALU.mult)
                v.tensor_tensor(row["mean2"][:], row["mean2"][:], scale2[:], ALU.mult)
                dve.drain()
                v.tensor_tensor(row["beta1"][:], row["beta1"][:], row["mean1"][:], ALU.add)
                v.tensor_tensor(shift2[:], shift2[:], row["mean2"][:], ALU.subtract)

            def sqrt_of(tile):
                return lambda act: nc.scalar.activation(tile[:], tile[:], ACT.Sqrt)

            small_rows(core, "l2_prepare", prepare, (), [
                (weight[:, :, 0:D], halves(both[0:D])), (weight[:, :, D:2 * D], halves(both[D:2 * D])),
                (row["gamma1"][:], spread(w["L2_gnn_bn1_gamma"])), (row["beta1"][:], spread(w["L2_gnn_bn1_beta"])),
                (row["mean1"][:], spread(w["L2_gnn_bn1_mean"])), (row["var1"][:], spread(w["L2_gnn_bn1_var"])),
                (scale2[:], spread(w["L2_gnn_bn2_gamma"])), (shift2[:], spread(w["L2_gnn_bn2_beta"])),
                (row["mean2"][:], spread(w["L2_gnn_bn2_mean"])), (row["var2"][:], spread(w["L2_gnn_bn2_var"])),
                (row["bias"][:], spread(w["L2_gnn_b"]))], [sqrt_of(row["var1"]), sqrt_of(row["var2"])])

            def evacuate(dve, t, j, out):
                gamma, mine = row["gamma1"][:].unsqueeze(1), own[:, bass.ds(t, 1), :]
                v.tensor_tensor(message[:, bass.ds(t, 1), :], out[:, 0:D].unsqueeze(1), gamma, ALU.mult)
                v.tensor_tensor(mine, out[:, D:2 * D].unsqueeze(1), gamma, ALU.mult)
                dve.drain()
                v.tensor_tensor(mine, mine, row["beta1"][:].unsqueeze(1), ALU.add)

            project(core, "l2_project", [x_t], [(0, weight, 0, True, True)], 2 * D, evacuate)
            small_rows(core, "l2_store", lambda dve, call: None, [(across(table), message[:])])
        best = sb("best", [TP, NT, D])
        max_edges(core, "l2_edges", table, *by_dst, best)

        def finish(dve, call):
            v.tensor_tensor(best[:], best[:], own[:], ALU.add)
            v.tensor_tensor(x[:], x[:], xn[:], ALU.add)
            dve.drain()
            v.scalar_tensor_tensor(best[:], best[:], 0.0, wide(scale2[:]), ALU.max, ALU.mult)
            v.tensor_tensor(x[:], x[:], wide(shift2[:]), ALU.add)
            dve.drain()
            v.tensor_tensor(x[:], x[:], best[:], ALU.add)

        small_rows(core, "l2_finish", finish)


def layer2_mix(core, w, x_t, xn):
    nc, x = core.nc, core.x
    v = nc.vector
    with Scope(core, "l2m") as sb:
        gain, shift, gain2, shift2 = (sb(n, [128, KC]) for n in ("gain", "shift", "gain2", "shift2"))
        small_rows(core, "l2m_load", lambda dve, call: None, (), [
            (gain[:], w["L2_mix_ln1_w"]), (shift[:], w["L2_mix_ln1_b"]), (gain2[:], w["L2_mix_ln2_w"]), (shift2[:], w["L2_mix_ln2_b"])])
        layer_norm(core, "l2m_norm", xn, None, None, x_t, False, gain, shift)
        with Scope(core, "l2m_slices") as sb2:
            wx, wo, bx = sb2("wx", [128, KC, D]), sb2("wo", [128, KC, D]), sb2("bx", [128, KC])
            slices, bo = sb2("slices", [128, 384]), sb2("bo", [TP, D])
            slice_attention(core, "l2m_at", x_t, wx, bx, slices, wo, bo, xn,
                            [(wx[:], halves(w["L2_mix_Wx"])), (wo[:], halves(w["L2_mix_Wo"])), (bx[:], w["L2_mix_bx"]),
                             (bo[:], spread(w["L2_mix_bo"]))],
                            [(slices[32 * h:32 * h + 32, 128 * k + 32 * h:128 * k + 32 * h + 32], w[f"L2_mix_{n}"])
                             for k, n in enumerate(("Wq", "Wk", "Wv")) for h in range(4)])
        layer_norm(core, "l2m_norm2", xn, None, None, x_t, False, gain2, shift2)
        w1, w2, b1, b2 = sb("w1", [128, KC, 1024]), sb("w2", [128, 8, D]), sb("b1", [128, 8]), sb("b2", [TP, D])
        W1, W2 = w["L2_mix_W1"], w["L2_mix_W2"]

        def load_weights(e):
            return [(w1[:, :, e * 512:(e + 1) * 512], halves(W1[:, e * 512:(e + 1) * 512])),
                    (w2[:, e * 4:(e + 1) * 4, :], W2[e * 512:(e + 1) * 512].rearrange("(c p) d -> p c d", p=128))]

        def take(dve, t, out):
            mine, mid = x[:, bass.ds(t, 1), :], xn[:, bass.ds(t, 1), :]
            v.tensor_tensor(mid, mid, out.unsqueeze(1), ALU.add)
            v.tensor_tensor(mine, mine, b2[:].unsqueeze(1), ALU.add)
            dve.drain()
            v.tensor_tensor(mine, mine, mid, ALU.add)

        feed_forward(core, "l2m_ff", x_t, 2, 4, load_weights, b1, ACT.Gelu, w1, w2, take,
                     loads=[(b1[:], w["L2_mix_b1"]), (b2[:], spread(w["L2_mix_b2"]))])


def layer2_ffn(core, w, x_t):
    nc, x = core.nc, core.x
    v = nc.vector
    E = 4
    table = nc.dram_tensor("l2f_rows", (N, 20), F32).ap()
    layer_norm(core, "l2f_norm", x, None, None, x_t)
    with Scope(core, "l2f") as sb:
        gates = sb("gates", [TP, NT, E])
        with Scope(core, "l2f_gat") as sb2:
            records, edge_group = sb2("records", [128, ET_GAT + ET_PAD, 4]), sb2("edge_group", [1, ET_GAT + ET_PAD], I32)
            edges = w["L2_ffn_edge_index"]
            group_edges(core, "l2f_group", E_GAT, ET_GAT, edges[1], edges[0], [], records, edge_group)
            weight, row = sb2("weight", [128, KC, 16]), sb2("row", [TP, NT, 20])
            to_src, to_dst, bias, gain, shift = (sb2(n, [TP, 16]) for n in ("to_src", "to_dst", "bias", "gain", "shift"))
            product, node, best = sb2("product", [TP, NT, 16]), sb2("node", [TP, NT, 8]), sb2("best", [TP, NT, 4])
            own, raw, sums, scores = sb2("own", [TP, NT, 4]), sb2("raw", [TP, NT, 4]), sb2("sums", [TP, NT, 20]), sb2("scores", [TP, NT, 4])
            mean, var, dev = sb2("mean", [TP, NT]), sb2("var", [TP, NT]), sb2("dev", [TP, NT])
            gathered_rows = sb2("gathered_rows", [128, ET_GAT, 20])

            def evacuate(dve, t, j, out):
                v.tensor_copy(row[:, bass.ds(t, 1), 0:16], out.unsqueeze(1))

            project(core, "l2f_features", [x_t], [(0, weight, 0, True, True)], 16, evacuate, [(weight[:], halves(w["L2_ffn_W_gat"]))])

            def rate(dve, call):
                for vector, to in ((to_src, row[:, :, 16:20]), (to_dst, node[:, :, 0:4])):
                    v.tensor_tensor(product[:], row[:, :, 0:16], wide(vector[:], 16), ALU.mult)
                    dve.drain()
                    v.tensor_reduce(to, product[:].rearrange("p t (a c) -> p t a c", a=4), AX_X, ALU.add)
                    dve.drain()
                v.tensor_copy(best[:], row[:, :, 16:20])

            small_rows(core, "l2f_rate", rate, [(across(table), row[:])], [
                (to_src[:], spread(w["L2_ffn_att_src"].rearrange("a c -> (a c)"))),
                (to_dst[:], spread(w["L2_ffn_att_dst"].rearrange("a c -> (a c)"))),
                (bias[:], spread(w["L2_ffn_b_gat"])), (gain[:], spread(w["L2_ffn_ln_gamma"])), (shift[:], spread(w["L2_ffn_ln_beta"]))])
            gat_edges(core, "l2f_edges", table, records, edge_group, gathered_rows, best)

            def start(dve, call):
                v.tensor_tensor(raw[:], best[:], node[:, :, 0:4], ALU.add)
                v.tensor_tensor(own[:], row[:, :, 16:20], node[:, :, 0:4], ALU.add)
                dve.drain()
                v.scalar_tensor_tensor(node[:, :, 4:8], raw[:], 0.2, raw[:], ALU.mult, ALU.max)
                v.scalar_tensor_tensor(own[:], own[:], 0.2, own[:], ALU.mult, ALU.max)
                dve.drain()
                v.tensor_tensor(own[:], own[:], node[:, :, 4:8], ALU.subtract)
                call(0)
                for a in range(4):
                    v.tensor_tensor(sums[:, :, 4 * a:4 * a + 4], row[:, :, 4 * a:4 * a + 4], own[:, :, a:a + 1].broadcast_to([TP, NT, 4]), ALU.mult)
                v.tensor_copy(sums[:, :, 16:20], own[:])

            small_rows(core, "l2f_start", start, (), (), [lambda act: nc.scalar.activation(own[:], own[:], ACT.Exp)])
            gat_sums(core, "l2f_sums", records, edge_group, gathered_rows, node, sums)

            def score(dve, call):
                v.tensor_scalar(raw[:], sums[:, :, 16:20], 1e-16, None, ALU.add)
                dve.drain()
                v.reciprocal(raw[:], raw[:])
                dve.drain()
                for a in range(4):
                    v.tensor_tensor(product[:, :, 4 * a:4 * a + 4], sums[:, :, 4 * a:4 * a + 4], raw[:, :, a:a + 1].broadcast_to([TP, NT, 4]), ALU.mult)
                dve.drain()
                v.tensor_tensor(product[:], product[:], wide(bias[:], 16), ALU.add)
                dve.drain()
                v.tensor_reduce(mean[:], product[:], AX_X, ALU.add)
                dve.drain()
                v.tensor_scalar(mean[:], mean[:], 1.0 / 16.0, None, ALU.mult)
                dve.drain()
                v.tensor_tensor(product[:], product[:], mean[:].unsqueeze(2).broadcast_to([TP, NT, 16]), ALU.subtract)
                dve.drain()
                v.tensor_tensor(row[:, :, 0:16], product[:], product[:], ALU.mult)
                dve.drain()
                v.tensor_reduce(var[:], row[:, :, 0:16], AX_X, ALU.add)
                dve.drain()
                v.tensor_scalar(var[:], var[:], 1.0 / 16.0, EPS, ALU.mult, ALU.add)
                call(0)
                v.reciprocal(dev[:], dev[:])
                dve.drain()
                v.tensor_tensor(product[:], product[:], dev[:].unsqueeze(2).broadcast_to([TP, NT, 16]), ALU.mult)
                dve.drain()
                v.tensor_tensor(product[:], product[:], wide(gain[:], 16), ALU.mult)
                dve.drain()
                v.tensor_tensor(product[:], product[:], wide(shift[:], 16), ALU.add)
                dve.drain()
                v.tensor_reduce(scores[:], product[:].rearrange("p t (a c) -> p t c a", a=4), AX_X, ALU.add)
                dve.drain()
                v.tensor_scalar(scores[:], scores[:], 0.25, None, ALU.mult)

            small_rows(core, "l2f_score", score, (), (), [lambda act: nc.scalar.activation(dev[:], var[:], ACT.Sqrt)])
            gate_top2(core, "l2f_gate", scores, E, gates, False)
        expert_layer(core, "l2f_experts", x_t, gates, E, 4, w["L2_ffn_W1"], w["L2_ffn_b1"], w["L2_ffn_W2"], w["L2_ffn_b2"])


def layer3(core, w, x_t, by_src, by_dst):
    nc, x = core.nc, core.x
    v = nc.vector
    nodes_table, edges_table, mid_table = (nc.dram_tensor(f"l3_table_{n}", (N, D), F32).ap() for n in ("nodes", "edges", "mid"))
    layer_norm(core, "l3_norm", x, None, nodes_table, x_t)
    with Scope(core, "l3") as sb:
        in_share, out_share = sb("in_share", [TP, NT]), sb("out_share", [TP, NT])
        has = sb("has", [TP, NT])
        slope, low = sb("slope", [TP, 1]), sb("low", [TP, U, D])
        weight, bias = sb("weight", [128, KC, D]), sb("bias", [TP, D])
        mid = sb("mid", [TP, NT, D])
        sums_t = sb("sums_t", [128, KC, N])
        for k in range(2):
            sides = ((by_dst, in_share), (by_src, out_share))
            source = (nodes_table, mid_table)[k]
            with Scope(core, f"l3_conv{k}") as sb2:
                sums = sb2("sums", [TP, NT, D + 1])
                for s, (records, share) in enumerate(sides):
                    sum_edges(core, f"l3_edges{k}_{s}", source, *records, sums if k == 0 else sums[:, :, 0:D], counted=k == 0)
                    source = edges_table

                    def shares(dve, call, share=share, s=s, sums=sums):
                        if k == 0:
                            v.tensor_scalar(share[:], sums[:, :, D], 1.0, None, ALU.max)
                            v.tensor_scalar(has[:], sums[:, :, D], 1.0, None, ALU.min)
                            dve.drain()
                            v.reciprocal(share[:], share[:])
                            dve.drain()
                            v.tensor_tensor(share[:], share[:], has[:], ALU.mult)
                            dve.drain()
                        if s == 0:
                            v.tensor_tensor(sums[:, :, 0:D], sums[:, :, 0:D], share[:].unsqueeze(2).broadcast_to([TP, NT, D]), ALU.mult)

                    if s == 0 or k == 0:
                        small_rows(core, f"l3_shares{k}_{s}", shares, [(across(edges_table), sums[:, :, 0:D])] if s == 0 else ())
                turn_rows(core, f"l3_turn{k}", sums[:, :, 0:D], sums_t, out_share)

            def evacuate(dve, t, j, out, k=k):
                mine, below = mid[:, bass.ds(t, 1), :], low[:, j:j + 1, :]
                if k == 0:
                    v.tensor_tensor(mine, out.unsqueeze(1), bias[:].unsqueeze(1), ALU.add)
                else:
                    v.tensor_tensor(mine, out.unsqueeze(1), mine, ALU.add)
                    dve.drain()
                    v.tensor_tensor(mine, mine, bias[:].unsqueeze(1), ALU.add)
                dve.drain()
                v.tensor_scalar(below, mine, 0.0, slope[:, 0:1], ALU.min, ALU.mult)
                dve.drain()
                v.scalar_tensor_tensor(mine, mine, 0.0, below, ALU.max, ALU.add)
                if k == 1:
                    dve.drain()
                    v.tensor_tensor(x[:, bass.ds(t, 1), :], x[:, bass.ds(t, 1), :], mine, ALU.add)

            loads = [(weight[:], halves(w[f"L3_gnn_W{k + 1}"])), (bias[:], spread(w[f"L3_gnn_b{k + 1}"]))]
            loads.append((slope[:], spread(w["L3_gnn_a"])) if k == 0 else (mid[:], across(nodes_table)))
            project(core, f"l3_conv{k}", [sums_t], [(0, weight, 0, True, True)], D, evacuate, loads)
            if k == 0:
                small_rows(core, "l3_store", lambda dve, call: None, [(across(mid_table), mid[:])])
    linear_attention(core, "l3_mix", x_t, w["L3_mix_Wq"], (w["L3_mix_Wkv"],), w["L3_mix_Wproj"], None, None, w["L3_mix_bproj"], True, "max")


def layer3_ffn(core, w, x_t, xn):
    nc, x = core.nc, core.x
    E = 8
    layer_norm(core, "l3f_norm", x, xn, None, x_t)
    with Scope(core, "l3f") as sb:
        scores, gates, router = sb("scores", [TP, NT, E]), sb("gates", [TP, NT, E]), sb("router", [128, KC, E])
        scores_of(core, "l3f_scores", x_t, w["L3_ffn_router_w"], None, E, scores, router, None)
        gate_top2(core, "l3f_gate", scores, E, gates, True)
        small_rows(core, "l3f_tokens", lambda dve, call: nc.vector.tensor_tensor(x[:], x[:], xn[:], ALU.add))
        expert_layer(core, "l3f_experts", x_t, gates, E, 2, w["L3_ffn_w1"], w["L3_ffn_b1"], w["L3_ffn_w2"], w["L3_ffn_b2"])


def clear_semaphores(core):
    nc = core.nc
    with nc.Block() as block:
        @block.gpsimd
        def _(pool):
            left = sorted(nc.released_uncleared_semaphores)
            for number in left:
                if number - 1 not in left:
                    first = number
                if number + 1 not in left:
                    pool.sem_clear(range(first, number + 1))


def program(nc, w, out):
    with ExitStack() as ctx:
        core = Core(nc, ctx)
        constants(core)
        by_src, by_dst = ((core.keep(f"{n}_records", [128, ET_MAIN + ET_PAD, 4]), core.keep(f"{n}_edge_group", [1, ET_MAIN + ET_PAD], I32))
                          for n in ("by_src", "by_dst"))
        group_edges(core, "group_src", E_MAIN, ET_MAIN, w["src"], w["dst"], [w["edge_weight"], w["edge_weight_n2"]], *by_src)
        group_edges(core, "group_dst", E_MAIN, ET_MAIN, w["dst"], w["src"], [], *by_dst)
        core.x = core.keep("x", [TP, NT, D])
        x_t = core.keep("x_t", [128, KC, N])
        small_rows(core, "load_x", lambda dve, call: None, (), [(core.x[:], across(w["x"]))])
        clear_semaphores(core)
        layer0(core, w, x_t, by_src)
        clear_semaphores(core)
        layer0_ffn(core, w, x_t)
        clear_semaphores(core)
        layer1(core, w, x_t, by_dst)
        clear_semaphores(core)
        layer1_ffn(core, w, x_t)
        with Scope(core, "normed2") as sb:
            xn = sb("rows", [TP, NT, D])
            clear_semaphores(core)
            layer2(core, w, x_t, by_dst, xn)
            clear_semaphores(core)
            layer2_mix(core, w, x_t, xn)
        clear_semaphores(core)
        layer2_ffn(core, w, x_t)
        clear_semaphores(core)
        layer3(core, w, x_t, by_src, by_dst)
        with Scope(core, "normed3") as sb:
            clear_semaphores(core)
            layer3_ffn(core, w, x_t, sb("rows", [TP, NT, D]))
        small_rows(core, "store_x", lambda dve, call: None, [(across(out), core.x[:])])


TURNED = ("L1_mix_Wq", "L1_mix_Wk", "L1_mix_Wv", "L1_mix_Wfc", "L1_ffn_router_w", "L2_mix_Wx", "L2_mix_Wq", "L2_mix_Wk",
          "L2_mix_Wv", "L2_mix_Wo", "L2_mix_W1", "L2_mix_W2", "L3_mix_Wq", "L3_mix_Wkv", "L3_mix_Wproj", "L3_ffn_router_w")
BY_CHANNEL = ("L0_mix_bq", "L0_ffn_gamma", "L0_ffn_beta", "L0_ffn_b1", "L1_mix_bq", "L1_ffn_b1", "L2_mix_ln1_w", "L2_mix_ln1_b",
              "L2_mix_ln2_w", "L2_mix_ln2_b", "L2_mix_bx", "L2_mix_b1", "L2_ffn_b1", "L3_ffn_b1")


def laid_out(name, array):
    if name in TURNED:
        return array.T
    if name in BY_CHANNEL:
        return array.reshape(-1, 128).T
    return array


def kernel(**inputs):
    import numpy as np
    import concourse.bacc as bacc
    from concourse.bass_utils import run_bass_kernel_spmd

    nc = bacc.Bacc("TRN2", target_bir_lowering=False, num_devices=1)
    arrays, w = {}, {}
    for name, value in inputs.items():
        array = np.ascontiguousarray(laid_out(name, np.asarray(value)))
        arrays[f"in_{name}"] = array
        w[name] = nc.dram_tensor(f"in_{name}", array.shape, mybir.dt.from_np(array.dtype), kind="ExternalInput").ap()
    out = nc.dram_tensor("out", (N, D), F32, kind="ExternalOutput").ap()
    program(nc, w, out)
    result = run_bass_kernel_spmd(nc, [arrays], core_ids=[0])
    return result.results[0]["out"]
```

```python
from contextlib import ExitStack

import concourse.bass as bass
from concourse import mybir

F32 = mybir.dt.float32
BF16 = mybir.dt.bfloat16
I32 = mybir.dt.int32
U32 = mybir.dt.uint32
ALU = mybir.AluOpType
ACT = mybir.ActivationFunctionType
AX_X = mybir.AxisListType.X

N = 3125
D = 256
TP = 125
NT = N // TP
KC = D // 128
U = 5
E_MAIN = 50000
E_GAT = 32768
EDGES = 128
NULL_KEY = 127.0
FAR = 1.0e30
EPS = 1e-5


def edge_tiles(edges):
    return (edges + NT * (EDGES - 1)) // EDGES


ET_MAIN = -(-edge_tiles(E_MAIN) // 16) * 16
ET_GAT = -(-edge_tiles(E_GAT) // 20) * 20
ET_PAD = 16


def run_slots(eng, count, unroll, phases):
    def slot(first, j):
        for lag, phase in phases:
            piece = first + (j - lag)
            if isinstance(piece, int) and not 0 <= piece < count:
                continue
            phase(piece, (j - lag) % unroll)

    assert count % unroll == 0 and all(lag <= unroll for lag, _ in phases)
    peeled = 2 if max(lag for lag, _ in phases) > 0 else 1
    for i in range(peeled * unroll):
        slot(i - i % unroll, i % unroll)
    with eng.Fori(peeled, count // unroll) as r:
        for j in range(unroll):
            slot(r * unroll, j)
    for j in range(max(lag for lag, _ in phases)):
        slot(count, j)


class GroupNumbers:

    def __init__(self, nc, edge_group, engine, K, lag, batches=2):
        self.nc, self.edge_group, self.engine, self.K, self.lag, self.batches = nc, edge_group, engine, K, lag, batches
        self.loaded = []

    def of_batch(self, q, j):
        if (j + self.lag) % self.batches == 0 or not self.loaded:
            _, values = self.nc.values_load_multi_w_load_instructions(
                self.edge_group[0:1, bass.ds(q * self.K, self.batches * self.K)], [self.engine], min_val=0, max_val=NT - 1)
            self.loaded = list(values)
        groups, self.loaded = self.loaded[:self.K], self.loaded[self.K:]
        return groups


def at(tile, count=TP):
    return bass.ds(tile * count, count)


class Core:

    def __init__(self, nc, ctx):
        self.nc, self.ctx = nc, ctx

    def keep(self, name, shape, dt=F32):
        return self.ctx.enter_context(self.nc.sbuf_tensor(name, shape, dt))

    def software_dma_semaphore(self, name):
        return self.ctx.enter_context(self.nc.semaphore(name))


def constants(core):
    nc = core.nc
    core.col_i = core.keep("col_i", [128, 128], I32)
    core.row_i = core.keep("row_i", [128, 1], I32)
    core.col = core.keep("col", [128, 128])
    core.row = core.keep("row", [128, 1])
    core.ident = core.keep("ident", [128, 128])
    core.ones = core.keep("ones", [128, 128])
    core.zeros = core.keep("zeros", [128, 128])
    core.wide_zeros = core.keep("wide_zeros", [128, D + 4])
    core.same_head = core.keep("same_head", [128, 128])
    core.head_of = core.keep("head_of", [128, 4])
    row_head = core.keep("row_head", [128, 1])
    col_head = core.keep("col_head", [128, 128])
    with nc.semaphore("numbers_written") as numbers_written, nc.Block() as block:
        @block.gpsimd
        def _(pool):
            nc.gpsimd.iota(core.col_i[:], [[1, 128]], base=0, channel_multiplier=0).then_inc(numbers_written, 1)
            nc.gpsimd.iota(core.row_i[:], [[0, 1]], base=0, channel_multiplier=1).then_inc(numbers_written, 1)

        @block.vector
        def _(dve):
            nc.vector.memset(core.ones[:], 1.0)
            nc.vector.memset(core.zeros[:], 0.0)
            nc.vector.memset(core.wide_zeros[:], 0.0)
            dve.wait_ge(numbers_written, 2)
            nc.vector.tensor_copy(core.col[:], core.col_i[:])
            nc.vector.tensor_copy(core.row[:], core.row_i[:])
            dve.drain()
            nc.vector.tensor_scalar(core.ident[:], core.col[:], core.row[:, 0:1], None, ALU.is_equal)
            nc.vector.tensor_scalar(row_head[:], core.row[:], 32.0, None, ALU.is_ge)
            nc.vector.tensor_scalar(col_head[:], core.col[:], 32.0, None, ALU.is_ge)
            for first in (64.0, 96.0):
                dve.drain()
                nc.vector.scalar_tensor_tensor(row_head[:], core.row[:], first, row_head[:], ALU.is_ge, ALU.add)
                nc.vector.scalar_tensor_tensor(col_head[:], core.col[:], first, col_head[:], ALU.is_ge, ALU.add)
            dve.drain()
            nc.vector.tensor_scalar(core.same_head[:], col_head[:], row_head[:, 0:1], None, ALU.is_equal)
            nc.vector.tensor_scalar(core.head_of[:], core.col[:, 0:4], row_head[:, 0:1], None, ALU.is_equal)


class EdgeGroups:

    K, B = 8, 2

    def __init__(self, core, name, edges, et, keep, records, edge_group):
        nc = core.nc
        self.core, self.name, self.edges, self.et, self.records, self.edge_group = core, name, edges, et, records, edge_group
        P = self.P = 125 if edges % 125 == 0 else 128
        T = self.T = edges // P
        self.rounds, self.done = T // (self.K * self.B), 0
        self.record_slots = nc.dram_tensor(f"{name}_record_slots", (128 * et, 4), F32).ap()
        self.pos_i, self.rec = keep(f"{name}_pos_i", [P, T], I32), keep(f"{name}_rec", [P, T, 4])
        self.slot_s, self.rec_s = core.keep(f"{name}_slot_s", [P, self.B, self.K], I32), core.keep(f"{name}_rec_s", [P, self.B, self.K, 4])
        self.staged = [core.software_dma_semaphore(f"{name}_staged{b}") for b in range(self.B)]
        self.scattered = [core.software_dma_semaphore(f"{name}_scattered{b}") for b in range(self.B)]
        self.records_landed = core.software_dma_semaphore(f"{name}_records_landed")

    def sync(self, sp, rounds):
        K, B = self.K, self.B

        def stage(r, b):
            t = (r * B + b) * K
            sp.dma_start(self.slot_s[:, b, :], self.pos_i[:, bass.ds(t, K)]).then_inc(self.staged[b], 16)
            sp.dma_start(self.rec_s[:, b, :, :], self.rec[:, bass.ds(t, K), :]).then_inc(self.staged[b], 16)

        first = self.done
        if first == 0:
            for b in range(B):
                stage(0, b)
        with sp.Fori(max(first, 1), first + rounds) as r:
            for b in range(B):
                sp.wait_ge(self.scattered[b], r * (16 * K))
                stage(r, b)
        if first + rounds == self.rounds:
            for b in range(B):
                sp.wait_ge(self.scattered[b], 16 * K * self.rounds)
            sp.dma_start(self.records[:, 0:self.et, :], self.record_slots.rearrange("(p t) w -> p t w", p=128)
                         ).then_inc(self.records_landed, 16)
            sp.wait_ge(self.records_landed, 16)

    def gpsimd(self, pool, rounds, batch_begun):
        with pool.Fori(self.done, self.done + rounds) as r:
            for b in range(self.B):
                pool.wait_ge(self.staged[b], r * 32 + 32)
                pool.sem_inc(batch_begun, 1)
                for k in range(self.K):
                    self.core.nc.gpsimd.indirect_dma_start(
                        out=self.record_slots, out_offset=bass.IndirectOffsetOnAxis(ap=self.slot_s[:, b, k:k + 1].bitcast(U32), axis=0),
                        in_=self.rec_s[:, b, k, :], in_offset=None).then_inc(self.scattered[b], 16)

    def prepare(self, key, other, weights, beside=None):
        core, name, edges, et, records, edge_group = self.core, self.name, self.edges, self.et, self.records, self.edge_group
        nc = core.nc
        P, T = self.P, self.T
        G = NT
        pos_i, rec, record_slots = self.pos_i, self.rec, self.record_slots
        CH = 16
        with ExitStack() as c:
            def sb(n, shape, dt=F32):
                return c.enter_context(nc.sbuf_tensor(f"{name}_{n}", shape, dt))

            def sem(n):
                return c.enter_context(nc.semaphore(f"{name}_{n}"))

            key_i = sb("key_i", [P, T], I32)
            other_i = sb("other_i", [P, T], I32)
            key_f = sb("key_f", [P, T])
            weight_s = sb("weight_s", [P, 2, T])
            high = sb("high", [P, T])
            bound = sb("bound", [P, G + 1])
            above = sb("above", [P, T, G + 1])
            member = sb("member", [P, T, G], BF16)
            rank = sb("rank", [P, T, G])
            before = sb("before", [P, T + 1, G])
            upper = sb("upper", [P, P], BF16)
            ones_b = sb("ones_b", [P, P], BF16)
            zero_row = sb("zero_row", [P, T])
            count_i = sb("count_i", [P, G], I32)
            tiles_f = sb("tiles_f", [P, G])
            tile_end = sb("tile_end", [P, G])
            slot_start = sb("slot_start", [P, G])
            pos, part_i, tile_i, tile_f = key_f, key_i, other_i, high
            null = records[:, 0:et, :]
            number_i = sb("number_i", [1, et + ET_PAD], I32)
            number = weight_s[0:1, :, :].rearrange("p w t -> p (w t)")[:, 0:et + ET_PAD]
            group_f = sb("group_f", [1, et + ET_PAD])
            counts = c.enter_context(nc.psum_tensor(f"{name}_counts", [P, 2, 2, 512], F32))
            lists_landed = sem("lists_landed")
            nulls_made = sem("nulls_made")
            nulls_stored = sem("nulls_stored")
            numbers_made = sem("numbers_made")
            members_made = sem("members_made")
            counts_made = sem("counts_made")
            counts_read = sem("counts_read")
            block = c.enter_context(nc.Block())
            CN = T // CH

            @block.sync
            def _(sp):
                sp.dma_start(key_i[:], key.rearrange("(p t) -> p t", p=P)).then_inc(lists_landed, 16)
                sp.dma_start(other_i[:], other.rearrange("(p t) -> p t", p=P)).then_inc(lists_landed, 16)
                for w, weight in enumerate(weights):
                    sp.dma_start(weight_s[:, w, :], weight.rearrange("(p t) -> p t", p=P)).then_inc(lists_landed, 16)
                sp.wait_ge(nulls_made, 1)
                sp.dma_start(record_slots.rearrange("(p t) w -> p t w", p=128), null).then_inc(nulls_stored, 16)
                sp.wait_ge(nulls_stored, 16)
                if beside is not None:
                    beside.sync(sp)

            @block.gpsimd
            def _(pool):
                nc.gpsimd.iota(number_i[:], [[1, et + ET_PAD]], base=0, channel_multiplier=0).then_inc(numbers_made, 1)
                if beside is not None:
                    beside.gpsimd(pool)

            @block.tensor
            def _(pe):
                pe.wait_ge(members_made, 1)
                for n in range(CN):
                    if n >= 2:
                        pe.wait_ge(counts_read, n - 1)
                    rhs = member[:, n * CH:(n + 1) * CH, :]
                    nc.tensor.matmul(counts[:, n % 2, 0, 0:CH * G], upper[:], rhs, start=True, stop=True)
                    nc.tensor.matmul(counts[:, n % 2, 1, 0:CH * G], ones_b[:], rhs, start=True, stop=True).then_inc(counts_made, 1)

            @block.scalar
            def _(act):
                for n in range(CN):
                    act.wait_ge(counts_made, n + 1)
                    nc.scalar.copy(rank[:, n * CH:(n + 1) * CH, :], counts[:, n % 2, 0, 0:CH * G])
                    nc.scalar.copy(above[:, n * CH:(n + 1) * CH, 0:G], counts[:, n % 2, 1, 0:CH * G]).then_inc(counts_read, 1)

            @block.vector
            def _(dve):
                v = nc.vector
                v.memset(null, 0.0)
                v.memset(zero_row[:], 0.0)
                v.memset(ones_b[:], 1.0)
                v.memset(before[:, 0, :], 0.0)
                v.memset(records[:, et:et + ET_PAD, :], 0.0)
                if len(weights) < 2:
                    v.memset(rec[:, :, 2 + len(weights):4], 0.0)
                v.tensor_scalar(upper[:], core.col[0:P, 0:P], core.row[0:P, 0:1], None, ALU.is_gt)
                v.tensor_scalar(bound[:], core.col[0:P, 0:G + 1], float(TP), None, ALU.mult)
                dve.drain()
                v.memset(null[:, :, 1:2], NULL_KEY)
                v.memset(records[:, et:et + ET_PAD, 1:2], NULL_KEY)
                dve.drain().then_inc(nulls_made, 1)
                dve.wait_ge(lists_landed, 16 * (2 + len(weights)))
                v.tensor_copy(key_f[:], key_i[:])
                v.tensor_copy(rec[:, :, 0], other_i[:])
                for w in range(len(weights)):
                    v.tensor_copy(rec[:, :, 2 + w], weight_s[:, w, :])
                dve.drain()
                v.tensor_tensor(above[:], key_f[:].unsqueeze(2).broadcast_to([P, T, G + 1]),
                                bound[:].unsqueeze(1).broadcast_to([P, T, G + 1]), ALU.is_ge)
                dve.drain()
                v.tensor_tensor(member[:], above[:, :, 0:G], above[:, :, 1:G + 1], ALU.subtract)
                v.tensor_reduce(high[:], above[:, :, 1:G], AX_X, ALU.add)
                dve.drain().then_inc(members_made, 1)
                v.scalar_tensor_tensor(rec[:, :, 1], high[:], -float(TP), key_f[:], ALU.mult, ALU.add)
                dve.wait_ge(counts_read, CN)
                for g in range(G):
                    v.tensor_tensor_scan(before[:, 1:T + 1, g], above[:, 0:T, g], zero_row[:], 0.0, ALU.add, ALU.add)
                dve.drain()
                v.tensor_scalar(count_i[:], before[:, T, :], float(EDGES - 1), None, ALU.add)
                dve.drain()
                v.tensor_scalar(count_i[:], count_i[:], 7, None, ALU.arith_shift_right)
                dve.drain()
                v.tensor_copy(tiles_f[:], count_i[:])
                dve.drain()
                v.tensor_tensor_scan(tile_end[:], tiles_f[:], zero_row[:, 0:G], 0.0, ALU.add, ALU.add)
                v.tensor_tensor(rank[:], rank[:], before[:, 0:T, :], ALU.add)
                dve.drain()
                v.tensor_tensor(slot_start[:], tile_end[:], tiles_f[:], ALU.subtract)
                dve.drain()
                v.tensor_scalar(slot_start[:], slot_start[:], float(EDGES), None, ALU.mult)
                dve.drain()
                v.tensor_tensor(rank[:], rank[:], slot_start[:].unsqueeze(1).broadcast_to([P, T, G]), ALU.add)
                dve.drain()
                v.tensor_tensor(rank[:], rank[:], member[:], ALU.mult)
                dve.drain()
                v.tensor_reduce(pos[:], rank[:], AX_X, ALU.add)
                dve.drain()
                v.tensor_copy(pos_i[:], pos[:])
                dve.drain()
                v.tensor_scalar(part_i[:], pos_i[:], EDGES - 1, None, ALU.bitwise_and)
                v.tensor_scalar(tile_i[:], pos_i[:], 7, None, ALU.arith_shift_right)
                dve.drain()
                v.tensor_copy(pos[:], part_i[:])
                v.tensor_copy(tile_f[:], tile_i[:])
                dve.drain()
                v.scalar_tensor_tensor(pos_i[:], pos[:], float(et), tile_f[:], ALU.mult, ALU.add)
                dve.wait_ge(numbers_made, 1)
                v.tensor_copy(number, number_i[:])
                v.memset(group_f[:], 0.0)
                dve.drain()
                for g in range(G - 1):
                    v.scalar_tensor_tensor(group_f[:], number, tile_end[0:1, g:g + 1], group_f[:], ALU.is_ge, ALU.add)
                    dve.drain()
                v.tensor_copy(edge_group[:], group_f[:])
        if beside is not None:
            beside.finish()


class Scatters:

    def __init__(self, groups, rounds):
        self.groups, self.rounds = groups, min(rounds, groups.rounds - groups.done)
        self.batch_begun = groups.core.ctx.enter_context(groups.core.nc.semaphore(f"{groups.name}_batch_begun{groups.done}"))

    def sync(self, sp):
        self.groups.sync(sp, self.rounds)

    def gpsimd(self, pool):
        self.groups.gpsimd(pool, self.rounds, self.batch_begun)

    def finish(self):
        self.groups.done += self.rounds


def sum_edges(core, name, table, records, edge_group, sums, words=(None,), counted=False, beside=None):
    nc = core.nc
    K, NB, NP = 4, 4 if words != (None,) else 8, 2
    Q = ET_MAIN // K
    weighted = words != (None,)
    nw = len(words)
    W = D + 1 if counted else D * nw
    assert not (counted and weighted)
    with ExitStack() as c:
        def sb(n, shape, dt=F32):
            return c.enter_context(nc.sbuf_tensor(f"{name}_{n}", shape, dt))

        def sem(n):
            return c.enter_context(nc.semaphore(f"{name}_{n}"))

        index = sb("index", [128, NB, K], I32)
        rows = sb("rows", [128, NB, K, W if counted else D])
        if weighted:
            scaled = sb("scaled", [128, NP, K, W])
        pick = sb("pick", [128, 4, K, TP])
        psum = c.enter_context(nc.psum_tensor(f"{name}_psum", [128, NP, K, D if W == D else 512], F32))
        indexed, batch_begun, picked, rows_scaled, summed, added = (
            sem(n) for n in ("indexed", "batch_begun", "picked", "rows_scaled", "summed", "added"))
        gathered = [core.software_dma_semaphore(f"{name}_gathered{b}") for b in range(NB)]
        rows_used = rows_scaled if weighted else summed
        if beside is not None:
            beside.allocate(c)
        block = c.enter_context(nc.Block())

        @block.gpsimd
        def _(pool):
            def gather(q, j):
                pool.wait_ge(indexed, q + 1)
                pool.sem_inc(batch_begun, 1)
                if not (isinstance(q, int) and q < NB):
                    pool.wait_ge(rows_used, q - (NB - 1))
                    pool.sem_inc(batch_begun, 1)
                for k in range(K):
                    nc.gpsimd.indirect_dma_start(
                        out=rows[:, j, k, 0:D], out_offset=None, in_=table,
                        in_offset=bass.IndirectOffsetOnAxis(ap=index[:, j, k:k + 1].bitcast(U32), axis=0),
                    ).then_inc(gathered[j], 16)

            run_slots(pool, Q, NB, [(0, gather)])

        @block.scalar
        def _(act):
            def number(q, j):
                if not (isinstance(q, int) and q < NB):
                    act.wait_ge(gathered[j], (q - j) * (16 * K // NB))
                nc.scalar.copy(index[:, j, :], records[:, bass.ds(q * K, K), 0]).then_inc(indexed, 1)

            def scale(q, j):
                act.wait_ge(gathered[j], (q - j) * (16 * K // NB) + 16 * K)
                reuse(act, summed, q, j, NP, NB)
                for k in range(K):
                    for i, word in enumerate(words):
                        ins = nc.scalar.activation(scaled[:, j % NP, k, i * D:(i + 1) * D], rows[:, j, k, :], ACT.Copy,
                                                   scale=records[:, bass.ds(q * K + k, 1), word])
                ins.then_inc(rows_scaled, 1)

            run_slots(act, Q, NB, [(0, number)] + ([(2, scale)] if weighted else []))

        @block.tensor
        def _(pe):
            def add_up(q, j):
                pe.wait_ge(picked, q + 1)
                if weighted:
                    pe.wait_ge(rows_scaled, q + 1)
                else:
                    pe.wait_ge(gathered[j], (q - j) * (16 * K // NB) + 16 * K)
                reuse(pe, added, q, j, NP, NB)
                for k in range(K):
                    source = scaled[:, j % NP, k, :] if weighted else rows[:, j, k, :]
                    ins = nc.tensor.matmul(psum[0:TP, j % NP, k, 0:W], pick[:, j % 4, k, :], source, start=True, stop=True)
                ins.then_inc(summed, 1)

            run_slots(pe, Q, NB, [(0, add_up)] + ([] if beside is None else beside.tensor_phases(pe)))

        @block.vector
        def _(dve):
            v = nc.vector
            v.memset(sums[:], 0.0)
            if counted:
                v.memset(rows[:, :, :, D:D + 1], 1.0)
            dve.drain()

            def choose(q, j):
                reuse(dve, summed, q, j, 4, NB)
                for k in range(K):
                    ins = v.tensor_scalar(pick[:, j % 4, k, :], core.col[:, 0:TP], records[:, bass.ds(q * K + k, 1), 1], None, ALU.is_equal)
                ins.then_inc(picked, 1)

            numbers = GroupNumbers(nc, edge_group, mybir.EngineType.DVE, K, 1)

            def collect(q, j):
                groups = numbers.of_batch(q, j)
                dve.wait_ge(summed, q + 1)
                for k in range(K):
                    total = sums[:, bass.ds(groups[k], 1), :]
                    v.tensor_tensor(total, total, psum[0:TP, j % NP, k, 0:W].unsqueeze(1), ALU.add)
                    last = dve.drain()
                last.then_inc(added, 1)

            run_slots(dve, Q, NB, [(0, choose), (1, collect)] + ([] if beside is None else beside.vector_phases(dve)))


def reuse(eng, sem, piece, j, buffers, unroll=U, each=1):
    back = next(i for i in range(1, unroll + 1) if ((j - i) % unroll) % buffers == j % buffers)
    if not (isinstance(piece, int) and piece < back):
        eng.wait_ge(sem, (piece - (back - 1)) * each)


def layer_norm(core, name, src, normed=None, table=None, turned=None, twice=False, gain=None, shift=None):
    nc = core.nc
    with ExitStack() as c:
        def sb(n, shape, dt=F32):
            return c.enter_context(nc.sbuf_tensor(f"{name}_{n}", shape, dt))

        def sem(n):
            return c.enter_context(nc.semaphore(f"{name}_{n}"))

        stats = sb("stats", [TP, NT, 6])
        mean = sb("mean", [TP, NT])
        var = sb("var", [TP, NT])
        tmp = sb("tmp", [TP, NT])
        dev = sb("dev", [TP, NT])
        scale = sb("scale", [TP, NT])
        dev2 = sb("dev2", [TP, NT])
        out_s = sb("out_s", [TP, U, D])
        pt = c.enter_context(nc.psum_tensor(f"{name}_pt", [128, U, 512], F32))
        var_ready, dev_ready, var2_ready, dev2_ready = sem("var"), sem("dev"), sem("var2"), sem("dev2")
        rows_done, rows_turned, turned_moved, rows_kept = sem("rows_done"), sem("rows_turned"), sem("turned_moved"), sem("rows_kept")
        rows_stored = [sem(f"rows_stored{j}") for j in range(U)]
        block = c.enter_context(nc.Block())

        @block.vector
        def _(dve):
            v = nc.vector
            with dve.Fori(0, NT) as t:
                v.bn_stats(stats[:, bass.ds(t, 1), :], src[:, bass.ds(t, 1), :])
            dve.drain()
            v.tensor_tensor(mean[:], stats[:, :, 1], stats[:, :, 4], ALU.add)
            v.tensor_tensor(tmp[:], stats[:, :, 1], stats[:, :, 4], ALU.subtract)
            v.tensor_tensor(var[:], stats[:, :, 2], stats[:, :, 5], ALU.add)
            dve.drain()
            v.tensor_tensor(tmp[:], tmp[:], tmp[:], ALU.mult)
            v.tensor_scalar(var[:], var[:], 1.0 / D, EPS, ALU.mult, ALU.add)
            dve.drain()
            v.scalar_tensor_tensor(var[:], tmp[:], 0.25, var[:], ALU.mult, ALU.add)
            dve.drain().then_inc(var_ready, 1)
            dve.wait_ge(dev_ready, 1)
            v.reciprocal(scale[:], dev[:])
            dve.drain()
            if twice:
                v.tensor_tensor(tmp[:], scale[:], scale[:], ALU.mult)
                v.tensor_scalar(var[:], var[:], -EPS, None, ALU.add)
                dve.drain()
                v.tensor_tensor(var[:], var[:], tmp[:], ALU.mult)
                dve.drain()
                v.tensor_scalar(var[:], var[:], EPS, None, ALU.add)
                dve.drain().then_inc(var2_ready, 1)
                dve.wait_ge(dev2_ready, 1)
                v.reciprocal(tmp[:], dev2[:])
                dve.drain()
                v.tensor_tensor(scale[:], scale[:], tmp[:], ALU.mult)
                dve.drain()
            v.scalar_tensor_tensor(mean[:], mean[:], -0.5, scale[:], ALU.mult, ALU.mult)
            dve.drain()

            def norm(t, j):
                if turned is not None:
                    reuse(dve, rows_turned, t, j, U)
                if normed is not None:
                    reuse(dve, rows_kept, t, j, U)
                if table is not None and not (isinstance(t, int) and t < U):
                    dve.wait_ge(rows_stored[j], (t - j) * 16 // U if isinstance(t, int) else (t - j) // U * 16)
                v.tensor_scalar(out_s[:, j, :], src[:, bass.ds(t, 1), :], scale[:, bass.ds(t, 1)], mean[:, bass.ds(t, 1)],
                                ALU.mult, ALU.add).then_inc(rows_done, 1)

            run_slots(dve, NT, U, [(0, norm)])

        @block.tensor
        def _(pe):
            def turn(t, j):
                pe.wait_ge(rows_done, t + 1)
                reuse(pe, turned_moved, t, j, U)
                for h in range(KC):
                    ins = nc.tensor.transpose(pt[:, j, h * TP:(h + 1) * TP], out_s[:, j, h * 128:(h + 1) * 128], core.ident[0:TP, 0:TP])
                ins.then_inc(rows_turned, 1)

            if turned is not None:
                run_slots(pe, NT, U, [(0, turn)])

        @block.scalar
        def _(act):
            act.wait_ge(var_ready, 1)
            nc.scalar.activation(dev[:], var[:], ACT.Sqrt).then_inc(dev_ready, 1)
            if twice:
                act.wait_ge(var2_ready, 1)
                nc.scalar.activation(dev2[:], var[:], ACT.Sqrt).then_inc(dev2_ready, 1)

            def move(t, j):
                act.wait_ge(rows_turned, t + 1)
                for h in range(KC):
                    source = pt[:, j, h * TP:(h + 1) * TP]
                    if gain is None:
                        ins = nc.scalar.copy(turned[:, h, at(t)], source)
                    else:
                        ins = nc.scalar.activation(turned[:, h, at(t)], source, ACT.Identity,
                                                   bias=shift[:, h:h + 1], scale=gain[:, h:h + 1])
                ins.then_inc(turned_moved, 1)

            if turned is not None:
                run_slots(act, NT, U, [(0, move)])

        @block.gpsimd
        def _(pool):
            def keep(t, j):
                pool.wait_ge(rows_done, t + 1)
                nc.gpsimd.tensor_copy(normed[:, bass.ds(t, 1), :], out_s[:, j:j + 1, :]).then_inc(rows_kept, 1)

            if normed is not None:
                run_slots(pool, NT, U, [(0, keep)])

        @block.sync
        def _(sp):
            def store(t, j):
                sp.wait_ge(rows_done, t + 1)
                sp.dma_start(table[at(t), :], out_s[:, j, :]).then_inc(rows_stored[j], 16)

            if table is not None:
                run_slots(sp, NT, U, [(0, store)])
                for j in range(U):
                    sp.wait_ge(rows_stored[j], 16 * (NT // U))


def turn_rows(core, name, src, turned, scale=None):
    nc = core.nc
    with ExitStack() as c:
        def sem(n):
            return c.enter_context(nc.semaphore(f"{name}_{n}"))

        out_s = c.enter_context(nc.sbuf_tensor(f"{name}_out_s", [TP, U, D], F32))
        pt = c.enter_context(nc.psum_tensor(f"{name}_pt", [128, U, 512], F32))
        rows_done, rows_turned, turned_moved = sem("rows_done"), sem("rows_turned"), sem("turned_moved")
        block = c.enter_context(nc.Block())

        @block.vector
        def _(dve):
            def stage(t, j):
                reuse(dve, rows_turned, t, j, U)
                factor = 1.0 if scale is None else scale[:, bass.ds(t, 1)]
                nc.vector.tensor_scalar(out_s[:, j, :], src[:, bass.ds(t, 1), :], factor, None, ALU.mult).then_inc(rows_done, 1)

            run_slots(dve, NT, U, [(0, stage)])

        @block.tensor
        def _(pe):
            def turn(t, j):
                pe.wait_ge(rows_done, t + 1)
                reuse(pe, turned_moved, t, j, U)
                for h in range(KC):
                    ins = nc.tensor.transpose(pt[:, j, h * TP:(h + 1) * TP], out_s[:, j, h * 128:(h + 1) * 128], core.ident[0:TP, 0:TP])
                ins.then_inc(rows_turned, 1)

            run_slots(pe, NT, U, [(0, turn)])

        @block.scalar
        def _(act):
            def move(t, j):
                act.wait_ge(rows_turned, t + 1)
                nc.scalar.copy(turned[:, :, at(t)], pt[:, j, 0:2 * TP].rearrange("p (h n) -> p h n", h=KC)).then_inc(turned_moved, 1)

            run_slots(act, NT, U, [(0, move)])


def project(core, name, sources, jobs, width, evacuate, loads=(), before=None):
    nc = core.nc
    banks = -(-width // 512)
    with ExitStack() as c:
        def sem(n):
            return c.enter_context(nc.semaphore(f"{name}_{n}"))

        staged = c.enter_context(nc.sbuf_tensor(f"{name}_staged", [128, U, len(sources), KC, TP], F32))
        out = c.enter_context(nc.psum_tensor(f"{name}_out", [128, U if banks == 1 else 3, banks * 512], F32))
        buffers = U if banks == 1 else 3
        weights_landed, sources_staged, products_made, products_taken = sem("weights_landed"), sem("sources_staged"), sem("products_made"), sem("products_taken")
        block = c.enter_context(nc.Block())

        @block.sync
        def _(sp):
            for tile, dram in loads:
                sp.dma_start(tile, dram).then_inc(weights_landed, 16)

        @block.scalar
        def _(act):
            def stage(t, j):
                reuse(act, products_made, t, j, U)
                for s, source in enumerate(sources):
                    ins = nc.scalar.copy(staged[:, j, s, :, :], source[:, :, at(t)])
                ins.then_inc(sources_staged, 1)

            run_slots(act, NT, U, [(0, stage)])

        @block.tensor
        def _(pe):
            if loads:
                pe.wait_ge(weights_landed, 16 * len(loads))

            def multiply(t, j):
                pe.wait_ge(sources_staged, t + 1)
                reuse(pe, products_taken, t, j, buffers)
                for s, weight, col, opens, closes in jobs:
                    for h in range(KC):
                        ins = nc.tensor.matmul(out[0:TP, j % buffers, col:col + weight.shape[-1]], staged[:, j, s, h, :],
                                               weight[:, h, :], start=opens and h == 0, stop=closes and h == KC - 1)
                ins.then_inc(products_made, 1)

            run_slots(pe, NT, U, [(0, multiply)])

        @block.vector
        def _(dve):
            if loads:
                dve.wait_ge(weights_landed, 16 * len(loads))
            if before is not None:
                before(dve)
                dve.drain()

            def take(t, j):
                dve.wait_ge(products_made, t + 1)
                evacuate(dve, t, j, out[0:TP, j % buffers, 0:width])
                dve.drain().then_inc(products_taken, 1)

            run_slots(dve, NT, U, [(0, take)])


def halves(matrix):
    return matrix.rearrange("(h p) n -> p h n", p=128)


def spread(row, count=TP):
    return row.partition_broadcast(count)


def gate_top2(core, name, scores, experts, gates, of_softmax):
    nc = core.nc
    shape = [TP, NT, experts]
    with ExitStack() as c:
        def sb(n, shape, dt=F32):
            return c.enter_context(nc.sbuf_tensor(f"{name}_{n}", shape, dt))

        def sem(n):
            return c.enter_context(nc.semaphore(f"{name}_{n}"))

        best, second, index = sb("best", [TP, NT]), sb("second", [TP, NT]), sb("index", [TP, NT])
        lower, pick, rest = sb("lower", shape), sb("pick", shape), sb("rest", shape)
        less_max, exped = sem("less_max"), sem("exped")
        block = c.enter_context(nc.Block())
        number = core.col[0:TP, 0:experts].unsqueeze(1).broadcast_to(shape)

        @block.scalar
        def _(act):
            act.wait_ge(less_max, 1)
            target = scores if of_softmax else second
            nc.scalar.activation(target[:], target[:], ACT.Exp).then_inc(exped, 1)

        @block.vector
        def _(dve):
            v = nc.vector

            def first_max(values, best):
                v.tensor_reduce(best[:], values[:], AX_X, ALU.max)
                dve.drain()
                v.tensor_tensor(lower[:], values[:], best[:].unsqueeze(2).broadcast_to(shape), ALU.is_lt)
                dve.drain()
                v.scalar_tensor_tensor(lower[:], lower[:], 64.0, number, ALU.mult, ALU.add)
                dve.drain()
                v.tensor_reduce(index[:], lower[:], AX_X, ALU.min)
                dve.drain()
                v.tensor_tensor(pick[:], number, index[:].unsqueeze(2).broadcast_to(shape), ALU.is_equal)
                dve.drain()

            if of_softmax:
                v.tensor_reduce(best[:], scores[:], AX_X, ALU.max)
                dve.drain()
                v.tensor_tensor(scores[:], scores[:], best[:].unsqueeze(2).broadcast_to(shape), ALU.subtract)
                dve.drain().then_inc(less_max, 1)
                dve.wait_ge(exped, 1)
                v.tensor_reduce(second[:], scores[:], AX_X, ALU.add)
                dve.drain()
                v.reciprocal(best[:], second[:])
                dve.drain()
                v.tensor_tensor(scores[:], scores[:], best[:].unsqueeze(2).broadcast_to(shape), ALU.mult)
                dve.drain()
            first_max(scores, best)
            v.tensor_copy(gates[:], pick[:])
            v.scalar_tensor_tensor(rest[:], pick[:], -FAR, scores[:], ALU.mult, ALU.add)
            dve.drain()
            first_max(rest, second)
            if of_softmax:
                v.tensor_tensor(index[:], best[:], second[:], ALU.add)
                dve.drain()
                v.tensor_scalar(index[:], index[:], 1e-12, None, ALU.max)
            else:
                v.tensor_tensor(second[:], second[:], best[:], ALU.subtract)
                dve.drain()
                v.memset(best[:], 1.0)
                dve.drain().then_inc(less_max, 1)
                dve.wait_ge(exped, 1)
                v.tensor_tensor(index[:], best[:], second[:], ALU.add)
            dve.drain()
            v.reciprocal(index[:], index[:])
            dve.drain()
            v.tensor_tensor(best[:], best[:], index[:], ALU.mult)
            v.tensor_tensor(second[:], second[:], index[:], ALU.mult)
            dve.drain()
            v.tensor_tensor(gates[:], gates[:], best[:].unsqueeze(2).broadcast_to(shape), ALU.mult)
            v.tensor_tensor(pick[:], pick[:], second[:].unsqueeze(2).broadcast_to(shape), ALU.mult)
            dve.drain()
            v.tensor_tensor(gates[:], gates[:], pick[:], ALU.add)


def pick_expert(core, name, scores, experts, chosen):
    nc = core.nc
    shape = [TP, NT, experts]
    with ExitStack() as c:
        def sb(n, shape, dt=F32):
            return c.enter_context(nc.sbuf_tensor(f"{name}_{n}", shape, dt))

        def sem(n):
            return c.enter_context(nc.semaphore(f"{name}_{n}"))

        best, index = sb("best", [TP, NT]), sb("index", [TP, NT])
        lower, pick_s = sb("lower", shape), sb("pick_s", [TP, U, experts])
        pt = c.enter_context(nc.psum_tensor(f"{name}_pt", [experts, U, 512], F32))
        picked, turned, moved = sem("picked"), sem("turned"), sem("moved")
        block = c.enter_context(nc.Block())
        number = core.col[0:TP, 0:experts].unsqueeze(1).broadcast_to(shape)

        @block.vector
        def _(dve):
            v = nc.vector
            v.tensor_reduce(best[:], scores[:], AX_X, ALU.max)
            dve.drain()
            v.tensor_tensor(lower[:], scores[:], best[:].unsqueeze(2).broadcast_to(shape), ALU.is_lt)
            dve.drain()
            v.scalar_tensor_tensor(lower[:], lower[:], 64.0, number, ALU.mult, ALU.add)
            dve.drain()
            v.tensor_reduce(index[:], lower[:], AX_X, ALU.min)
            dve.drain()

            def pick(t, j):
                reuse(dve, turned, t, j, U)
                v.tensor_scalar(pick_s[:, j, :], core.col[0:TP, 0:experts], index[:, bass.ds(t, 1)], None,
                                ALU.is_equal).then_inc(picked, 1)

            run_slots(dve, NT, U, [(0, pick)])

        @block.tensor
        def _(pe):
            def turn(t, j):
                pe.wait_ge(picked, t + 1)
                reuse(pe, moved, t, j, U)
                nc.tensor.transpose(pt[:, j, 0:TP], pick_s[:, j, :], core.ident[0:TP, 0:TP]).then_inc(turned, 1)

            run_slots(pe, NT, U, [(0, turn)])

        @block.scalar
        def _(act):
            def move(t, j):
                act.wait_ge(turned, t + 1)
                nc.scalar.copy(chosen[:, at(t)], pt[:, j, 0:TP]).then_inc(moved, 1)

            run_slots(act, NT, U, [(0, move)])


def feed_forward(core, name, x_t, units, chunks, load_weights, b1, function, w1, w2, take, gates=None, b2=None,
                 chosen=None, loads=(), beside=None):
    nc = core.nc
    HID = chunks * 128
    with ExitStack() as c:
        def sb(n, shape, dt=F32):
            return c.enter_context(nc.sbuf_tensor(f"{name}_{n}", shape, dt))

        def sem(n):
            return c.enter_context(nc.semaphore(f"{name}_{n}"))

        hidden_s = sb("hidden_s", [128, 2, chunks, TP])
        hidden_p = c.enter_context(nc.psum_tensor(f"{name}_hidden_p", [128, 2, 512], F32))
        out_p = c.enter_context(nc.psum_tensor(f"{name}_out_p", [128, 2, 512], F32))
        if chosen is not None:
            experts = chosen.shape[0]
            expert_i = sb("expert_i", [experts, units * HID], I32)
            push = sb("push", [experts, units * HID])
            less_one = sb("less_one", [experts, N])
            chosen_s = sb("chosen_s", [experts, TP])
        numbers_made, push_made, chosen_staged = sem("numbers_made"), sem("push_made"), sem("chosen_staged")
        weights_landed = [sem(f"weights_landed{e}") for e in range(units)]
        extras_landed = sem("extras_landed")
        hidden_made, hidden_done, out_made, out_taken = sem("hidden_made"), sem("hidden_done"), sem("out_made"), sem("out_taken")
        block = c.enter_context(nc.Block())

        @block.sync
        def _(sp):
            for tile, dram in loads:
                sp.dma_start(tile, dram).then_inc(extras_landed, 16)
            for e in range(units):
                for tile, dram in load_weights(e):
                    sp.dma_start(tile, dram).then_inc(weights_landed[e], 16)
            if beside is not None:
                beside.sync(sp)

        @block.gpsimd
        def _(pool):
            if chosen is not None:
                nc.gpsimd.iota(expert_i[:], [[1, experts], [0, units * HID // experts]], base=0,
                               channel_multiplier=0).then_inc(numbers_made, 1)
            if beside is not None:
                beside.gpsimd(pool)

        @block.tensor
        def _(pe):
            if loads:
                pe.wait_ge(extras_landed, 16 * len(loads))
            if chosen is not None:
                pe.wait_ge(push_made, 1)

            def hidden(t, e):
                n = t * units + e
                if isinstance(t, int) and t == 0:
                    pe.wait_ge(weights_landed[e], 16 * len(load_weights(e)))
                if not (isinstance(n, int) and n < 2):
                    pe.wait_ge(hidden_done, n - 1)
                for i in range(chunks):
                    col = (e * chunks + i) * 128
                    out = hidden_p[:, e % 2, i * TP:(i + 1) * TP]
                    for h in range(KC):
                        ins = nc.tensor.matmul(out, w1[:, h, col:col + 128], x_t[:, h, at(t)],
                                               start=h == 0, stop=h == KC - 1 and chosen is None)
                    if chosen is not None:
                        ins = nc.tensor.matmul(out, push[:, col:col + 128], less_one[:, at(t)], start=False, stop=True)
                ins.then_inc(hidden_made, 1)

            def output(t, e):
                n = t * units + e
                pe.wait_ge(hidden_done, n + 1)
                if gates is not None:
                    if not (isinstance(n, int) and n < 2):
                        pe.wait_ge(out_taken, n - 1)
                    out = out_p[0:TP, e % 2, 0:D]
                    opens, closes = True, True
                else:
                    if e == 0 and not (isinstance(t, int) and t == 0):
                        pe.wait_ge(out_taken, t)
                    out = out_p[0:TP, 0, 0:D]
                    opens, closes = e == 0, e == units - 1
                    if e == 0 and chosen is not None:
                        pe.wait_ge(chosen_staged, t + 1)
                        nc.tensor.matmul(out, chosen_s[:], b2[:], start=True, stop=False)
                        opens = False
                for i in range(chunks):
                    ins = nc.tensor.matmul(out, hidden_s[:, e % 2, i, :], w2[:, e * chunks + i, :],
                                           start=opens and i == 0, stop=closes and i == chunks - 1)
                ins.then_inc(out_made, 1)

            def tile(t):
                for e in range(units):
                    hidden(t, e)
                    if e:
                        output(t, e - 1)
                    elif not (isinstance(t, int) and t == 0):
                        output(t - 1, units - 1)

            tile(0)
            with pe.Fori(1, NT) as t:
                tile(t)
            output(NT - 1, units - 1)

        @block.scalar
        def _(act):
            if loads:
                act.wait_ge(extras_landed, 16 * len(loads))

            def tile(t):
                if chosen is not None:
                    if not (isinstance(t, int) and t == 0):
                        act.wait_ge(out_made, (t - 1) * units + 1)
                    nc.scalar.copy(chosen_s[:], chosen[:, at(t)]).then_inc(chosen_staged, 1)
                for e in range(units):
                    n = t * units + e
                    act.wait_ge(hidden_made, n + 1)
                    if not (isinstance(n, int) and n < 2):
                        act.wait_ge(out_made, n - 1)
                    for i in range(chunks):
                        ins = nc.scalar.activation(hidden_s[:, e % 2, i, :], hidden_p[:, e % 2, i * TP:(i + 1) * TP],
                                                   function, bias=b1[:, e * chunks + i:e * chunks + i + 1])
                    ins.then_inc(hidden_done, 1)

            tile(0)
            with act.Fori(1, NT) as t:
                tile(t)

        @block.vector
        def _(dve):
            v = nc.vector
            if chosen is not None:
                dve.wait_ge(numbers_made, 1)
                v.tensor_scalar(push[:], expert_i[:], core.row[0:experts, 0:1], FAR, ALU.is_equal, ALU.mult)
                v.tensor_scalar(less_one[:], chosen[:], -1.0, None, ALU.add)
                dve.drain().then_inc(push_made, 1)
            if loads:
                dve.wait_ge(extras_landed, 16 * len(loads))

            def tile(t):
                mine = core.x[:, bass.ds(t, 1), :]
                if gates is None:
                    dve.wait_ge(out_made, t * units + units)
                    take(dve, t, out_p[0:TP, 0, 0:D])
                    dve.drain().then_inc(out_taken, 1)
                    return
                for e in range(units):
                    gate = gates[:, bass.ds(t, 1), e]
                    v.scalar_tensor_tensor(mine, b2[:, e:e + 1, :], gate, mine, ALU.mult, ALU.add)
                    dve.drain()
                    dve.wait_ge(out_made, t * units + e + 1)
                    v.scalar_tensor_tensor(mine, out_p[0:TP, e % 2, 0:D].unsqueeze(1), gate, mine, ALU.mult, ALU.add)
                    dve.drain().then_inc(out_taken, 1)

            tile(0)
            with dve.Fori(1, NT) as t:
                tile(t)

    if beside is not None:
        beside.finish()


def attention(core, name, x_t, wq, wkv, wo, bq, bkv, bo, loads, feature, norm, beside=None):
    nc = core.nc
    G = 128 + 4
    with ExitStack() as c:
        mixing = c.enter_context(nc.sbuf_tensor(f"{name}_mixing", [128, KC, G], F32))
        with ExitStack() as c:
            def sb(n, shape, dt=F32):
                return c.enter_context(nc.sbuf_tensor(f"{name}_{n}", shape, dt))

            def sem(n):
                return c.enter_context(nc.semaphore(f"{name}_{n}"))

            staged = sb("staged", [128, U, KC, TP])
            kv_s = sb("kv_s", [TP, U, 2 * D + 1])
            below_s = sb("below_s", [TP, U, D])
            exp_s = sb("exp_s", [TP, U, D])
            kv_p = c.enter_context(nc.psum_tensor(f"{name}_kv_p", [128, U, 512], F32))
            total_p = c.enter_context(nc.psum_tensor(f"{name}_total_p", [128, KC, 512], F32))
            landed, sources_staged, kv_made, kv_taken = sem("landed"), sem("staged"), sem("kv_made"), sem("kv_taken")
            below_made, exp_made, keys_done, keys_used, all_added = sem("below_made"), sem("exp_made"), sem("keys_done"), sem("keys_used"), sem("all_added")
            block = c.enter_context(nc.Block())

            @block.sync
            def _(sp):
                for tile, dram in loads:
                    sp.dma_start(tile, dram).then_inc(landed, 16)
                if beside is not None:
                    beside[0].sync(sp)

            if beside is not None:
                @block.gpsimd
                def _(pool):
                    beside[0].gpsimd(pool)

            @block.tensor
            def _(pe):
                pe.wait_ge(landed, 16 * len(loads))
                for h in range(KC):
                    nc.tensor.matmul(total_p[:, h, 0:D + 1], core.zeros[:], core.wide_zeros[:, 0:D + 1], start=True, stop=False,
                                     skip_group_check=True)

                def products(t, j):
                    pe.wait_ge(sources_staged, t + 1)
                    reuse(pe, kv_taken, t, j, U)
                    for h in range(KC):
                        ins = nc.tensor.matmul(kv_p[0:TP, j, :], staged[:, j, h, :], wkv[:, h, :], start=h == 0, stop=h == KC - 1)
                    ins.then_inc(kv_made, 1)

                def totals(t, j):
                    pe.wait_ge(keys_done, t + 1)
                    for h in range(KC):
                        ins = nc.tensor.matmul(total_p[:, h, 0:D + 1], kv_s[:, j, h * 128:(h + 1) * 128], kv_s[:, j, D:2 * D + 1],
                                               start=False, stop=False, skip_group_check=True)
                    ins.then_inc(keys_used, 1)

                run_slots(pe, NT, U, [(0, products), (2, totals)])

            @block.scalar
            def _(act):
                def stage(t, j):
                    reuse(act, kv_made, t, j, U)
                    nc.scalar.copy(staged[:, j, :, :], x_t[:, :, at(t)]).then_inc(sources_staged, 1)

                def exp(t, j):
                    act.wait_ge(below_made, t + 1)
                    nc.scalar.activation(exp_s[:, j, :], below_s[:, j, :], ACT.Exp).then_inc(exp_made, 1)

                run_slots(act, NT, U, [(0, stage)] + ([(1, exp)] if feature else []))

            @block.vector
            def _(dve):
                v = nc.vector
                v.memset(kv_s[:, :, 2 * D:2 * D + 1], 1.0)
                dve.wait_ge(landed, 16 * len(loads))

                def take(t, j):
                    dve.wait_ge(kv_made, t + 1)
                    reuse(dve, keys_used, t, j, U)
                    if bkv is None:
                        v.tensor_copy(kv_s[:, j, 0:2 * D], kv_p[0:TP, j, :])
                    else:
                        v.tensor_tensor(kv_s[:, j, 0:2 * D], kv_p[0:TP, j, :], bkv[:], ALU.add)
                    dve.drain().then_inc(kv_taken, 1)
                    if feature:
                        v.tensor_scalar(below_s[:, j, :], kv_s[:, j, 0:D], 0.0, None, ALU.min)
                        dve.drain().then_inc(below_made, 1)
                    else:
                        dve.sem_inc(keys_done, 1)

                def join(t, j):
                    dve.wait_ge(exp_made, t + 1)
                    v.scalar_tensor_tensor(kv_s[:, j, 0:D], kv_s[:, j, 0:D], 0.0, exp_s[:, j, :], ALU.max, ALU.add)
                    dve.drain().then_inc(keys_done, 1)

                run_slots(dve, NT, U, [(0, take)] + ([(1, join)] if feature else []))
                dve.wait_ge(keys_used, NT)
                scale = 1.0 / N if norm == "length" else 1.0
                for h in range(KC):
                    v.scalar_tensor_tensor(mixing[:, h, 0:128], total_p[:, h, h * 128:(h + 1) * 128], scale, core.same_head[:],
                                           ALU.mult, ALU.mult)
                    v.tensor_scalar(mixing[:, h, 128:G], core.head_of[:], total_p[:, h, D:D + 1], None, ALU.mult)

        if beside is not None:
            beside[0].finish()
            second = beside[1]()
        with ExitStack() as c:
            staged_q = c.enter_context(nc.sbuf_tensor(f"{name}_queries", [128, U, KC, TP], F32))
            low = c.enter_context(nc.sbuf_tensor(f"{name}_low", [128, U, KC, TP], F32))
            high = c.enter_context(nc.sbuf_tensor(f"{name}_high", [128, U, KC, TP], F32))
            share = c.enter_context(nc.sbuf_tensor(f"{name}_share", [TP, U, 8], F32))
            mixed = c.enter_context(nc.sbuf_tensor(f"{name}_mixed", [TP, U, D], F32))
            mixed_t = c.enter_context(nc.sbuf_tensor(f"{name}_mixed_t", [128, U, KC, TP], F32))
            q_p = c.enter_context(nc.psum_tensor(f"{name}_q_p", [128, 2, 512], F32))
            mixed_p = c.enter_context(nc.psum_tensor(f"{name}_mixed_p", [128, 2, 512], F32))
            turned_p = c.enter_context(nc.psum_tensor(f"{name}_turned_p", [128, 2, 512], F32))
            out_p = c.enter_context(nc.psum_tensor(f"{name}_out_p", [128, 2, 512], F32))

            def sem(n):
                return c.enter_context(nc.semaphore(f"{name}_{n}"))

            q_made, q_split, high_made, exp_made, queries_done = sem("q_made"), sem("q_split"), sem("high_made"), sem("q_exp_made"), sem("queries_done")
            mixed_made, mixed_done, turned_made, turned_moved, out_made, out_added = (
                sem("mixed_made"), sem("mixed_done"), sem("turned_made"), sem("turned_moved"), sem("out_made"), sem("out_added"))
            block = c.enter_context(nc.Block())

            if beside is not None:
                @block.sync
                def _(sp):
                    second.sync(sp)

                @block.gpsimd
                def _(pool):
                    second.gpsimd(pool)

            @block.tensor
            def _(pe):
                def queries(t, j):
                    reuse(pe, high_made if feature else queries_done, t, j, 2)
                    for o in range(KC):
                        for h in range(KC):
                            ins = nc.tensor.matmul(q_p[:, j % 2, o * TP:(o + 1) * TP], wq[:, h, o * 128:(o + 1) * 128],
                                                   x_t[:, h, at(t)], start=h == 0, stop=h == KC - 1)
                    ins.then_inc(q_made, 1)

                def mix(t, j):
                    pe.wait_ge(queries_done, t + 1)
                    reuse(pe, mixed_done, t, j, 2)
                    for h in range(KC):
                        ins = nc.tensor.matmul(mixed_p[0:TP, j % 2, h * G:(h + 1) * G], staged_q[:, j, h, :], mixing[:, h, :],
                                               start=True, stop=True)
                    ins.then_inc(mixed_made, 1)

                def turn(t, j):
                    pe.wait_ge(mixed_done, t + 1)
                    reuse(pe, turned_moved, t, j, 2)
                    for h in range(KC):
                        ins = nc.tensor.transpose(turned_p[:, j % 2, h * TP:(h + 1) * TP], mixed[:, j, h * 128:(h + 1) * 128],
                                                  core.ident[0:TP, 0:TP])
                    ins.then_inc(turned_made, 1)

                def output(t, j):
                    pe.wait_ge(turned_moved, t + 1)
                    reuse(pe, out_added, t, j, 2)
                    for h in range(KC):
                        ins = nc.tensor.matmul(out_p[0:TP, j % 2, 0:D], mixed_t[:, j, h, :], wo[:, h, :], start=h == 0, stop=h == KC - 1)
                    ins.then_inc(out_made, 1)

                run_slots(pe, NT, U, [(0, queries), (1, mix), (2, turn), (3, output)])

            def half(tile, j, h):
                return tile[:, j % 2, h * TP:(h + 1) * TP]

            @block.scalar
            def _(act):
                def split(t, j):
                    act.wait_ge(q_made, t + 1)
                    target = high if feature else staged_q
                    reuse(act, queries_done if feature else mixed_made, t, j, U)
                    for h in range(KC):
                        if bq is None:
                            ins = nc.scalar.copy(target[:, j, h, :], half(q_p, j, h))
                        else:
                            ins = nc.scalar.activation(target[:, j, h, :], half(q_p, j, h), ACT.Identity, bias=bq[:, h:h + 1])
                    ins.then_inc(high_made if feature else queries_done, 1)
                    if feature:
                        act.wait_ge(q_split, t + 1)
                        nc.scalar.activation(low[:, j, :, :], low[:, j, :, :], ACT.Exp).then_inc(exp_made, 1)

                def move(t, j):
                    act.wait_ge(turned_made, t + 1)
                    reuse(act, out_made, t, j, U)
                    nc.scalar.copy(mixed_t[:, j, :, :], turned_p[:, j % 2, 0:2 * TP].rearrange("p (h n) -> p h n", h=KC)
                                   ).then_inc(turned_moved, 1)

                run_slots(act, NT, U, [(0, split), (2, move)])

            @block.vector
            def _(dve):
                v = nc.vector
                if bo is not None:
                    v.tensor_tensor(core.x[:], core.x[:], bo[:].unsqueeze(1).broadcast_to([TP, NT, D]), ALU.add)
                    dve.drain()

                def below(t, j):
                    dve.wait_ge(high_made, t + 1)
                    v.tensor_scalar(low[:, j, :, :], high[:, j, :, :], 0.0, None, ALU.min)
                    dve.drain().then_inc(q_split, 1)

                def join(t, j):
                    dve.wait_ge(exp_made, t + 1)
                    reuse(dve, mixed_made, t, j, U)
                    v.scalar_tensor_tensor(staged_q[:, j, :, :], high[:, j, :, :], 0.0, low[:, j, :, :], ALU.max, ALU.add)
                    dve.drain().then_inc(queries_done, 1)

                def share_out(t, j):
                    dve.wait_ge(mixed_made, t + 1)
                    reuse(dve, turned_made, t, j, U)
                    sums = mixed_p[0:TP, j % 2, 0:2 * G].rearrange("p (h g) -> p h g", h=KC)
                    if norm == "length":
                        v.tensor_copy(mixed[:, j, :].rearrange("p (h g) -> p h g", h=KC), sums[:, :, 0:128])
                    else:
                        how = ALU.add if norm == "add" else ALU.max
                        v.tensor_scalar(share[:, j, :].rearrange("p (h g) -> p h g", h=KC), sums[:, :, 128:G], 1e-6, None, how)
                        dve.drain()
                        v.reciprocal(share[:, j, :], share[:, j, :])
                        dve.drain()
                        for h in range(KC):
                            v.tensor_tensor(mixed[:, j, h * 128:(h + 1) * 128].rearrange("p (g d) -> p g d", g=4),
                                            sums[:, h, 0:128].rearrange("p (g d) -> p g d", g=4),
                                            share[:, j, 4 * h:4 * h + 4].unsqueeze(2).broadcast_to([TP, 4, 32]), ALU.mult)
                    dve.drain().then_inc(mixed_done, 1)

                def add(t, j):
                    dve.wait_ge(out_made, t + 1)
                    mine = core.x[:, bass.ds(t, 1), :]
                    v.tensor_tensor(mine, mine, out_p[0:TP, j % 2, 0:D].unsqueeze(1), ALU.add)
                    dve.drain().then_inc(out_added, 1)

                run_slots(dve, NT, U, ([(0, below), (1, join)] if feature else []) + [(1, share_out), (3, add)])

        if beside is not None:
            second.finish()


def blend(core, name, low, high, mlp, attend, attend_mix, loads):
    nc = core.nc
    with ExitStack() as c:
        def sb(n, shape, dt=F32):
            return c.enter_context(nc.sbuf_tensor(f"{name}_{n}", shape, dt))

        def sem(n):
            return c.enter_context(nc.semaphore(f"{name}_{n}"))

        product = sb("product", [TP, NT, D])
        logit, mix, term = sb("logit", [TP, NT, 3]), sb("mix", [TP, NT, 3]), sb("term", [TP, NT, 3])
        best = sb("best", [TP, NT])
        landed, logits_made, sigmoid_made, shifted, exp_made = sem("landed"), sem("logits_made"), sem("sigmoid_made"), sem("shifted"), sem("exp_made")
        block = c.enter_context(nc.Block())

        @block.sync
        def _(sp):
            for tile, dram in loads:
                sp.dma_start(tile, dram).then_inc(landed, 16)

        @block.scalar
        def _(act):
            act.wait_ge(logits_made, 1)
            nc.scalar.activation(logit[:], logit[:], ACT.Sigmoid).then_inc(sigmoid_made, 1)
            act.wait_ge(shifted, 1)
            nc.scalar.activation(mix[:], mix[:], ACT.Exp).then_inc(exp_made, 1)

        @block.vector
        def _(dve):
            v = nc.vector
            dve.wait_ge(landed, 16 * len(loads))
            for k, branch in enumerate((low, high, mlp)):
                v.tensor_tensor(product[:], branch, attend[:, k:k + 1, :].broadcast_to([TP, NT, D]), ALU.mult)
                dve.drain()
                v.tensor_reduce(logit[:, :, k], product[:], AX_X, ALU.add)
                dve.drain()
            v.memset(mix[:], 0.0)
            dve.drain().then_inc(logits_made, 1)
            dve.wait_ge(sigmoid_made, 1)
            shape = [TP, NT, 3]
            for k in range(3):
                v.tensor_tensor(term[:], logit[:, :, k:k + 1].broadcast_to(shape),
                                attend_mix[:, 3 * k:3 * k + 3].unsqueeze(1).broadcast_to(shape), ALU.mult)
                dve.drain()
                v.tensor_tensor(mix[:], mix[:], term[:], ALU.add)
                dve.drain()
            v.tensor_scalar(mix[:], mix[:], 1.0 / 3.0, None, ALU.mult)
            dve.drain()
            v.tensor_reduce(best[:], mix[:], AX_X, ALU.max)
            dve.drain()
            v.tensor_tensor(mix[:], mix[:], best[:].unsqueeze(2).broadcast_to(shape), ALU.subtract)
            dve.drain().then_inc(shifted, 1)
            dve.wait_ge(exp_made, 1)
            v.tensor_reduce(best[:], mix[:], AX_X, ALU.add)
            dve.drain()
            v.reciprocal(best[:], best[:])
            dve.drain()
            v.tensor_scalar(best[:], best[:], 3.0, None, ALU.mult)
            dve.drain()
            v.tensor_tensor(mix[:], mix[:], best[:].unsqueeze(2).broadcast_to(shape), ALU.mult)
            dve.drain()
            for k, branch in enumerate((low, high, mlp)):
                with dve.Fori(0, NT) as t:
                    mine = core.x[:, bass.ds(t, 1), :]
                    v.scalar_tensor_tensor(mine, branch[:, bass.ds(t, 1), :], mix[:, bass.ds(t, 1), k], mine, ALU.mult, ALU.add)
                dve.drain()


class NodeOrder:

    def __init__(self, core, name, records, ordered_records, K, unroll):
        self.core, self.name, self.records, self.ordered_records = core, name, records, ordered_records
        self.K, self.unroll = K, unroll

    def allocate(self, c):
        nc, name, K = self.core.nc, self.name, self.K

        def sb(n, shape):
            return c.enter_context(nc.sbuf_tensor(f"{name}_{n}", shape, F32))

        self.own, self.diag = sb("own", [128, ET_MAIN]), sb("diag", [128, 2, K, 128])
        self.rank, self.perm = sb("rank", [128, K]), sb("perm", [128, 2, K, 128])
        self.own_p = c.enter_context(nc.psum_tensor(f"{name}_own_p", [128, 2, 512], F32))
        self.moved_p = c.enter_context(nc.psum_tensor(f"{name}_moved_p", [128, 2, 512], F32))
        self.diag_made, self.own_made, self.ordered, self.moved = (
            c.enter_context(nc.semaphore(f"{name}_{n}")) for n in ("diag_made", "own_made", "ordered", "moved"))

    def tensor_phases(self, pe):
        nc, K = self.core.nc, self.K

        def spread_own(q, j):
            pe.wait_ge(self.diag_made, q + 1)
            reuse(pe, self.ordered, q, j, 2, self.unroll)
            nc.tensor.matmul(self.own_p[:, j % 2, :], self.core.ones[:], self.diag[:, j % 2, :, :].rearrange("p k e -> p (k e)"),
                             start=True, stop=True).then_inc(self.own_made, 1)

        def move(q, j):
            pe.wait_ge(self.ordered, q + 1)
            for k in range(K):
                ins = nc.tensor.matmul(self.moved_p[:, j % 2, 4 * k:4 * k + 4], self.perm[:, j % 2, k, :],
                                       self.records[:, bass.ds(q * K + k, 1), :], start=True, stop=True)
            ins.then_inc(self.moved, 1)

        return [(0, spread_own), (2, move)]

    def vector_phases(self, dve):
        nc, K = self.core.nc, self.K
        v, wide_k = nc.vector, [128, K, 128]
        v.tensor_scalar(self.own[:], self.records[:, 0:ET_MAIN, 1], 128.0, self.core.row[:, 0:1], ALU.mult, ALU.add)
        dve.drain()

        def make_diag(q, j):
            reuse(dve, self.own_made, q, j, 2, self.unroll)
            v.tensor_tensor(self.diag[:, j % 2, :, :], self.core.ident[:].unsqueeze(1).broadcast_to(wide_k),
                            self.own[:, bass.ds(q * K, K)].unsqueeze(2).broadcast_to(wide_k), ALU.mult).then_inc(self.diag_made, 1)

        def order(q, j):
            dve.wait_ge(self.own_made, q + 1)
            lower = self.diag[:, j % 2, :, :]
            v.tensor_tensor(lower, self.own_p[:, j % 2, :].rearrange("p (k e) -> p k e", k=K),
                            self.own[:, bass.ds(q * K, K)].unsqueeze(2).broadcast_to(wide_k), ALU.is_lt)
            dve.drain()
            v.tensor_reduce(self.rank[:], lower, AX_X, ALU.add)
            dve.drain()
            reuse(dve, self.moved, q, j, 2, self.unroll)
            v.tensor_tensor(self.perm[:, j % 2, :, :], self.core.col[:].unsqueeze(1).broadcast_to(wide_k),
                            self.rank[:].unsqueeze(2).broadcast_to(wide_k), ALU.is_equal)
            dve.drain().then_inc(self.ordered, 1)

        def keep(q, j):
            dve.wait_ge(self.moved, q + 1)
            v.tensor_copy(self.ordered_records[:, bass.ds(q * K, K), :],
                          self.moved_p[:, j % 2, 0:4 * K].rearrange("p (k w) -> p k w", w=4))

        return [(0, make_diag), (3, keep), (1, order)]


def max_edges(core, name, table, records, edge_group, best):
    nc = core.nc
    K, NB = 4, 4
    Q = ET_MAIN // K
    FLAG = float(2.0 ** 100)
    with ExitStack() as c:
        def sb(n, shape, dt=F32):
            return c.enter_context(nc.sbuf_tensor(f"{name}_{n}", shape, dt))

        def psum(n, shape):
            return c.enter_context(nc.psum_tensor(f"{name}_{n}", shape, F32))

        def sem(n):
            return c.enter_context(nc.semaphore(f"{name}_{n}"))

        index = sb("index", [128, NB, K], I32)
        rows = sb("rows", [128, NB, K, D])
        key = sb("key", [128, ET_MAIN])
        flag = sb("flag", [128, ET_MAIN])
        last = sb("last", [128, ET_MAIN])
        step = sb("step", [128, 128])
        next_row = sb("next_row", [128, 128])
        below, above = sb("below", [128, 1]), sb("above", [128, 1])
        steps = sb("steps", [128, 2, K, 128])
        break_s = sb("break_s", [128, 2, K, 128])
        pick = sb("pick", [128, 2, K, TP])
        scanned = sb("scanned", [128, 2, KC, K * 128])
        back_s = sb("back_s", [128, 2, K, D])
        absent = sb("absent", [TP, K])
        break_p = psum("break_p", [128, 512])
        turned_p = psum("turned_p", [128, KC, 512])
        back_p = psum("back_p", [128, KC, 512])
        out_p = psum("out_p", [128, K, D])
        present_p = psum("present_p", [128, 512])
        indexed, batch_begun = sem("indexed"), sem("batch_begun")
        gathered = [core.software_dma_semaphore(f"{name}_gathered{b}") for b in range(NB)]
        keys_made, next_made, keys_done, steps_made, breaks_made, breaks_moved, turned, scans_done, back_made, back_moved, picked, out_made, taken = (
            sem(n) for n in ("keys_made", "next_made", "keys_done", "steps_made", "breaks_made", "breaks_moved", "turned", "scans_done",
                             "back_made", "back_moved", "picked", "out_made", "taken"))
        block = c.enter_context(nc.Block())

        @block.gpsimd
        def _(pool):
            def gather(q, j):
                pool.wait_ge(indexed, q + 1)
                pool.sem_inc(batch_begun, 1)
                if not (isinstance(q, int) and q < NB):
                    pool.wait_ge(turned, q - (NB - 1))
                    pool.sem_inc(batch_begun, 1)
                for k in range(K):
                    nc.gpsimd.indirect_dma_start(
                        out=rows[:, j, k, :], out_offset=None, in_=table,
                        in_offset=bass.IndirectOffsetOnAxis(ap=index[:, j, k:k + 1].bitcast(U32), axis=0),
                    ).then_inc(gathered[j], 16)

            run_slots(pool, Q, NB, [(0, gather)])

        @block.scalar
        def _(act):
            def number(q, j):
                if not (isinstance(q, int) and q < NB):
                    act.wait_ge(gathered[j], (q - j) * (16 * K // NB))
                nc.scalar.copy(index[:, j, :], records[:, bass.ds(q * K, K), 0]).then_inc(indexed, 1)

            def make_steps(q, j):
                if isinstance(q, int) and q == 0:
                    act.wait_ge(keys_done, 1)
                reuse(act, breaks_made, q, j, 2, NB)
                for k in range(K):
                    ins = nc.scalar.activation(steps[:, j % 2, k, :], step[:], ACT.Copy, scale=flag[:, bass.ds(q * K + k, 1)])
                ins.then_inc(steps_made, 1)

            def move_breaks(q, j):
                act.wait_ge(breaks_made, q + 1)
                reuse(act, scans_done, q, j, 2, NB)
                nc.scalar.copy(break_s[:, j % 2, :, :].rearrange("p k e -> p (k e)"), break_p[:]).then_inc(breaks_moved, 1)

            def move_back(q, j):
                act.wait_ge(back_made, q + 1)
                reuse(act, out_made, q, j, 2, NB)
                nc.scalar.copy(back_s[:, j % 2, :, :], back_p[:].rearrange("p h (k d) -> p (h k) d", d=D)).then_inc(back_moved, 1)

            run_slots(act, Q, NB, [(0, number), (0, make_steps), (1, move_breaks), (2, move_back)])

        @block.tensor
        def _(pe):
            pe.wait_ge(keys_made, 1)
            nc.tensor.matmul(break_p[:, 0:ET_MAIN], next_row[:], key[:], start=True, stop=True).then_inc(next_made, 1)
            pe.wait_ge(keys_done, 1)

            def spread_breaks(q, j):
                pe.wait_ge(steps_made, q + 1)
                reuse(pe, breaks_moved, q, j, 1, NB)
                nc.tensor.matmul(break_p[:], core.ones[:], steps[:, j % 2, :, :].rearrange("p k e -> p (k e)"),
                                 start=True, stop=True).then_inc(breaks_made, 1)

            def turn(q, j):
                pe.wait_ge(gathered[j], (q - j) * (16 * K // NB) + 16 * K)
                reuse(pe, scans_done, q, j, 1, NB)
                for h in range(KC):
                    for k in range(K):
                        ins = nc.tensor.transpose(turned_p[:, h, k * 128:(k + 1) * 128], rows[:, j, k, h * 128:(h + 1) * 128], core.ident[:])
                ins.then_inc(turned, 1)

            def turn_back(q, j):
                pe.wait_ge(scans_done, q + 1)
                reuse(pe, back_moved, q, j, 1, NB)
                for k in range(K):
                    for h in range(KC):
                        ins = nc.tensor.transpose(back_p[:, k // 2, (k % 2) * D + h * 128:(k % 2) * D + (h + 1) * 128],
                                                  scanned[:, j % 2, h, k * 128:(k + 1) * 128], core.ident[:])
                ins.then_inc(back_made, 1)

            def choose(q, j):
                pe.wait_ge(picked, q + 1)
                pe.wait_ge(back_moved, q + 1)
                reuse(pe, taken, q, j, 1, NB)
                for k in range(K):
                    nc.tensor.matmul(out_p[0:TP, k, :], pick[:, j % 2, k, :], back_s[:, j % 2, k, :], start=True, stop=True)
                    ins = nc.tensor.matmul(present_p[0:TP, k:k + 1], pick[:, j % 2, k, :], core.ones[:, 0:1], start=True, stop=True)
                ins.then_inc(out_made, 1)

            run_slots(pe, Q, NB, [(0, spread_breaks), (1, turn), (2, turn_back), (3, choose)])

        @block.vector
        def _(dve):
            v = nc.vector
            v.memset(best[:], -FAR)
            v.tensor_scalar(key[:], records[:, 0:ET_MAIN, 1], 1.0, None, ALU.add)
            v.tensor_scalar(above[:], core.row[:], 1.0, None, ALU.add)
            v.tensor_scalar(below[:], core.row[:], -1.0, None, ALU.add)
            dve.drain()
            v.tensor_scalar(flag[:], key[:], FLAG, None, ALU.mult)
            v.tensor_scalar(next_row[:], core.col[:], below[:, 0:1], None, ALU.is_equal)
            v.scalar_tensor_tensor(step[:], core.col[:], above[:, 0:1], core.ident[:], ALU.is_equal, ALU.subtract)
            dve.drain().then_inc(keys_made, 1)
            dve.wait_ge(next_made, 1)
            v.tensor_tensor(last[:], key[:], break_p[:, 0:ET_MAIN], ALU.not_equal)
            dve.drain().then_inc(keys_done, 1)
            v.tensor_tensor(last[:], last[:], key[:], ALU.mult)
            dve.drain()
            v.tensor_scalar(last[:], last[:], -1.0, None, ALU.add)
            dve.drain()

            def scan(q, j):
                dve.wait_ge(breaks_moved, q + 1)
                dve.wait_ge(turned, q + 1)
                reuse(dve, back_made, q, j, 2, NB)
                for h in range(KC):
                    ins = v.tensor_tensor_scan(scanned[:, j % 2, h, :], break_s[:, j % 2, :, :].rearrange("p k e -> p (k e)"),
                                               turned_p[:, h, :], -FAR, ALU.add, ALU.max)
                ins.then_inc(scans_done, 1)

            def mark(q, j):
                reuse(dve, out_made, q, j, 2, NB)
                v.tensor_tensor(pick[:, j % 2, :, :], core.col[:, 0:TP].unsqueeze(1).broadcast_to([128, K, TP]),
                                last[:, bass.ds(q * K, K)].unsqueeze(2).broadcast_to([128, K, TP]), ALU.is_equal).then_inc(picked, 1)

            numbers = GroupNumbers(nc, edge_group, mybir.EngineType.DVE, K, 3)

            def take(q, j):
                groups = numbers.of_batch(q, j)
                dve.wait_ge(out_made, q + 1)
                v.tensor_scalar(absent[:], present_p[0:TP, 0:K], -1.0, 4.0 * FAR, ALU.add, ALU.mult)
                dve.drain()
                for k in range(K):
                    mine = best[:, bass.ds(groups[k], 1), :]
                    v.scalar_tensor_tensor(mine, out_p[0:TP, k, :].unsqueeze(1), absent[:, k:k + 1], mine, ALU.add, ALU.max)
                    last_drain = dve.drain()
                last_drain.then_inc(taken, 1)

            run_slots(dve, Q, NB, [(1, scan), (2, mark), (3, take)])


def small_rows(core, name, body, stores=(), loads=(), functions=()):
    nc = core.nc
    with ExitStack() as c:
        landed, asked, answered, done, stored = (c.enter_context(nc.semaphore(f"{name}_{n}"))
                                                 for n in ("landed", "asked", "answered", "done", "stored"))
        block = c.enter_context(nc.Block())

        @block.sync
        def _(sp):
            for tile, dram in loads:
                sp.dma_start(tile, dram).then_inc(landed, 16)
            if stores:
                sp.wait_ge(done, 1)
                for dram, tile in stores:
                    sp.dma_start(dram, tile).then_inc(stored, 16)
                sp.wait_ge(stored, 16 * len(stores))

        @block.scalar
        def _(act):
            for k, function in enumerate(functions):
                act.wait_ge(asked, k + 1)
                function(act).then_inc(answered, 1)

        @block.vector
        def _(dve):
            if loads:
                dve.wait_ge(landed, 16 * len(loads))

            def call(k):
                dve.drain().then_inc(asked, 1)
                dve.wait_ge(answered, k + 1)

            body(dve, call)
            dve.drain().then_inc(done, 1)


def gat_edges(core, name, table, records, edge_group, gathered_rows, best):
    nc = core.nc
    K, NB = 5, 4
    Q = ET_GAT // K
    with ExitStack() as c:
        def sb(n, shape, dt=F32):
            return c.enter_context(nc.sbuf_tensor(f"{name}_{n}", shape, dt))

        def sem(n):
            return c.enter_context(nc.semaphore(f"{name}_{n}"))

        index = sb("index", [128, NB, K], I32)
        rows = sb("rows", [128, NB, K, 20])
        other = sb("other", [128, K, TP])
        score = sb("score", [128, 2, K, 4, TP])
        top = sb("top", [TP, K, 4])
        turned_p = c.enter_context(nc.psum_tensor(f"{name}_turned_p", [128, K, 4, 128], F32))
        indexed, batch_begun, rows_kept, scored, turned, topped = (
            sem(n) for n in ("indexed", "batch_begun", "rows_kept", "scored", "turned", "topped"))
        gathered = [core.software_dma_semaphore(f"{name}_gathered{b}") for b in range(NB)]
        block = c.enter_context(nc.Block())

        @block.gpsimd
        def _(pool):
            def gather(q, j):
                pool.wait_ge(indexed, q + 1)
                pool.sem_inc(batch_begun, 1)
                if not (isinstance(q, int) and q < NB):
                    pool.wait_ge(scored, q - (NB - 1))
                    pool.sem_inc(batch_begun, 1)
                    pool.wait_ge(rows_kept, q - (NB - 1))
                    pool.sem_inc(batch_begun, 1)
                for k in range(K):
                    nc.gpsimd.indirect_dma_start(
                        out=rows[:, j, k, :], out_offset=None, in_=table,
                        in_offset=bass.IndirectOffsetOnAxis(ap=index[:, j, k:k + 1].bitcast(U32), axis=0),
                    ).then_inc(gathered[j], 16)

            run_slots(pool, Q, NB, [(0, gather)])

        @block.scalar
        def _(act):
            def number(q, j):
                if not (isinstance(q, int) and q < NB):
                    act.wait_ge(gathered[j], (q - j) // NB * (16 * K))
                nc.scalar.copy(index[:, j, :], records[:, bass.ds(q * K, K), 0]).then_inc(indexed, 1)

            def keep(q, j):
                act.wait_ge(gathered[j], (q - j) // NB * (16 * K) + 16 * K)
                nc.scalar.copy(gathered_rows[:, bass.ds(q * K, K), :], rows[:, j, :, :]).then_inc(rows_kept, 1)

            run_slots(act, Q, NB, [(0, number), (2, keep)])

        @block.tensor
        def _(pe):
            def turn(q, j):
                pe.wait_ge(scored, q + 1)
                reuse(pe, topped, q, j, 1, NB)
                for k in range(K):
                    for a in range(4):
                        ins = nc.tensor.transpose(turned_p[0:TP, k, a, :], score[:, j % 2, k, a, :], core.ident[:])
                ins.then_inc(turned, 1)

            run_slots(pe, Q, NB, [(2, turn)])

        @block.vector
        def _(dve):
            v = nc.vector

            numbers = GroupNumbers(nc, edge_group, mybir.EngineType.DVE, K, 3)

            def rate(q, j):
                for k in range(K):
                    v.tensor_scalar(other[:, k, :], core.col[:, 0:TP], records[:, bass.ds(q * K + k, 1), 1], -FAR,
                                    ALU.not_equal, ALU.mult)
                dve.drain()
                dve.wait_ge(gathered[j], (q - j) // NB * (16 * K) + 16 * K)
                reuse(dve, turned, q, j, 2, NB)
                for k in range(K):
                    v.tensor_tensor(score[:, j % 2, k, :, :], other[:, k:k + 1, :].broadcast_to([128, 4, TP]),
                                    rows[:, j, k, 16:20].unsqueeze(2).broadcast_to([128, 4, TP]), ALU.add)
                dve.drain().then_inc(scored, 1)

            def take(q, j):
                groups = numbers.of_batch(q, j)
                dve.wait_ge(turned, q + 1)
                v.tensor_reduce(top[:], turned_p[0:TP, :, :, :], AX_X, ALU.max)
                dve.drain()
                for k in range(K):
                    mine = best[:, bass.ds(groups[k], 1), :]
                    v.tensor_tensor(mine, mine, top[:, k:k + 1, :], ALU.max)
                    last = dve.drain()
                last.then_inc(topped, 1)

            run_slots(dve, Q, NB, [(2, rate), (3, take)])


def gat_sums(core, name, records, edge_group, gathered_rows, node_scores, sums):
    nc = core.nc
    K, NB = 5, 4
    Q = ET_GAT // K
    with ExitStack() as c:
        def sb(n, shape, dt=F32):
            return c.enter_context(nc.sbuf_tensor(f"{name}_{n}", shape, dt))

        def psum(n, shape):
            return c.enter_context(nc.psum_tensor(f"{name}_{n}", shape, F32))

        def sem(n):
            return c.enter_context(nc.semaphore(f"{name}_{n}"))

        pick = sb("pick", [128, NB, K, TP])
        pick_t = sb("pick_t", [TP, 2, K, 128])
        raw = sb("raw", [128, K, 4])
        rated = sb("rated", [128, 2, K, 4])
        message = sb("message", [128, 2, K, 20])
        turned_p = psum("turned_p", [128, 2, 1024])
        node_p = psum("node_p", [128, 2, 512])
        out_p = psum("out_p", [128, 2, 512])
        picked, turned, moved, nodes_made, rated_done, exp_made, messages_done, out_made, taken = (
            sem(n) for n in ("picked", "turned", "moved", "nodes_made", "rated_done", "exp_made", "messages_done", "out_made", "taken"))
        block = c.enter_context(nc.Block())

        @block.tensor
        def _(pe):
            numbers = GroupNumbers(nc, edge_group, mybir.EngineType.PE, K, 1)

            def turn(q, j):
                pe.wait_ge(picked, q + 1)
                reuse(pe, moved, q, j, 2, NB)
                for k in range(K):
                    ins = nc.tensor.transpose(turned_p[0:TP, j % 2, k * 128:(k + 1) * 128], pick[:, j, k, :], core.ident[:])
                ins.then_inc(turned, 1)

            def look_up(q, j):
                groups = numbers.of_batch(q, j)
                pe.wait_ge(moved, q + 1)
                reuse(pe, rated_done, q, j, 2, NB)
                for k in range(K):
                    ins = nc.tensor.matmul(node_p[:, j % 2, k * 8:(k + 1) * 8], pick_t[:, j % 2, k, :], node_scores[:, bass.ds(groups[k], 1), :],
                                           start=True, stop=True)
                ins.then_inc(nodes_made, 1)

            def add_up(q, j):
                pe.wait_ge(messages_done, q + 1)
                reuse(pe, taken, q, j, 2, NB)
                for k in range(K):
                    ins = nc.tensor.matmul(out_p[0:TP, j % 2, k * 20:(k + 1) * 20], pick[:, j, k, :], message[:, j % 2, k, :], start=True, stop=True)
                ins.then_inc(out_made, 1)

            run_slots(pe, Q, NB, [(0, turn), (1, look_up), (3, add_up)])

        @block.scalar
        def _(act):
            def move(q, j):
                act.wait_ge(turned, q + 1)
                reuse(act, nodes_made, q, j, 2, NB)
                nc.scalar.copy(pick_t[:, j % 2, :, :], turned_p[0:TP, j % 2, 0:K * 128]).then_inc(moved, 1)

            def exp(q, j):
                act.wait_ge(rated_done, q + 1)
                nc.scalar.activation(rated[:, j % 2, :, :], rated[:, j % 2, :, :], ACT.Exp).then_inc(exp_made, 1)

            run_slots(act, Q, NB, [(0, move), (2, exp)])

        @block.vector
        def _(dve):
            v = nc.vector
            numbers = GroupNumbers(nc, edge_group, mybir.EngineType.DVE, K, 4)

            def choose(q, j):
                reuse(dve, out_made, q, j, NB, NB)
                for k in range(K):
                    v.tensor_scalar(pick[:, j, k, :], core.col[:, 0:TP], records[:, bass.ds(q * K + k, 1), 1], None, ALU.is_equal)
                dve.drain().then_inc(picked, 1)

            def rate(q, j):
                dve.wait_ge(nodes_made, q + 1)
                reuse(dve, messages_done, q, j, 2, NB)
                node = node_p[:, j % 2, 0:8 * K].rearrange("p (k s) -> p k s", k=K)
                v.tensor_tensor(raw[:], gathered_rows[:, bass.ds(q * K, K), 16:20], node[:, :, 0:4], ALU.add)
                dve.drain()
                v.scalar_tensor_tensor(raw[:], raw[:], 0.2, raw[:], ALU.mult, ALU.max)
                dve.drain()
                v.tensor_tensor(rated[:, j % 2, :, :], raw[:], node[:, :, 4:8], ALU.subtract)
                dve.drain().then_inc(rated_done, 1)

            def send(q, j):
                dve.wait_ge(exp_made, q + 1)
                reuse(dve, out_made, q, j, 2, NB)
                for a in range(4):
                    v.tensor_tensor(message[:, j % 2, :, 4 * a:4 * a + 4], gathered_rows[:, bass.ds(q * K, K), 4 * a:4 * a + 4],
                                    rated[:, j % 2, :, a:a + 1].broadcast_to([128, K, 4]), ALU.mult)
                v.tensor_copy(message[:, j % 2, :, 16:20], rated[:, j % 2, :, :])
                dve.drain().then_inc(messages_done, 1)

            def take(q, j):
                groups = numbers.of_batch(q, j)
                dve.wait_ge(out_made, q + 1)
                for k in range(K):
                    mine = sums[:, bass.ds(groups[k], 1), :]
                    v.tensor_tensor(mine, mine, out_p[0:TP, j % 2, k * 20:(k + 1) * 20].unsqueeze(1), ALU.add)
                    last = dve.drain()
                last.then_inc(taken, 1)

            run_slots(dve, Q, NB, [(0, choose), (2, rate), (3, send), (4, take)])


def slice_attention(core, name, x_t, wx, bx, slices, wo, bo, residual, loads, square_loads):
    nc = core.nc
    with ExitStack() as outer:
        def keep(n, shape):
            return outer.enter_context(nc.sbuf_tensor(f"{name}_{n}", shape, F32))

        mid_t = keep("mid_t", [128, KC, N])
        queries = keep("queries", [TP, NT, D])
        tile_best = keep("tile_best", [128, KC, NT])
        key_best = keep("key_best", [128, KC])
        key_best_b = keep("key_best_b", [TP, D])
        mixing = keep("mixing", [128, KC, 128])

        with ExitStack() as c:
            def sem(n):
                return c.enter_context(nc.semaphore(f"{name}_{n}"))

            mid_s = c.enter_context(nc.sbuf_tensor(f"{name}_mid_s", [128, U, KC, TP], F32))
            diag = c.enter_context(nc.sbuf_tensor(f"{name}_diag", [128, KC, 128], F32))
            mid_p = c.enter_context(nc.psum_tensor(f"{name}_mid_p", [128, 3, 512], F32))
            key_p = c.enter_context(nc.psum_tensor(f"{name}_key_p", [128, 3, 512], F32))
            spread_p = c.enter_context(nc.psum_tensor(f"{name}_spread_p", [128, 512], F32))
            landed, slices_cleared, squares_landed = sem("landed"), sem("slices_cleared"), sem("squares_landed")
            mid_made, mid_taken, keys_made, keys_taken, diag_made, spread_made = (
                sem(n) for n in ("mid_made", "mid_taken", "keys_made", "keys_taken", "diag_made", "spread_made"))
            block = c.enter_context(nc.Block())

            @block.sync
            def _(sp):
                for tile, dram in loads:
                    sp.dma_start(tile, dram).then_inc(landed, 16)
                sp.wait_ge(slices_cleared, 1)
                for tile, dram in square_loads:
                    sp.dma_start(tile, dram).then_inc(squares_landed, 16)

            @block.tensor
            def _(pe):
                pe.wait_ge(landed, 16 * len(loads))
                pe.wait_ge(squares_landed, 16 * len(square_loads))

                def mid(t, j):
                    reuse(pe, mid_taken, t, j, 3)
                    for o in range(KC):
                        for h in range(KC):
                            ins = nc.tensor.matmul(mid_p[:, j % 3, o * TP:(o + 1) * TP], wx[:, h, o * 128:(o + 1) * 128],
                                                   x_t[:, h, at(t)], start=h == 0, stop=h == KC - 1)
                    ins.then_inc(mid_made, 1)

                def keys(t, j):
                    pe.wait_ge(mid_taken, t + 1)
                    reuse(pe, keys_taken, t, j, 3)
                    for h in range(KC):
                        ins = nc.tensor.matmul(key_p[:, j % 3, h * TP:(h + 1) * TP], slices[:, 128:256], mid_s[:, j, h, :],
                                               start=True, stop=True)
                    ins.then_inc(keys_made, 1)

                run_slots(pe, NT, U, [(0, mid), (1, keys)])
                pe.wait_ge(diag_made, 1)
                nc.tensor.matmul(spread_p[0:TP, 0:D], core.ones[:, 0:TP], diag[:].rearrange("p h n -> p (h n)"),
                                 start=True, stop=True).then_inc(spread_made, 1)

            @block.scalar
            def _(act):
                act.wait_ge(landed, 16 * len(loads))

                def take(t, j):
                    act.wait_ge(mid_made, t + 1)
                    reuse(act, keys_made, t, j, U)
                    for h in range(KC):
                        nc.scalar.activation(mid_s[:, j, h, :], mid_p[:, j % 3, h * TP:(h + 1) * TP], ACT.Identity, bias=bx[:, h:h + 1])
                    act.drain().then_inc(mid_taken, 1)
                    nc.scalar.copy(mid_t[:, :, at(t)], mid_s[:, j, :, :])

                run_slots(act, NT, U, [(0, take)])

            @block.vector
            def _(dve):
                v = nc.vector
                v.memset(slices[:], 0.0)
                dve.drain().then_inc(slices_cleared, 1)

                def take(t, j):
                    dve.wait_ge(keys_made, t + 1)
                    v.tensor_reduce(tile_best[:, :, bass.ds(t, 1)], key_p[:, j % 3, 0:2 * TP].rearrange("p (h n) -> p h n", h=KC),
                                    AX_X, ALU.max).then_inc(keys_taken, 1)

                run_slots(dve, NT, U, [(0, take)])
                dve.drain()
                v.tensor_reduce(key_best[:], tile_best[:], AX_X, ALU.max)
                dve.drain()
                for h in range(KC):
                    v.tensor_scalar(diag[:, h, :], core.ident[:], key_best[:, h:h + 1], None, ALU.mult)
                dve.drain().then_inc(diag_made, 1)
                dve.wait_ge(spread_made, 1)
                v.tensor_copy(key_best_b[:], spread_p[0:TP, 0:D])

        with ExitStack() as c:
            def sem(n):
                return c.enter_context(nc.semaphore(f"{name}_{n}"))

            staged = c.enter_context(nc.sbuf_tensor(f"{name}_staged", [128, U, KC, TP], F32))
            kv_s = c.enter_context(nc.sbuf_tensor(f"{name}_kv_s", [TP, U, 2 * D + 1], F32))
            query_best = c.enter_context(nc.sbuf_tensor(f"{name}_query_best", [TP, 8], F32))
            qkv_p = c.enter_context(nc.psum_tensor(f"{name}_qkv_p", [128, 3, KC, 512], F32))
            total_p = c.enter_context(nc.psum_tensor(f"{name}_total_p", [128, KC, 512], F32))
            staged_done, qkv_made, qkv_taken, keys_done, keys_used = (
                sem(n) for n in ("staged_done", "qkv_made", "qkv_taken", "keys_done", "keys_used"))
            block = c.enter_context(nc.Block())

            @block.gpsimd
            def _(pool):
                def stage(t, j):
                    reuse(pool, qkv_made, t, j, U)
                    nc.gpsimd.tensor_copy(staged[:, j, :, :], mid_t[:, :, at(t)]).then_inc(staged_done, 1)

                run_slots(pool, NT, U, [(0, stage)])

            @block.tensor
            def _(pe):
                for h in range(KC):
                    nc.tensor.matmul(total_p[:, h, 0:D + 1], core.zeros[:], core.wide_zeros[:, 0:D + 1], start=True, stop=False,
                                     skip_group_check=True)

                def products(t, j):
                    pe.wait_ge(staged_done, t + 1)
                    reuse(pe, qkv_taken, t, j, 3)
                    for h in range(KC):
                        ins = nc.tensor.matmul(qkv_p[0:TP, j % 3, h, 0:384], staged[:, j, h, :], slices[:], start=True, stop=True)
                    ins.then_inc(qkv_made, 1)

                def totals(t, j):
                    pe.wait_ge(keys_done, t + 1)
                    for h in range(KC):
                        ins = nc.tensor.matmul(total_p[:, h, 0:D + 1], kv_s[:, j, h * 128:(h + 1) * 128], kv_s[:, j, D:2 * D + 1],
                                               start=False, stop=False, skip_group_check=True)
                    ins.then_inc(keys_used, 1)

                run_slots(pe, NT, U, [(0, products), (2, totals)])

            @block.scalar
            def _(act):
                def exp(t, j):
                    act.wait_ge(qkv_taken, t + 1)
                    nc.scalar.activation(queries[:, bass.ds(t, 1), :], queries[:, bass.ds(t, 1), :], ACT.Exp)
                    nc.scalar.activation(kv_s[:, j, 0:D], kv_s[:, j, 0:D], ACT.Exp).then_inc(keys_done, 1)

                run_slots(act, NT, U, [(0, exp)])

            @block.vector
            def _(dve):
                v = nc.vector
                v.memset(kv_s[:, :, 2 * D:2 * D + 1], 1.0)

                def take(t, j):
                    dve.wait_ge(qkv_made, t + 1)
                    reuse(dve, keys_used, t, j, U)
                    q = qkv_p[0:TP, j % 3, :, 0:128]
                    for h in range(KC):
                        v.tensor_reduce(query_best[:, 4 * h:4 * h + 4], q[:, h, :].rearrange("p (g s) -> p g s", g=4), AX_X, ALU.max)
                    v.tensor_tensor(kv_s[:, j, 0:D].rearrange("p (h s) -> p h s", h=KC), qkv_p[0:TP, j % 3, :, 128:256],
                                    key_best_b[:].rearrange("p (h s) -> p h s", h=KC), ALU.subtract)
                    v.tensor_copy(kv_s[:, j, D:2 * D].rearrange("p (h s) -> p h s", h=KC), qkv_p[0:TP, j % 3, :, 256:384])
                    dve.drain()
                    for h in range(KC):
                        v.tensor_tensor(queries[:, bass.ds(t, 1), h * 128:(h + 1) * 128].rearrange("p o (g s) -> p (o g) s", g=4),
                                        q[:, h, :].rearrange("p (g s) -> p g s", g=4),
                                        query_best[:, 4 * h:4 * h + 4].unsqueeze(2).broadcast_to([TP, 4, 32]), ALU.subtract)
                    dve.drain().then_inc(qkv_taken, 1)

                run_slots(dve, NT, U, [(0, take)])
                dve.wait_ge(keys_used, NT)

                for h in range(KC):
                    v.reciprocal(key_best[:, h:h + 1], total_p[:, h, D:D + 1])
                dve.drain()
                for h in range(KC):
                    v.scalar_tensor_tensor(mixing[:, h, :], total_p[:, h, h * 128:(h + 1) * 128], key_best[:, h:h + 1],
                                           core.same_head[:], ALU.mult, ALU.mult)

        with ExitStack() as c:
            def sb(n, shape):
                return c.enter_context(nc.sbuf_tensor(f"{name}_{n}", shape, F32))

            def psum(n):
                return c.enter_context(nc.psum_tensor(f"{name}_{n}", [128, 2, 512], F32))

            def sem(n):
                return c.enter_context(nc.semaphore(f"{name}_{n}"))

            query_s, query_t, share = sb("query_s", [TP, U, D]), sb("query_t", [128, U, KC, TP]), sb("share", [TP, U, 8])
            mixed, mixed_t = sb("mixed", [TP, U, D]), sb("mixed_t", [128, U, KC, TP])
            query_p, mixed_p, turned_p, out_p = psum("query_p"), psum("mixed_p"), psum("turned_p"), psum("out_p")
            query_staged, query_turned, query_moved, mixed_made, mixed_done, turned_made, turned_moved, out_made, out_added = (
                sem(n) for n in ("query_staged", "query_turned", "query_moved", "mixed_made", "mixed_done", "turned_made",
                                 "turned_moved", "out_made", "out_added"))
            block = c.enter_context(nc.Block())

            def turn_tile(to, source, j):
                for h in range(KC):
                    ins = nc.tensor.transpose(to[:, j % 2, h * TP:(h + 1) * TP], source[:, j, h * 128:(h + 1) * 128],
                                              core.ident[0:TP, 0:TP])
                return ins

            @block.tensor
            def _(pe):
                def turn_query(t, j):
                    pe.wait_ge(query_staged, t + 1)
                    reuse(pe, query_moved, t, j, 2)
                    turn_tile(query_p, query_s, j).then_inc(query_turned, 1)

                def mix(t, j):
                    pe.wait_ge(query_moved, t + 1)
                    reuse(pe, mixed_done, t, j, 2)
                    for h in range(KC):
                        ins = nc.tensor.matmul(mixed_p[0:TP, j % 2, h * 128:(h + 1) * 128], query_t[:, j, h, :], mixing[:, h, :],
                                               start=True, stop=True)
                    ins.then_inc(mixed_made, 1)

                def turn(t, j):
                    pe.wait_ge(mixed_done, t + 1)
                    reuse(pe, turned_moved, t, j, 2)
                    turn_tile(turned_p, mixed, j).then_inc(turned_made, 1)

                def output(t, j):
                    pe.wait_ge(turned_moved, t + 1)
                    reuse(pe, out_added, t, j, 2)
                    for h in range(KC):
                        ins = nc.tensor.matmul(out_p[0:TP, j % 2, 0:D], mixed_t[:, j, h, :], wo[:, h, :], start=h == 0, stop=h == KC - 1)
                    ins.then_inc(out_made, 1)

                run_slots(pe, NT, U, [(0, turn_query), (1, mix), (2, turn), (3, output)])

            @block.scalar
            def _(act):
                def move(to, source, j):
                    return nc.scalar.copy(to[:, j, :, :], source[:, j % 2, 0:2 * TP].rearrange("p (h n) -> p h n", h=KC))

                def move_query(t, j):
                    act.wait_ge(query_turned, t + 1)
                    reuse(act, mixed_made, t, j, U)
                    move(query_t, query_p, j).then_inc(query_moved, 1)

                def move_mixed(t, j):
                    act.wait_ge(turned_made, t + 1)
                    reuse(act, out_made, t, j, U)
                    move(mixed_t, turned_p, j).then_inc(turned_moved, 1)

                run_slots(act, NT, U, [(0, move_query), (2, move_mixed)])

            @block.vector
            def _(dve):
                v = nc.vector

                def stage(t, j):
                    reuse(dve, query_turned, t, j, U)
                    reuse(dve, mixed_done, t, j, U)
                    mine = queries[:, bass.ds(t, 1), :]
                    v.tensor_copy(query_s[:, j:j + 1, :], mine)
                    v.tensor_reduce(share[:, j, :], mine.rearrange("p o (g s) -> p (o g) s", s=32), AX_X, ALU.add)
                    dve.drain().then_inc(query_staged, 1)
                    v.reciprocal(share[:, j, :], share[:, j, :])

                def share_out(t, j):
                    dve.drain()
                    dve.wait_ge(mixed_made, t + 1)
                    reuse(dve, turned_made, t, j, U)
                    v.tensor_tensor(mixed[:, j, :].rearrange("p (g d) -> p g d", g=8), mixed_p[0:TP, j % 2, 0:D].rearrange("p (g d) -> p g d", g=8),
                                    share[:, j, :].unsqueeze(2).broadcast_to([TP, 8, 32]), ALU.mult)
                    dve.drain().then_inc(mixed_done, 1)

                def add(t, j):
                    dve.wait_ge(out_made, t + 1)
                    mine = residual[:, bass.ds(t, 1), :]
                    v.tensor_tensor(mine, mine, out_p[0:TP, j % 2, 0:D].unsqueeze(1), ALU.add)
                    dve.drain().then_inc(out_added, 1)

                v.tensor_tensor(residual[:], residual[:], bo[:].unsqueeze(1).broadcast_to([TP, NT, D]), ALU.add)
                dve.drain()
                run_slots(dve, NT, U, [(0, stage), (1, share_out), (3, add)])


def across(matrix):
    return matrix.rearrange("(t p) n -> p t n", p=TP)


def wide(row, width=D):
    return row.unsqueeze(1).broadcast_to([TP, NT, width])


class Carver:

    def __init__(self, tensor):
        self.tensor, self.used = tensor, 0

    def __call__(self, name, shape, dt=F32):
        words = int(shape[1]) * (int(shape[2]) if len(shape) > 2 else 1)
        tile = self.tensor[0:shape[0], self.used:self.used + words]
        self.used += words
        if dt != F32:
            tile = tile.bitcast(dt)
        return tile.rearrange("p (t w) -> p t w", t=shape[1]) if len(shape) > 2 else tile


class Scope:

    def __init__(self, core, name):
        self.core, self.name, self.stack = core, name, ExitStack()

    def __enter__(self):
        return self

    def __exit__(self, *error):
        if error[0] is None:
            self.stack.close()

    def __call__(self, name, shape, dt=F32):
        return self.stack.enter_context(self.core.nc.sbuf_tensor(f"{self.name}_{name}", shape, dt))


def scores_of(core, name, x_t, weight, bias, experts, scores, router, shift):
    nc = core.nc

    def evacuate(dve, t, j, out):
        mine = scores[:, bass.ds(t, 1), :]
        if bias is None:
            nc.vector.tensor_copy(mine, out.unsqueeze(1))
        else:
            nc.vector.tensor_tensor(mine, out.unsqueeze(1), shift[:].unsqueeze(1), ALU.add)

    loads = [(router[:], halves(weight))] + ([] if bias is None else [(shift[:], spread(bias))])
    project(core, name, [x_t], [(0, router, 0, True, True)], experts, evacuate, loads)


def expert_layer(core, name, x_t, gates, experts, chunks, w1, b1, w2, b2, beside=None):
    nc = core.nc
    H = chunks * 128
    with Scope(core, name) as sb:
        w1_s, w2_s = sb("w1", [128, KC, experts * H]), sb("w2", [128, experts * chunks, D])
        b1_s, b2_s = sb("b1", [128, experts * chunks]), sb("b2", [TP, experts, D])

        def load_weights(e):
            return [(w1_s[:, :, e * H:(e + 1) * H], halves(w1[e])),
                    (w2_s[:, e * chunks:(e + 1) * chunks, :], w2[e].rearrange("(c p) d -> p c d", p=128))]

        feed_forward(core, f"{name}_ff", x_t, experts, chunks, load_weights, b1_s, ACT.Gelu, w1_s, w2_s, None, gates, b2_s,
                     loads=[(b1_s[:], b1), (b2_s[:], spread(b2))], beside=beside)


def linear_attention(core, name, x_t, wq, wkv, wo, bq, bkv, bo, feature, norm, beside=None):
    with Scope(core, name) as sb:
        wq_s, wkv_s, wo_s = sb("wq", [128, KC, D]), sb("wkv", [128, KC, 2 * D]), sb("wo", [128, KC, D])
        bo_s = sb("bo", [TP, D])
        bq_s, bkv_s = (None, None) if bq is None else (sb("bq", [128, KC]), sb("bkv", [TP, 2 * D]))
        part = 2 * D // len(wkv)
        loads = [(wkv_s[:, :, i * part:(i + 1) * part], halves(w)) for i, w in enumerate(wkv)]
        if bq is not None:
            loads += [(bkv_s[:, i * D:(i + 1) * D], spread(b)) for i, b in enumerate(bkv)] + [(bq_s[:], bq)]
        loads += [(wq_s[:], halves(wq)), (wo_s[:], halves(wo)), (bo_s[:], spread(bo))]
        attention(core, f"{name}_at", x_t, wq_s, wkv_s, wo_s, bq_s, bkv_s, bo_s, loads, feature, norm, beside)


def layer0(core, w, x_t, by_src, src_groups):
    nc, x = core.nc, core.x
    table = nc.dram_tensor("l0_rows", (N, D), F32).ap()
    layer_norm(core, "l0_norm", x, None, table, x_t)
    linear_attention(core, "l0_mix", x_t, w["L0_mix_wq"], (w["L0_mix_wk"], w["L0_mix_wv"]), w["L0_mix_wo"], w["L0_mix_bq"],
                     (w["L0_mix_bk"], w["L0_mix_bv"]), w["L0_mix_bo"], True, "add",
                     beside=(Scatters(src_groups, 5), lambda: Scatters(src_groups, 7)))
    assert src_groups.done == src_groups.rounds
    clear_semaphores(core)
    with Scope(core, "l0") as sb:
        sums = sb("sums", [TP, NT, 2 * D])
        sum_edges(core, "l0_edges", table, *by_src, sums, words=(2, 3))
        with Scope(core, "l0_gnn") as sb2:
            sums_t, weight = sb2("sums_t", [128, KC, N]), sb2("weight", [128, KC, D])
            for k, branch in enumerate(("low", "high")):
                half = sums[:, :, k * D:(k + 1) * D]
                turn_rows(core, f"l0_turn_{branch}", half, sums_t)

                def evacuate(dve, t, j, out, half=half):
                    nc.vector.tensor_scalar(half[:, bass.ds(t, 1), :], out.unsqueeze(1), 0.0, None, ALU.max)

                project(core, f"l0_{branch}", [sums_t], [(0, weight, 0, True, True)], D, evacuate,
                        [(weight[:], halves(w[f"L0_gnn_weight_{branch}"]))])
        with Scope(core, "l0_mlp") as sb2:
            mlp = sb2("rows", [TP, NT, D])
            with Scope(core, "l0_mlp_weight") as sb3:
                weight = sb3("s", [128, KC, D])

                def evacuate_mlp(dve, t, j, out):
                    nc.vector.tensor_scalar(mlp[:, bass.ds(t, 1), :], out.unsqueeze(1), 0.0, None, ALU.max)

                project(core, "l0_mlp", [x_t], [(0, weight, 0, True, True)], D, evacuate_mlp,
                        [(weight[:], halves(w["L0_gnn_weight_mlp"]))])
            attend, attend_mix = sb2("attend", [TP, 3, D]), sb2("attend_mix", [TP, 9])
            blend(core, "l0_blend", sums[:, :, 0:D], sums[:, :, D:2 * D], mlp[:], attend, attend_mix,
                  [(attend[:, k, :], spread(w[f"L0_gnn_att_vec_{b}"].rearrange("d o -> (d o)"))) for k, b in enumerate(("low", "high", "mlp"))]
                  + [(attend_mix[:], spread(w["L0_gnn_att_vec"].rearrange("a b -> (a b)")))])


def layer0_ffn(core, w, x_t, dst_groups):
    E = 8
    with Scope(core, "l0f") as sb:
        gain, shift = sb("gain", [128, KC]), sb("shift", [128, KC])
        scores, gates, router, bias = sb("scores", [TP, NT, E]), sb("gates", [TP, NT, E]), sb("router", [128, KC, E]), sb("bias", [TP, E])
        small_rows(core, "l0f_load", lambda dve, call: None, (), [(gain[:], w["L0_ffn_gamma"]), (shift[:], w["L0_ffn_beta"])])
        layer_norm(core, "l0f_norm", core.x, None, None, x_t, True, gain, shift)
        scores_of(core, "l0f_scores", x_t, w["L0_ffn_Wr"], w["L0_ffn_br"], E, scores, router, bias)
        gate_top2(core, "l0f_gate", scores, E, gates, False)
        expert_layer(core, "l0f_experts", x_t, gates, E, 4, w["L0_ffn_W1"], w["L0_ffn_b1"], w["L0_ffn_W2"], w["L0_ffn_b2"],
                     Scatters(dst_groups, dst_groups.rounds))


def layer1(core, w, x_t, by_dst, spare):
    nc, x = core.nc, core.x
    table = nc.dram_tensor("l1_rows", (N, D), F32).ap()
    layer_norm(core, "l1_norm", x, None, table, x_t)
    with Scope(core, "l1") as sb:
        sums, sums_t = sb("sums", [TP, NT, D]), sb("sums_t", [128, KC, N])
        own, other = sb("own", [128, KC, D]), sb("other", [128, KC, D])
        ordered = spare[:, 0:4 * ET_MAIN].rearrange("p (t w) -> p t w", w=4)
        sum_edges(core, "l1_edges", table, *by_dst, sums, beside=NodeOrder(core, "order_dst", by_dst[0], ordered, 4, 8))
        small_rows(core, "l1_ordered", lambda dve, call: nc.vector.tensor_copy(by_dst[0][:, 0:ET_MAIN, :], ordered))
        turn_rows(core, "l1_turn", sums, sums_t)

        def evacuate(dve, t, j, out):
            mine = x[:, bass.ds(t, 1), :]
            nc.vector.scalar_tensor_tensor(mine, out.unsqueeze(1), 0.0, mine, ALU.max, ALU.add)

        project(core, "l1_gnn", [x_t, sums_t], [(0, own, 0, True, False), (1, other, 0, False, True)], D, evacuate,
                [(own[:], halves(w["L1_gnn_W"])), (other[:], halves(w["L1_gnn_M"]))])
    clear_semaphores(core)
    linear_attention(core, "l1_mix", x_t, w["L1_mix_Wq"], (w["L1_mix_Wk"], w["L1_mix_Wv"]), w["L1_mix_Wfc"], w["L1_mix_bq"],
                     (w["L1_mix_bk"], w["L1_mix_bv"]), w["L1_mix_bfc"], False, "length")


def layer1_ffn(core, w, x_t, gat_groups):
    nc, x = core.nc, core.x
    E = 32
    layer_norm(core, "l1f_norm", x, None, None, x_t)
    with Scope(core, "l1f") as sb:
        chosen = sb("chosen", [E, N])
        with Scope(core, "l1f_router") as sb2:
            scores, router, bias = sb2("scores", [TP, NT, E]), sb2("weight", [128, KC, E]), sb2("bias", [TP, E])
            scores_of(core, "l1f_scores", x_t, w["L1_ffn_router_w"], w["L1_ffn_router_b"], E, scores, router, bias)
            pick_expert(core, "l1f_pick", scores, E, chosen)
        w1, w2, b1, b2 = sb("w1", [128, KC, 2048]), sb("w2", [128, 16, D]), sb("b1", [128, 16]), sb("b2", [E, D])
        W1, W2 = w["L1_ffn_W1"], w["L1_ffn_W2"]

        def load_weights(e):
            eight = slice(e * 8, (e + 1) * 8)
            return [(w1[:, h, e * 512:(e + 1) * 512].rearrange("p (e h) -> p e h", e=8),
                     W1[eight, h * 128:(h + 1) * 128, :].rearrange("e p h -> p e h")) for h in range(KC)] + [
                (w2[:, e * 4:(e + 1) * 4, :], W2[eight].rearrange("(i two) h d -> (two h) i d", two=2))]

        def take(dve, t, out):
            mine = x[:, bass.ds(t, 1), :]
            nc.vector.scalar_tensor_tensor(mine, out.unsqueeze(1), 0.0, mine, ALU.max, ALU.add)

        feed_forward(core, "l1f_ff", x_t, 4, 4, load_weights, b1, ACT.Relu, w1, w2, take, None, b2, chosen,
                     loads=[(b1[:], w["L1_ffn_b1"]), (b2[:], w["L1_ffn_b2"])], beside=Scatters(gat_groups, gat_groups.rounds))


def layer2(core, w, x_t, by_dst, xn, spare):
    nc, x = core.nc, core.x
    v = nc.vector
    table = nc.dram_tensor("l2_messages", (N, D), F32).ap()
    layer_norm(core, "l2_norm", x, xn, None, x_t)
    with Scope(core, "l2") as sb:
        own = spare[0:TP, :].rearrange("p (t d) -> p t d", t=NT)
        scale2, shift2 = sb("scale2", [TP, D]), sb("shift2", [TP, D])
        with Scope(core, "l2_messages") as sb2:
            weight = sb2("weight", [128, KC, 2 * D])
            row = {n: sb2(n, [TP, D]) for n in ("gamma1", "beta1", "mean1", "var1", "mean2", "var2", "bias")}
            message = sb2("message", [TP, NT, D])
            both = w["L2_gnn_W"]

            def prepare(dve, call):
                v.tensor_tensor(weight[:, :, D:2 * D], weight[:, :, D:2 * D], weight[:, :, 0:D], ALU.subtract)
                v.tensor_scalar(row["var1"][:], row["var1"][:], EPS, None, ALU.add)
                v.tensor_scalar(row["var2"][:], row["var2"][:], EPS, None, ALU.add)
                call(0)
                call(1)
                v.reciprocal(row["var1"][:], row["var1"][:])
                v.reciprocal(row["var2"][:], row["var2"][:])
                v.tensor_tensor(row["mean1"][:], row["bias"][:], row["mean1"][:], ALU.subtract)
                dve.drain()
                v.tensor_tensor(row["gamma1"][:], row["gamma1"][:], row["var1"][:], ALU.mult)
                v.tensor_tensor(scale2[:], scale2[:], row["var2"][:], ALU.mult)
                dve.drain()
                v.tensor_tensor(row["mean1"][:], row["mean1"][:], row["gamma1"][:], ALU.mult)
                v.tensor_tensor(row["mean2"][:], row["mean2"][:], scale2[:], ALU.mult)
                dve.drain()
                v.tensor_tensor(row["beta1"][:], row["beta1"][:], row["mean1"][:], ALU.add)
                v.tensor_tensor(shift2[:], shift2[:], row["mean2"][:], ALU.subtract)

            def sqrt_of(tile):
                return lambda act: nc.scalar.activation(tile[:], tile[:], ACT.Sqrt)

            small_rows(core, "l2_prepare", prepare, (), [
                (weight[:, :, 0:D], halves(both[0:D])), (weight[:, :, D:2 * D], halves(both[D:2 * D])),
                (row["gamma1"][:], spread(w["L2_gnn_bn1_gamma"])), (row["beta1"][:], spread(w["L2_gnn_bn1_beta"])),
                (row["mean1"][:], spread(w["L2_gnn_bn1_mean"])), (row["var1"][:], spread(w["L2_gnn_bn1_var"])),
                (scale2[:], spread(w["L2_gnn_bn2_gamma"])), (shift2[:], spread(w["L2_gnn_bn2_beta"])),
                (row["mean2"][:], spread(w["L2_gnn_bn2_mean"])), (row["var2"][:], spread(w["L2_gnn_bn2_var"])),
                (row["bias"][:], spread(w["L2_gnn_b"]))], [sqrt_of(row["var1"]), sqrt_of(row["var2"])])

            def evacuate(dve, t, j, out):
                gamma, mine = row["gamma1"][:].unsqueeze(1), own[:, bass.ds(t, 1), :]
                v.tensor_tensor(message[:, bass.ds(t, 1), :], out[:, 0:D].unsqueeze(1), gamma, ALU.mult)
                v.tensor_tensor(mine, out[:, D:2 * D].unsqueeze(1), gamma, ALU.mult)
                dve.drain()
                v.tensor_tensor(mine, mine, row["beta1"][:].unsqueeze(1), ALU.add)

            project(core, "l2_project", [x_t], [(0, weight, 0, True, True)], 2 * D, evacuate)
            small_rows(core, "l2_store", lambda dve, call: None, [(across(table), message[:])])
        best = sb("best", [TP, NT, D])
        max_edges(core, "l2_edges", table, *by_dst, best)

        def finish(dve, call):
            v.tensor_tensor(best[:], best[:], own[:], ALU.add)
            v.tensor_tensor(x[:], x[:], xn[:], ALU.add)
            dve.drain()
            v.scalar_tensor_tensor(best[:], best[:], 0.0, wide(scale2[:]), ALU.max, ALU.mult)
            v.tensor_tensor(x[:], x[:], wide(shift2[:]), ALU.add)
            dve.drain()
            v.tensor_tensor(x[:], x[:], best[:], ALU.add)

        small_rows(core, "l2_finish", finish)


def layer2_mix(core, w, x_t, xn):
    nc, x = core.nc, core.x
    v = nc.vector
    with Scope(core, "l2m") as sb:
        gain, shift, gain2, shift2 = (sb(n, [128, KC]) for n in ("gain", "shift", "gain2", "shift2"))
        small_rows(core, "l2m_load", lambda dve, call: None, (), [
            (gain[:], w["L2_mix_ln1_w"]), (shift[:], w["L2_mix_ln1_b"]), (gain2[:], w["L2_mix_ln2_w"]), (shift2[:], w["L2_mix_ln2_b"])])
        layer_norm(core, "l2m_norm", xn, None, None, x_t, False, gain, shift)
        with Scope(core, "l2m_slices") as sb2:
            wx, wo, bx = sb2("wx", [128, KC, D]), sb2("wo", [128, KC, D]), sb2("bx", [128, KC])
            slices, bo = sb2("slices", [128, 384]), sb2("bo", [TP, D])
            slice_attention(core, "l2m_at", x_t, wx, bx, slices, wo, bo, xn,
                            [(wx[:], halves(w["L2_mix_Wx"])), (wo[:], halves(w["L2_mix_Wo"])), (bx[:], w["L2_mix_bx"]),
                             (bo[:], spread(w["L2_mix_bo"]))],
                            [(slices[32 * h:32 * h + 32, 128 * k + 32 * h:128 * k + 32 * h + 32], w[f"L2_mix_{n}"])
                             for k, n in enumerate(("Wq", "Wk", "Wv")) for h in range(4)])
        layer_norm(core, "l2m_norm2", xn, None, None, x_t, False, gain2, shift2)
        w1, w2, b1, b2 = sb("w1", [128, KC, 1024]), sb("w2", [128, 8, D]), sb("b1", [128, 8]), sb("b2", [TP, D])
        W1, W2 = w["L2_mix_W1"], w["L2_mix_W2"]

        def load_weights(e):
            return [(w1[:, :, e * 512:(e + 1) * 512], halves(W1[:, e * 512:(e + 1) * 512])),
                    (w2[:, e * 4:(e + 1) * 4, :], W2[e * 512:(e + 1) * 512].rearrange("(c p) d -> p c d", p=128))]

        def take(dve, t, out):
            mine, mid = x[:, bass.ds(t, 1), :], xn[:, bass.ds(t, 1), :]
            v.tensor_tensor(mid, mid, out.unsqueeze(1), ALU.add)
            v.tensor_tensor(mine, mine, b2[:].unsqueeze(1), ALU.add)
            dve.drain()
            v.tensor_tensor(mine, mine, mid, ALU.add)

        feed_forward(core, "l2m_ff", x_t, 2, 4, load_weights, b1, ACT.Gelu, w1, w2, take,
                     loads=[(b1[:], w["L2_mix_b1"]), (b2[:], spread(w["L2_mix_b2"]))])


def layer2_ffn(core, w, x_t, records, edge_group):
    nc, x = core.nc, core.x
    v = nc.vector
    E = 4
    table = nc.dram_tensor("l2f_rows", (N, 20), F32).ap()
    layer_norm(core, "l2f_norm", x, None, None, x_t)
    with Scope(core, "l2f") as sb:
        gates = sb("gates", [TP, NT, E])
        with Scope(core, "l2f_gat") as sb2:
            weight, row = sb2("weight", [128, KC, 16]), sb2("row", [TP, NT, 20])
            to_src, to_dst, bias, gain, shift = (sb2(n, [TP, 16]) for n in ("to_src", "to_dst", "bias", "gain", "shift"))
            product, node, best = sb2("product", [TP, NT, 16]), sb2("node", [TP, NT, 8]), sb2("best", [TP, NT, 4])
            own, raw, sums, scores = sb2("own", [TP, NT, 4]), sb2("raw", [TP, NT, 4]), sb2("sums", [TP, NT, 20]), sb2("scores", [TP, NT, 4])
            mean, var, dev = sb2("mean", [TP, NT]), sb2("var", [TP, NT]), sb2("dev", [TP, NT])
            gathered_rows = sb2("gathered_rows", [128, ET_GAT, 20])

            def evacuate(dve, t, j, out):
                v.tensor_copy(row[:, bass.ds(t, 1), 0:16], out.unsqueeze(1))

            project(core, "l2f_features", [x_t], [(0, weight, 0, True, True)], 16, evacuate, [(weight[:], halves(w["L2_ffn_W_gat"]))])

            def rate(dve, call):
                for vector, to in ((to_src, row[:, :, 16:20]), (to_dst, node[:, :, 0:4])):
                    v.tensor_tensor(product[:], row[:, :, 0:16], wide(vector[:], 16), ALU.mult)
                    dve.drain()
                    v.tensor_reduce(to, product[:].rearrange("p t (a c) -> p t a c", a=4), AX_X, ALU.add)
                    dve.drain()
                v.tensor_copy(best[:], row[:, :, 16:20])

            small_rows(core, "l2f_rate", rate, [(across(table), row[:])], [
                (to_src[:], spread(w["L2_ffn_att_src"].rearrange("a c -> (a c)"))),
                (to_dst[:], spread(w["L2_ffn_att_dst"].rearrange("a c -> (a c)"))),
                (bias[:], spread(w["L2_ffn_b_gat"])), (gain[:], spread(w["L2_ffn_ln_gamma"])), (shift[:], spread(w["L2_ffn_ln_beta"]))])
            clear_semaphores(core)
            gat_edges(core, "l2f_edges", table, records, edge_group, gathered_rows, best)

            def start(dve, call):
                v.tensor_tensor(raw[:], best[:], node[:, :, 0:4], ALU.add)
                v.tensor_tensor(own[:], row[:, :, 16:20], node[:, :, 0:4], ALU.add)
                dve.drain()
                v.scalar_tensor_tensor(node[:, :, 4:8], raw[:], 0.2, raw[:], ALU.mult, ALU.max)
                v.scalar_tensor_tensor(own[:], own[:], 0.2, own[:], ALU.mult, ALU.max)
                dve.drain()
                v.tensor_tensor(own[:], own[:], node[:, :, 4:8], ALU.subtract)
                call(0)
                for a in range(4):
                    v.tensor_tensor(sums[:, :, 4 * a:4 * a + 4], row[:, :, 4 * a:4 * a + 4], own[:, :, a:a + 1].broadcast_to([TP, NT, 4]), ALU.mult)
                v.tensor_copy(sums[:, :, 16:20], own[:])

            small_rows(core, "l2f_start", start, (), (), [lambda act: nc.scalar.activation(own[:], own[:], ACT.Exp)])
            gat_sums(core, "l2f_sums", records, edge_group, gathered_rows, node, sums)

            def score(dve, call):
                v.tensor_scalar(raw[:], sums[:, :, 16:20], 1e-16, None, ALU.add)
                dve.drain()
                v.reciprocal(raw[:], raw[:])
                dve.drain()
                for a in range(4):
                    v.tensor_tensor(product[:, :, 4 * a:4 * a + 4], sums[:, :, 4 * a:4 * a + 4], raw[:, :, a:a + 1].broadcast_to([TP, NT, 4]), ALU.mult)
                dve.drain()
                v.tensor_tensor(product[:], product[:], wide(bias[:], 16), ALU.add)
                dve.drain()
                v.tensor_reduce(mean[:], product[:], AX_X, ALU.add)
                dve.drain()
                v.tensor_scalar(mean[:], mean[:], 1.0 / 16.0, None, ALU.mult)
                dve.drain()
                v.tensor_tensor(product[:], product[:], mean[:].unsqueeze(2).broadcast_to([TP, NT, 16]), ALU.subtract)
                dve.drain()
                v.tensor_tensor(row[:, :, 0:16], product[:], product[:], ALU.mult)
                dve.drain()
                v.tensor_reduce(var[:], row[:, :, 0:16], AX_X, ALU.add)
                dve.drain()
                v.tensor_scalar(var[:], var[:], 1.0 / 16.0, EPS, ALU.mult, ALU.add)
                call(0)
                v.reciprocal(dev[:], dev[:])
                dve.drain()
                v.tensor_tensor(product[:], product[:], dev[:].unsqueeze(2).broadcast_to([TP, NT, 16]), ALU.mult)
                dve.drain()
                v.tensor_tensor(product[:], product[:], wide(gain[:], 16), ALU.mult)
                dve.drain()
                v.tensor_tensor(product[:], product[:], wide(shift[:], 16), ALU.add)
                dve.drain()
                v.tensor_reduce(scores[:], product[:].rearrange("p t (a c) -> p t c a", a=4), AX_X, ALU.add)
                dve.drain()
                v.tensor_scalar(scores[:], scores[:], 0.25, None, ALU.mult)

            small_rows(core, "l2f_score", score, (), (), [lambda act: nc.scalar.activation(dev[:], var[:], ACT.Sqrt)])
            gate_top2(core, "l2f_gate", scores, E, gates, False)
        expert_layer(core, "l2f_experts", x_t, gates, E, 4, w["L2_ffn_W1"], w["L2_ffn_b1"], w["L2_ffn_W2"], w["L2_ffn_b2"])


def layer3(core, w, x_t, by_src, by_dst, spare):
    nc, x = core.nc, core.x
    v = nc.vector
    nodes_table, edges_table, mid_table = (nc.dram_tensor(f"l3_table_{n}", (N, D), F32).ap() for n in ("nodes", "edges", "mid"))
    layer_norm(core, "l3_norm", x, None, nodes_table, x_t)
    with Scope(core, "l3") as sb:
        in_share, out_share = sb("in_share", [TP, NT]), sb("out_share", [TP, NT])
        has = sb("has", [TP, NT])
        slope, low = sb("slope", [TP, 1]), sb("low", [TP, U, D])
        weight, bias = sb("weight", [128, KC, D]), sb("bias", [TP, D])
        mid = spare[0:TP, :].rearrange("p (t d) -> p t d", t=NT)
        sums_t = sb("sums_t", [128, KC, N])
        for k in range(2):
            clear_semaphores(core)
            sides = ((by_dst, in_share), (by_src, out_share))
            source = (nodes_table, mid_table)[k]
            with Scope(core, f"l3_conv{k}") as sb2:
                sums = sb2("sums", [TP, NT, D + 1])
                for s, (records, share) in enumerate(sides):
                    sum_edges(core, f"l3_edges{k}_{s}", source, *records, sums if k == 0 else sums[:, :, 0:D], counted=k == 0)
                    source = edges_table

                    def shares(dve, call, share=share, s=s, sums=sums):
                        if k == 0:
                            v.tensor_scalar(share[:], sums[:, :, D], 1.0, None, ALU.max)
                            v.tensor_scalar(has[:], sums[:, :, D], 1.0, None, ALU.min)
                            dve.drain()
                            v.reciprocal(share[:], share[:])
                            dve.drain()
                            v.tensor_tensor(share[:], share[:], has[:], ALU.mult)
                            dve.drain()
                        if s == 0:
                            v.tensor_tensor(sums[:, :, 0:D], sums[:, :, 0:D], share[:].unsqueeze(2).broadcast_to([TP, NT, D]), ALU.mult)

                    if s == 0 or k == 0:
                        small_rows(core, f"l3_shares{k}_{s}", shares, [(across(edges_table), sums[:, :, 0:D])] if s == 0 else ())
                turn_rows(core, f"l3_turn{k}", sums[:, :, 0:D], sums_t, out_share)

            def evacuate(dve, t, j, out, k=k):
                mine, below = mid[:, bass.ds(t, 1), :], low[:, j:j + 1, :]
                if k == 0:
                    v.tensor_tensor(mine, out.unsqueeze(1), bias[:].unsqueeze(1), ALU.add)
                else:
                    v.tensor_tensor(mine, out.unsqueeze(1), mine, ALU.add)
                    dve.drain()
                    v.tensor_tensor(mine, mine, bias[:].unsqueeze(1), ALU.add)
                dve.drain()
                v.tensor_scalar(below, mine, 0.0, slope[:, 0:1], ALU.min, ALU.mult)
                dve.drain()
                v.scalar_tensor_tensor(mine, mine, 0.0, below, ALU.max, ALU.add)
                if k == 1:
                    dve.drain()
                    v.tensor_tensor(x[:, bass.ds(t, 1), :], x[:, bass.ds(t, 1), :], mine, ALU.add)

            loads = [(weight[:], halves(w[f"L3_gnn_W{k + 1}"])), (bias[:], spread(w[f"L3_gnn_b{k + 1}"]))]
            loads.append((slope[:], spread(w["L3_gnn_a"])) if k == 0 else (mid[:], across(nodes_table)))
            project(core, f"l3_conv{k}", [sums_t], [(0, weight, 0, True, True)], D, evacuate, loads)
            if k == 0:
                small_rows(core, "l3_store", lambda dve, call: None, [(across(mid_table), mid[:])])
    clear_semaphores(core)
    linear_attention(core, "l3_mix", x_t, w["L3_mix_Wq"], (w["L3_mix_Wkv"],), w["L3_mix_Wproj"], None, None, w["L3_mix_bproj"], True, "max")


def layer3_ffn(core, w, x_t, xn):
    nc, x = core.nc, core.x
    E = 8
    layer_norm(core, "l3f_norm", x, xn, None, x_t)
    with Scope(core, "l3f") as sb:
        scores, gates, router = sb("scores", [TP, NT, E]), sb("gates", [TP, NT, E]), sb("router", [128, KC, E])
        scores_of(core, "l3f_scores", x_t, w["L3_ffn_router_w"], None, E, scores, router, None)
        gate_top2(core, "l3f_gate", scores, E, gates, True)
        small_rows(core, "l3f_tokens", lambda dve, call: nc.vector.tensor_tensor(x[:], x[:], xn[:], ALU.add))
        expert_layer(core, "l3f_experts", x_t, gates, E, 2, w["L3_ffn_w1"], w["L3_ffn_b1"], w["L3_ffn_w2"], w["L3_ffn_b2"])


def clear_semaphores(core):
    nc = core.nc
    with nc.Block() as block:
        @block.gpsimd
        def _(pool):
            left = sorted(nc.released_uncleared_semaphores)
            for number in left:
                if number - 1 not in left:
                    first = number
                if number + 1 not in left:
                    pool.sem_clear(range(first, number + 1))


def program(nc, w, out):
    with ExitStack() as ctx:
        core = Core(nc, ctx)
        constants(core)
        by_src, by_dst, by_target = (
            (core.keep(f"{n}_records", [128, et + ET_PAD, 4]), core.keep(f"{n}_edge_group", [1, et + ET_PAD], I32))
            for n, et in (("by_src", ET_MAIN), ("by_dst", ET_MAIN), ("by_target", ET_GAT)))
        spare = core.keep("spare", [128, NT * D])
        keep = Carver(spare)
        src_groups = EdgeGroups(core, "src_groups", E_MAIN, ET_MAIN, keep, *by_src)
        dst_groups = EdgeGroups(core, "dst_groups", E_MAIN, ET_MAIN, keep, *by_dst)
        gat_groups = EdgeGroups(core, "gat_groups", E_GAT, ET_GAT, keep, *by_target)
        src_groups.prepare(w["src"], w["dst"], [w["edge_weight"], w["edge_weight_n2"]])
        dst_groups.prepare(w["dst"], w["src"], [], Scatters(src_groups, 7))
        gat_groups.prepare(w["L2_ffn_edge_index"][1], w["L2_ffn_edge_index"][0], [], Scatters(src_groups, 6))
        core.x = core.keep("x", [TP, NT, D])
        x_t = core.keep("x_t", [128, KC, N])
        small_rows(core, "load_x", lambda dve, call: None, (), [(core.x[:], across(w["x"]))])
        clear_semaphores(core)
        layer0(core, w, x_t, by_src, src_groups)
        clear_semaphores(core)
        layer0_ffn(core, w, x_t, dst_groups)
        clear_semaphores(core)
        layer1(core, w, x_t, by_dst, spare)
        clear_semaphores(core)
        layer1_ffn(core, w, x_t, gat_groups)
        with Scope(core, "normed2") as sb:
            xn = sb("rows", [TP, NT, D])
            clear_semaphores(core)
            layer2(core, w, x_t, by_dst, xn, spare)
            clear_semaphores(core)
            layer2_mix(core, w, x_t, xn)
        clear_semaphores(core)
        layer2_ffn(core, w, x_t, *by_target)
        clear_semaphores(core)
        layer3(core, w, x_t, by_src, by_dst, spare)
        with Scope(core, "normed3") as sb:
            clear_semaphores(core)
            layer3_ffn(core, w, x_t, sb("rows", [TP, NT, D]))
        small_rows(core, "store_x", lambda dve, call: None, [(across(out), core.x[:])])


TURNED = ("L1_mix_Wq", "L1_mix_Wk", "L1_mix_Wv", "L1_mix_Wfc", "L1_ffn_router_w", "L2_mix_Wx", "L2_mix_Wq", "L2_mix_Wk",
          "L2_mix_Wv", "L2_mix_Wo", "L2_mix_W1", "L2_mix_W2", "L3_mix_Wq", "L3_mix_Wkv", "L3_mix_Wproj", "L3_ffn_router_w")
BY_CHANNEL = ("L0_mix_bq", "L0_ffn_gamma", "L0_ffn_beta", "L0_ffn_b1", "L1_mix_bq", "L1_ffn_b1", "L2_mix_ln1_w", "L2_mix_ln1_b",
              "L2_mix_ln2_w", "L2_mix_ln2_b", "L2_mix_bx", "L2_mix_b1", "L2_ffn_b1", "L3_ffn_b1")


def laid_out(name, array):
    if name in TURNED:
        return array.T
    if name in BY_CHANNEL:
        return array.reshape(-1, 128).T
    return array


def kernel(**inputs):
    import numpy as np
    import concourse.bacc as bacc
    from concourse.bass_utils import run_bass_kernel_spmd

    nc = bacc.Bacc("TRN2", target_bir_lowering=False, num_devices=1)
    arrays, w = {}, {}
    for name, value in inputs.items():
        array = np.ascontiguousarray(laid_out(name, np.asarray(value)))
        arrays[f"in_{name}"] = array
        w[name] = nc.dram_tensor(f"in_{name}", array.shape, mybir.dt.from_np(array.dtype), kind="ExternalInput").ap()
    out = nc.dram_tensor("out", (N, D), F32, kind="ExternalOutput").ap()
    program(nc, w, out)
    result = run_bass_kernel_spmd(nc, [arrays], core_ids=[0])
    return result.results[0]["out"]
```
